# Optimizing a Trainium2 kernel written in Bass

```python
import numpy as np
import jax
import jax.numpy as jnp

def _softmax(x, axis=-1):
    return jax.nn.softmax(x, axis=axis)

def _gelu(x):
    return jax.nn.gelu(x, approximate=True)

def _silu(x):
    return jax.nn.silu(x)

def _sigmoid(x):
    return jax.nn.sigmoid(x)

def _layernorm(x, axis=-1, eps=1e-05):
    m = jnp.mean(x, axis=axis, keepdims=True)
    v = jnp.var(x, axis=axis, keepdims=True)
    return (x - m) / jnp.sqrt(v + eps)

def _scatter_add(tgt, idx, src, axis=0):
    return tgt.at[idx].add(src)

def _segment_sum(src, seg, n):
    return jax.ops.segment_sum(src, seg, n)
kernel_name = 'mk_adaln_d1_jaxref_r8_1df6d0'

def setup_inputs(seed: int=0):
    np.random.seed(seed)
    _w = jnp.asarray

    def _L0_attn_setup():
        import jax, jax.numpy as jnp
        import numpy as np
        N_HEAD = 16
        LATENT = 32

        def _rotate_half(x):
            xe = x[..., ::2]
            xo = x[..., 1::2]
            return jnp.stack((-xo, xe), axis=-1).reshape(x.shape)

        def _rope_tables(T, latent_dim, dtype):
            inv_freq = 1.0 / 10000.0 ** (jnp.arange(0, latent_dim, 2, dtype=jnp.float32) / latent_dim)
            t = jnp.arange(T, dtype=jnp.float32)
            freqs = jnp.outer(t, inv_freq)
            cos = jnp.repeat(jnp.cos(freqs), 2, axis=-1)[:, :latent_dim]
            sin = jnp.repeat(jnp.sin(freqs), 2, axis=-1)[:, :latent_dim]
            return (cos.astype(dtype), sin.astype(dtype))
        key = jax.random.key(seed)
        ks = jax.random.split(key, 14)
        C = 128
        hd = C // N_HEAD
        L = LATENT
        s = 0.02
        return {'x': jax.random.normal(ks[0], (4, 256, C), jnp.float32), 'c_attn_w': jax.random.normal(ks[1], (3 * C, C), jnp.float32) * s, 'c_attn_b': jnp.zeros((3 * C,), jnp.float32), 'q2l_w': jax.random.normal(ks[2], (L, hd), jnp.float32) * s, 'q2l_b': jnp.zeros((L,), jnp.float32), 'kv2l_w': jax.random.normal(ks[3], (L, hd), jnp.float32) * s, 'kv2l_b': jnp.zeros((L,), jnp.float32), 'l2o_w': jax.random.normal(ks[4], (hd, L), jnp.float32) * s, 'l2o_b': jnp.zeros((hd,), jnp.float32), 'wqk_w': jax.random.normal(ks[5], (L, L), jnp.float32) * s, 'wqk_b': jnp.zeros((L,), jnp.float32), 'cproj_w': jax.random.normal(ks[6], (C, C), jnp.float32) * s, 'cproj_b': jnp.zeros((C,), jnp.float32)}
    _L0_attn_in = _L0_attn_setup()

    def _L0_ffn_setup():
        import jax, jax.numpy as jnp
        import numpy as np
        B, S, H, E, K = (2, 256, 128, 8, 2)
        FF = 4 * H
        EPS = 1e-05
        key = jax.random.key(seed)
        ks = jax.random.split(key, 5)
        rn = lambda k, shape, scale: jax.random.normal(k, shape, dtype=jnp.float32) * scale
        return {'x': rn(ks[0], (B, S, H), 1.0), 'router_W': rn(ks[1], (H, E), H ** (-0.5)), 'router_b': jnp.zeros((E,), jnp.float32), 'ln_g': jnp.ones((E, H), jnp.float32), 'ln_b': jnp.zeros((E, H), jnp.float32), 'W1': rn(ks[2], (E, H, FF), H ** (-0.5)), 'b1': jnp.zeros((E, FF), jnp.float32), 'W2': rn(ks[3], (E, FF, H), FF ** (-0.5)), 'b2': jnp.zeros((E, H), jnp.float32)}
    _L0_ffn_in = _L0_ffn_setup()
    _L0_c = _w((lambda *s: np.random.randn(*s).astype(np.float32) * 0.05)(16, 128))
    _L0_wmod = _w((lambda *s: np.random.randn(*s).astype(np.float32) * 0.05)(128, 6 * 128) * 128 ** (-0.5))
    _d = {'L0_attn_x': _L0_attn_in['x'], 'L0_attn_c_attn_w': _L0_attn_in['c_attn_w'], 'L0_attn_c_attn_b': _L0_attn_in['c_attn_b'], 'L0_attn_q2l_w': _L0_attn_in['q2l_w'], 'L0_attn_q2l_b': _L0_attn_in['q2l_b'], 'L0_attn_kv2l_w': _L0_attn_in['kv2l_w'], 'L0_attn_kv2l_b': _L0_attn_in['kv2l_b'], 'L0_attn_l2o_w': _L0_attn_in['l2o_w'], 'L0_attn_l2o_b': _L0_attn_in['l2o_b'], 'L0_attn_wqk_w': _L0_attn_in['wqk_w'], 'L0_attn_wqk_b': _L0_attn_in['wqk_b'], 'L0_attn_cproj_w': _L0_attn_in['cproj_w'], 'L0_attn_cproj_b': _L0_attn_in['cproj_b'], 'L0_ffn_router_W': _L0_ffn_in['router_W'], 'L0_ffn_router_b': _L0_ffn_in['router_b'], 'L0_ffn_ln_g': _L0_ffn_in['ln_g'], 'L0_ffn_ln_b': _L0_ffn_in['ln_b'], 'L0_ffn_W1': _L0_ffn_in['W1'], 'L0_ffn_b1': _L0_ffn_in['b1'], 'L0_ffn_W2': _L0_ffn_in['W2'], 'L0_ffn_b2': _L0_ffn_in['b2'], 'L0_c': _L0_c, 'L0_wmod': _L0_wmod}
    _x0 = _d['L0_attn_x']
    _d['L0_attn_x'] = jax.random.normal(jax.random.fold_in(jax.random.key(seed), 1), (16, 512, 128), dtype=_x0.dtype)
    del _x0
    return _d

def reference(L0_attn_x, L0_attn_c_attn_w, L0_attn_c_attn_b, L0_attn_q2l_w, L0_attn_q2l_b, L0_attn_kv2l_w, L0_attn_kv2l_b, L0_attn_l2o_w, L0_attn_l2o_b, L0_attn_wqk_w, L0_attn_wqk_b, L0_attn_cproj_w, L0_attn_cproj_b, L0_ffn_router_W, L0_ffn_router_b, L0_ffn_ln_g, L0_ffn_ln_b, L0_ffn_W1, L0_ffn_b1, L0_ffn_W2, L0_ffn_b2, L0_c, L0_wmod):

    def _L0_attn_ref(x, c_attn_w, c_attn_b, q2l_w, q2l_b, kv2l_w, kv2l_b, l2o_w, l2o_b, wqk_w, wqk_b, cproj_w, cproj_b):
        import jax, jax.numpy as jnp
        import numpy as np
        N_HEAD = 16
        LATENT = 32

        def _rotate_half(x):
            xe = x[..., ::2]
            xo = x[..., 1::2]
            return jnp.stack((-xo, xe), axis=-1).reshape(x.shape)

        def _rope_tables(T, latent_dim, dtype):
            inv_freq = 1.0 / 10000.0 ** (jnp.arange(0, latent_dim, 2, dtype=jnp.float32) / latent_dim)
            t = jnp.arange(T, dtype=jnp.float32)
            freqs = jnp.outer(t, inv_freq)
            cos = jnp.repeat(jnp.cos(freqs), 2, axis=-1)[:, :latent_dim]
            sin = jnp.repeat(jnp.sin(freqs), 2, axis=-1)[:, :latent_dim]
            return (cos.astype(dtype), sin.astype(dtype))
        B, T, C = x.shape
        H = N_HEAD
        hd = C // H
        L = q2l_w.shape[0]
        qkv = x @ c_attn_w.T + c_attn_b
        q, k, v = jnp.split(qkv, 3, axis=2)

        def heads(t):
            return t.reshape(B, T, H, hd).transpose(0, 2, 1, 3)
        q, k, v = (heads(q), heads(k), heads(v))
        q_lat = q @ q2l_w.T + q2l_b
        k_lat = k @ kv2l_w.T + kv2l_b
        v_lat = v @ kv2l_w.T + kv2l_b
        cos, sin = _rope_tables(T, L, x.dtype)
        cos = cos[None, None]
        sin = sin[None, None]
        q_lat = q_lat * cos + _rotate_half(q_lat) * sin
        k_lat = k_lat * cos + _rotate_half(k_lat) * sin
        q_for_k = q_lat @ wqk_w.T + wqk_b
        att = jnp.einsum('bhql,bhkl->bhqk', q_for_k, k_lat) * L ** (-0.5)
        causal = jnp.tril(jnp.ones((T, T), dtype=bool))
        att = jnp.where(causal[None, None], att, -jnp.inf)
        att = jax.nn.softmax(att, axis=-1)
        y_lat = jnp.einsum('bhqk,bhkl->bhql', att, v_lat)
        y = y_lat @ l2o_w.T + l2o_b
        y = y.transpose(0, 2, 1, 3).reshape(B, T, C)
        return y @ cproj_w.T + cproj_b

    def _L0_ffn_ref(x, router_W, router_b, ln_g, ln_b, W1, b1, W2, b2):
        import jax, jax.numpy as jnp
        import numpy as np
        B, S, H, E, K = (2, 256, 128, 8, 2)
        FF = 4 * H
        EPS = 1e-05
        logits = x @ router_W + router_b
        w, idx = jax.lax.top_k(logits, K)
        w = jax.nn.softmax(w, axis=-1)
        gates = jnp.einsum('bske,bsk->bse', jax.nn.one_hot(idx, E, dtype=x.dtype), w)
        mu = jnp.mean(x, axis=-1, keepdims=True)
        var = jnp.mean(jnp.square(x - mu), axis=-1, keepdims=True)
        xhat = (x - mu) * jax.lax.rsqrt(var + EPS)
        h = xhat[:, :, None, :] * ln_g + ln_b
        a = jax.nn.gelu(jnp.einsum('bseh,ehf->bsef', h, W1) + b1, approximate=False)
        y = jnp.einsum('bsef,efh->bseh', a, W2) + b2
        y = y + x[:, :, None, :]
        out = jnp.einsum('bseh,bse->bsh', y, gates)
        return out
    x = L0_attn_x
    mod = (_silu(L0_c) @ L0_wmod).reshape(L0_c.shape[0], 6, 1, -1)
    sa, ca, ga, sb, cb, gb = (mod[:, 0], mod[:, 1], mod[:, 2], mod[:, 3], mod[:, 4], mod[:, 5])
    ga = (2 * (ga >= 0) - 1) * jnp.maximum(jnp.abs(ga), 0.25)
    gb = (2 * (gb >= 0) - 1) * jnp.maximum(jnp.abs(gb), 0.25)
    h = _layernorm(x, axis=-1) * (1 + ca) + sa
    x = x + ga * _L0_attn_ref(h, L0_attn_c_attn_w, L0_attn_c_attn_b, L0_attn_q2l_w, L0_attn_q2l_b, L0_attn_kv2l_w, L0_attn_kv2l_b, L0_attn_l2o_w, L0_attn_l2o_b, L0_attn_wqk_w, L0_attn_wqk_b, L0_attn_cproj_w, L0_attn_cproj_b)
    h = _layernorm(x, axis=-1) * (1 + cb) + sb
    x = x + gb * _L0_ffn_ref(h, L0_ffn_router_W, L0_ffn_router_b, L0_ffn_ln_g, L0_ffn_ln_b, L0_ffn_W1, L0_ffn_b1, L0_ffn_W2, L0_ffn_b2)
    return x

_drawn_inputs = setup_inputs


def setup_inputs(seed=0):
    import zlib

    import numpy as np

    out = dict(_drawn_inputs(seed))
    spreads = {'L0_attn_c_attn_b': (0.0, 0.8),
     'L0_attn_q2l_b': (0.0, 0.8),
     'L0_attn_kv2l_b': (0.0, 0.8),
     'L0_attn_l2o_b': (0.0, 0.677),
     'L0_attn_wqk_b': (0.0, 0.8),
     'L0_attn_cproj_b': (0.0, 0.283),
     'L0_ffn_router_b': (0.0, 0.312),
     'L0_ffn_ln_g': (1.0, 0.6),
     'L0_ffn_ln_b': (0.0, 0.65),
     'L0_ffn_b1': (0.0, 0.658),
     'L0_ffn_b2': (0.0, 0.454)}
    factors = {'L0_attn_c_attn_w': 8.0,
     'L0_attn_q2l_w': 8.0,
     'L0_attn_kv2l_w': 8.0,
     'L0_attn_l2o_w': 8.0,
     'L0_attn_wqk_w': 8.0,
     'L0_attn_cproj_w': 6.063}
    for name, (base, spread) in spreads.items():
        noise = np.random.default_rng([zlib.crc32(name.encode()), seed]).standard_normal(out[name].shape)
        drawn = base * np.exp(spread * noise) if base else spread * noise
        out[name] = jnp.asarray(drawn.astype(out[name].dtype))
    for name, factor in factors.items():
        out[name] = (out[name] * factor).astype(out[name].dtype)
    return out
```

```python
import concourse.bass as bass
from concourse import mybir
from contextlib import ExitStack

F32 = mybir.dt.float32
F32R = mybir.dt.float32r
BF16 = mybir.dt.bfloat16
U32 = mybir.dt.uint32
I32 = mybir.dt.int32
ALU = mybir.AluOpType
ACT = mybir.ActivationFunctionType
AX = mybir.AxisListType

B, T, C = 16, 512, 128
H, HD, L = 16, 8, 32
E, FF = 8, 512
P = 128
HG = P // L
NCH = H // HG
TT = T // P
VW = HD + 1
SCALE = float(L) ** -0.5
LN_EPS = 1e-5
RSQRT_MAGIC = 0x5F3759DF
MOD_SA, MOD_CA, MOD_GA, MOD_SB, MOD_CB, MOD_GB = range(6)

ROW_MAX = 3 * L

P_OFF = [0, 512, 1024, 896]
P_COLS = 1280
PIECES = 10
ST_BANK = [0, 1, 2, 0, 1, 2, 0, 1, 2, 1]
ST_BACK = [4, 2, 4, 3, 3, 3, 3, 3, 3, 2]
LN_STEPS = 14


def wait(eng, sem, n):
    if isinstance(n, int) and n <= 0:
        return
    eng.wait_ge(sem, n)


def piece(p):
    pair, q = divmod(p, 5)
    h = 2 * pair
    return [(0, [h]), (0, [h + 1]), (1, [h]), (1, [h + 1]), (2, [h, h + 1])][q]


SMALL = [("b_attn", 3), ("q2l_b", 1), ("kv2l_b", 1), ("wqk_b", 1), ("q2l_t", L), ("kv2l_t", L), ("wqk_t", L),
         ("cproj_t", C), ("ln_g_t", E), ("ln_b_t", E), ("b1_t", E * FF // P), ("cond_t", B)]
SMALL_AT = {name: (sum(w for _, w in SMALL[:n]), width) for n, (name, width) in enumerate(SMALL)}


def adaln_block(nc, x, w_attn, kv2l_h_d, kvb_col, l2o_t, l2o_b, cproj_b, router_w, router_b, w1, w2, b2, wmod,
                small, c_cos, c_sin, c_mats, c_masks, out):
    top = ExitStack()
    with top:
        def sb(ctx, name, shape, dt=F32):
            return ctx.enter_context(nc.sbuf_tensor(name, shape, dt))

        def sem(name):
            return top.enter_context(nc.semaphore(name))

        bank = [top.enter_context(nc.psum_tensor(f"bank{i}", [P, 512], F32)) for i in range(8)]

        d_mod = nc.dram_tensor("d_mod", [B, 4 * C], F32, kind="Internal").ap()
        d_xh = nc.dram_tensor("d_xh", [B * T, C], F32, kind="Internal").ap()
        d_base = nc.dram_tensor("d_base", [B * T, C], F32, kind="Internal").ap()
        d_gate = nc.dram_tensor("d_gate", [B * T, E], F32, kind="Internal").ap()

        par = sb(top, "par", [P, sum(w for _, w in SMALL)])

        def param(name):
            at, width = SMALL_AT[name]
            return par[:, at:at + width]

        attn = ExitStack()
        ident = sb(top, "ident", [P, P])
        cos_t = sb(attn, "cos_t", [P, T])
        sin_t = sb(attn, "sin_t", [P, T])
        ident_bf = sb(attn, "ident_bf", [P, P], BF16)
        mask_q = sb(attn, "mask_q", [P, P], BF16)
        mask_k = sb(attn, "mask_k", [P, P], BF16)
        iota_e = sb(attn, "iota_e", [P, E])
        wq = [sb(attn, f"wq{i}", [P, H * L], F32R) for i in range(2)]
        wk = [sb(attn, f"wk{i}", [P, H * L], F32R) for i in range(2)]
        wkr = [sb(attn, f"wkr{i}", [P, H * L], F32R) for i in range(2)]
        wv = [sb(attn, f"wv{i}", [P, C], F32R) for i in range(2)]
        wqk_c = sb(attn, "wqk_c", [P, P])
        wqk_s = sb(attn, "wqk_s", [P, P])
        bias_q = sb(attn, "bias_q", [P, NCH])
        bias_k = sb(attn, "bias_k", [P, NCH])
        bias_kr = sb(attn, "bias_kr", [P, NCH])
        bias_v = sb(attn, "bias_v", [P, C])
        bias_c = sb(attn, "bias_c", [P, C])
        wr = sb(attn, "wr", [P, E])
        bias_r = sb(attn, "bias_r", [P, E])
        mod_s = sb(attn, "mod_s", [P, B])
        mod_c = sb(attn, "mod_c", [P, B])

        setup = ExitStack()
        with attn:
            with setup:
                prepare(nc, setup, sb, sem, bank, locals())
            attention(nc, attn, sb, sem, bank, locals())
        feed_forward(nc, top, sb, sem, bank, locals())


def prepare(nc, ctx, sb, sem, bank, v):
    mats = sb(ctx, "mats", [P, 2 * P])
    rot = mats[:, P:2 * P]
    masks = sb(ctx, "masks", [P, 2 * P])
    sel = sb(ctx, "sel", [P, H + HG + E])
    wa = sb(ctx, "wa", [P, 3, C])
    par, param = v["par"], v["param"]
    ba = param("b_attn")
    q2l_r, kv2l_r = param("q2l_t"), param("kv2l_t")
    kv2l_h = sb(ctx, "kv2l_h", [L, H, HD])
    l2o_t = sb(ctx, "l2o_t", [L, HD])
    l2o_br = sb(ctx, "l2o_br", [P, HD])
    kvb = sb(ctx, "kvb", [L, 1])
    qbc, kbc, wqk_rep = param("q2l_b"), param("kv2l_b"), param("wqk_t")
    wqk_bd = sb(ctx, "wqk_bd", [P, L, HG])
    eq = sb(ctx, "eq", [P, NCH, L, HG])
    ek = sb(ctx, "ek", [P, NCH, L, HG])
    er = sb(ctx, "er", [P, NCH, L, HG])
    g_bd = sb(ctx, "g_bd", [P, H, HD])
    g_small = sb(ctx, "g_small", [P, HD])
    bv_rep = sb(ctx, "bv_rep", [P, P])
    kvb_rep = sb(ctx, "kvb_rep", [L, P])
    l2o_rep = sb(ctx, "l2o_rep", [L, H, HD])
    cin = param("cond_t")
    ce, cs, cst = sb(ctx, "ce", [P, B]), sb(ctx, "cs", [P, B]), sb(ctx, "cst", [P, B])
    wm = sb(ctx, "wm", [P, 6, C])
    rows = sb(ctx, "rows", [B, 4, C])
    absr = sb(ctx, "absr", [B, 2, C])
    sgn = sb(ctx, "sgn", [B, 2, C])
    full = sb(ctx, "full", [P, H * L])

    loaded = sem("setup_loaded")
    step = sem("setup_step")
    spread_ready, folded, folded_bias = sem("spread_ready"), sem("folded"), sem("folded_bias")
    bias_ready, wqk_ready, rotated = sem("bias_ready"), sem("wqk_ready"), sem("rotated")
    value_folded, g_ready = sem("value_folded"), sem("g_ready")
    exp_ready, silu_ready = sem("exp_ready"), sem("silu_ready")
    modulated, rows_ready, stored = sem("modulated"), sem("rows_ready"), sem("mod_rows_stored")
    n_loads = 0

    with nc.Block() as block:
        @block.sync
        def _(sp):
            nonlocal n_loads

            def load(dst, src):
                nonlocal n_loads
                sp.dma_start(dst, src).then_inc(loaded, 16)
                n_loads += 1

            load(mats[:], v["c_mats"])
            load(masks[:], v["c_masks"][:, 0:2 * P])
            load(sel[:], v["c_masks"][:, 2 * P:2 * P + H + HG + E])
            load(v["cos_t"][:], v["c_cos"])
            load(v["sin_t"][:], v["c_sin"])
            load(par[:], v["small"])
            load(wa[:], v["w_attn"].rearrange("(a p) c -> p a c", p=P))
            load(kv2l_h[:].rearrange("l h d -> l (h d)"), v["kv2l_h_d"])
            load(l2o_t[:], v["l2o_t"])
            load(l2o_br[:], v["l2o_b"].broadcast_to((P, HD)))
            load(kvb[:], v["kvb_col"])
            load(v["bias_c"][:], v["cproj_b"].broadcast_to((P, C)))
            load(v["wr"][:], v["router_w"])
            load(v["bias_r"][:], v["router_b"].broadcast_to((P, E)))
            load(wm[:], v["wmod"].rearrange("p (m c) -> p m c", c=C))
            sp.wait_ge(rows_ready, 1)
            sp.dma_start(v["d_mod"], rows[:].rearrange("b m c -> b (m c)")).then_inc(stored, 16)
            sp.wait_ge(stored, 16)

        head_of_row = sel[:, 0:H]
        head_in_chunk = sel[:, H:H + HG]
        flat = lambda ap: ap.rearrange("p c l h -> p (c l h)")

        @block.tensor
        def _(pe):
            pe.wait_ge(loaded, 16 * n_loads)
            for n, (rows_of, spread_w) in enumerate(((0, eq), (1, ek), (1, er))):
                pe.wait_ge(spread_ready, n + 1)
                pe.matmul(bank[n][:], wa[:, rows_of, :], flat(spread_w[:]), start=True, stop=True).then_inc(folded, 1)
            for n, spread_w in ((0, eq), (1, ek)):
                for c in range(NCH):
                    last = pe.matmul(bank[3][:, NCH * n + c:NCH * n + c + 1], spread_w[:, c].rearrange("p l h -> p (l h)"),
                                     ba[:, n:n + 1], start=True, stop=True)
            last.then_inc(folded_bias, 1)
            pe.wait_ge(bias_ready, 1)
            pe.matmul(bank[4][:, 0:NCH], rot, v["bias_k"][:], start=True, stop=True).then_inc(rotated, 1)
            pe.wait_ge(wqk_ready, 1)
            pe.matmul(bank[5][:, 0:P], rot, v["wqk_c"][:], start=True, stop=True).then_inc(rotated, 1)
            pe.matmul(bank[6][:, 0:HD], kv2l_h[:].rearrange("l h d -> l (h d)"), l2o_t[:],
                      start=True, stop=True).then_inc(value_folded, 1)
            pe.wait_ge(g_ready, 1)
            pe.matmul(bank[6][:, 0:C], wa[:, 2, :], g_bd[:].rearrange("p h d -> p (h d)"), start=True, stop=True)
            pe.matmul(bank[7][:, 0:C], bv_rep[:], g_bd[:].rearrange("p h d -> p (h d)"), start=True, stop=False)
            pe.matmul(bank[7][:, 0:C], kvb_rep[:], l2o_rep[:].rearrange("l h d -> l (h d)"),
                      start=False, stop=True).then_inc(value_folded, 1)
            pe.wait_ge(silu_ready, 1)
            pe.matmul(bank[0][:, 0:B], wm[:, MOD_SA, :], cst[:], start=True, stop=True)
            pe.matmul(bank[1][:, 0:B], wm[:, MOD_CA, :], cst[:], start=True, stop=True)
            pe.matmul(bank[2][0:B, :], cst[:], wm[:, MOD_GA:, :].rearrange("p m c -> p (m c)"),
                      start=True, stop=True).then_inc(modulated, 1)

        @block.scalar
        def _(act):
            act.wait_ge(loaded, 16 * n_loads)
            act.activation(ce[:], cin, ACT.Exp, scale=-1.0).then_inc(exp_ready, 1)

        @block.vector
        def _(dve):
            steps = 0

            def link(ins):
                nonlocal steps
                steps += 1
                ins.then_inc(step, 1)
                dve.wait_ge(step, steps)

            dve.wait_ge(loaded, 16 * n_loads)
            dve.tensor_copy(v["ident"][:], mats[:, 0:P])
            dve.tensor_copy(v["ident_bf"][:], mats[:, 0:P])
            dve.tensor_copy(v["mask_q"][:], masks[:, 0:P])
            dve.tensor_copy(v["mask_k"][:], masks[:, P:2 * P])
            dve.tensor_copy(v["iota_e"][:], sel[:, H + HG:H + HG + E])
            for dst, src in ((eq, q2l_r), (ek, kv2l_r)):
                for c in range(NCH):
                    ins = dve.tensor_tensor(
                        dst[:, c], src.unsqueeze(2).broadcast_to((P, L, HG)),
                        head_of_row[:, HG * c:HG * c + HG].unsqueeze(1).broadcast_to((P, L, HG)), ALU.mult)
                link(ins)
                dve.sem_inc(spread_ready, 1)
            for c in range(NCH):
                dve.tensor_scalar(er[:, c, 0:L:2, :], ek[:, c, 1:L:2, :], -1.0, None, ALU.mult)
                ins = dve.tensor_copy(er[:, c, 1:L:2, :], ek[:, c, 0:L:2, :])
            ins.then_inc(spread_ready, 1)
            link(dve.tensor_tensor(wqk_bd[:], wqk_rep.unsqueeze(2).broadcast_to((P, L, HG)),
                                   head_in_chunk.unsqueeze(1).broadcast_to((P, L, HG)), ALU.mult))
            dve.tensor_copy(v["wqk_c"][:], wqk_bd[:].rearrange("p l h -> p (l h)")).then_inc(wqk_ready, 1)
            dve.tensor_copy(bv_rep[:], ba[:, 2:3].broadcast_to((P, P)))
            dve.tensor_copy(kvb_rep[:], kvb[:].broadcast_to((L, P)))
            dve.tensor_copy(l2o_rep[:], l2o_t[:].unsqueeze(1).broadcast_to((L, H, HD)))
            for n, dst in enumerate((v["wq"], v["wk"], v["wkr"])):
                dve.wait_ge(folded, n + 1)
                link(dve.tensor_copy(full[:], bank[n][:]))
                link(dve.tensor_copy(dst[0][:], full[:]))
                link(dve.tensor_tensor(dst[1][:], full[:], dst[0][:].bitcast(F32), ALU.subtract))
            dve.wait_ge(folded_bias, 1)
            dve.tensor_scalar(v["bias_q"][:], bank[3][:, 0:NCH], qbc, None, ALU.add)
            dve.tensor_scalar(v["bias_k"][:], bank[3][:, NCH:2 * NCH], kbc, None, ALU.add).then_inc(bias_ready, 1)
            dve.wait_ge(rotated, 2)
            dve.tensor_scalar(v["bias_kr"][:], bank[4][:, 0:NCH], -1.0, None, ALU.mult)
            dve.tensor_copy(v["wqk_s"][:], bank[5][:, 0:P])
            dve.wait_ge(value_folded, 1)
            link(dve.tensor_copy(g_small[:], bank[6][:, 0:HD]))
            dve.tensor_tensor(g_bd[:], g_small[:].unsqueeze(1).broadcast_to((P, H, HD)),
                              head_of_row.unsqueeze(2).broadcast_to((P, H, HD)), ALU.mult).then_inc(g_ready, 1)
            dve.wait_ge(value_folded, 2)
            link(dve.tensor_copy(full[:, 0:C], bank[6][:, 0:C]))
            link(dve.tensor_copy(v["wv"][0][:], full[:, 0:C]))
            dve.tensor_tensor(v["wv"][1][:], full[:, 0:C], v["wv"][0][:].bitcast(F32), ALU.subtract)
            dve.tensor_tensor(v["bias_v"][:].rearrange("p (h d) -> p h d", d=HD),
                              bank[7][:, 0:C].rearrange("p (h d) -> p h d", d=HD),
                              l2o_br[:].unsqueeze(1).broadcast_to((P, H, HD)), ALU.add)
            dve.wait_ge(exp_ready, 1)
            link(dve.tensor_scalar(ce[:], ce[:], 1.0, None, ALU.add))
            link(dve.reciprocal(cs[:], ce[:]))
            dve.tensor_tensor(cst[:], cs[:], cin, ALU.mult).then_inc(silu_ready, 1)
            dve.wait_ge(modulated, 1)
            dve.tensor_copy(v["mod_s"][:], bank[0][:, 0:B])
            dve.tensor_scalar(v["mod_c"][:], bank[1][:, 0:B], 1.0, None, ALU.add)
            link(dve.tensor_copy(rows[:], bank[2][0:B, :].rearrange("b (m c) -> b m c", c=C)))
            link(dve.tensor_scalar(rows[:, 2, :], rows[:, 2, :], 1.0, None, ALU.add))
            link(dve.tensor_scalar(absr[:], rows[:, 0:4:3, :], -1.0, None, ALU.mult))
            link(dve.tensor_tensor(absr[:], absr[:], rows[:, 0:4:3, :], ALU.max))
            link(dve.tensor_scalar(absr[:], absr[:], 0.25, None, ALU.max))
            link(dve.tensor_scalar(sgn[:], rows[:, 0:4:3, :], 0.0, None, ALU.is_ge))
            link(dve.tensor_scalar(sgn[:], sgn[:], 2.0, -1.0, ALU.mult, ALU.add))
            dve.tensor_tensor(rows[:, 0:4:3, :], absr[:], sgn[:], ALU.mult).then_inc(rows_ready, 1)


def attention(nc, ctx, sb, sem, bank, v):
    ident = v["ident"]
    qs = [sb(ctx, f"q_stack{c}", [P, HG * T], F32R) for c in range(NCH)]
    ks = [sb(ctx, f"k_stack{c}", [P, HG * T], F32R) for c in range(NCH)]
    zero2 = sb(ctx, "zero2", [2, HG * T], F32R)
    prob = [sb(ctx, f"prob{i}", [P, HG * P_COLS]) for i in range(2)]
    u_sb = sb(ctx, "u_sb", [P, NCH, T])
    x_in = sb(ctx, "x_in", [P, TT, C])
    xn = sb(ctx, "xn", [P, TT, C])
    hf = sb(ctx, "hf", [P, T])
    hh, hl = sb(ctx, "hh", [P, T], F32R), sb(ctx, "hl", [P, T], F32R)
    q_cos, q_sin = sb(ctx, "q_cos", [P, T]), sb(ctx, "q_sin", [P, T])
    k_cos, k_sin, k_sum = sb(ctx, "k_cos", [P, T]), sb(ctx, "k_sin", [P, T]), sb(ctx, "k_sum", [P, T])
    qh, ql = sb(ctx, "qh", [P, T], F32R), sb(ctx, "ql", [P, T], F32R)
    kh, kl = sb(ctx, "kh", [P, T], F32R), sb(ctx, "kl", [P, T], F32R)
    vx = [sb(ctx, f"vx{i}", [P, TT, H, VW]) for i in range(2)]
    mx = [sb(ctx, f"mx{i}", [P, HG * TT]) for i in range(2)]
    mh, ml = sb(ctx, "mh", [HG * TT, P], F32R), sb(ctx, "ml", [HG * TT, P], F32R)
    y = sb(ctx, "y", [P, TT, C])
    rden = sb(ctx, "rden", [P, TT, H])
    y_t = sb(ctx, "y_t", [P, T])
    x_res = sb(ctx, "x_res", [P, TT, C])
    mod_b = sb(ctx, "mod_b", [P, 4, C])
    wc_g, bias_cg = sb(ctx, "wc_g", [P, C]), sb(ctx, "bias_cg", [P, C])
    xb = sb(ctx, "xb", [P, TT, C])
    x1 = sb(ctx, "x1", [P, TT, C])
    xn2 = sb(ctx, "xn2", [P, TT, C])
    h2 = sb(ctx, "h2", [P, TT, C])
    h2_t = sb(ctx, "h2_t", [P, T])
    xh = sb(ctx, "xh", [P, TT, C])
    base = sb(ctx, "base", [P, TT, C])
    gate = sb(ctx, "gate", [P, TT, E])
    lg = sb(ctx, "lg", [P, TT, E])
    top8 = sb(ctx, "top8", [P, TT, 8])
    idx8 = sb(ctx, "idx8", [P, TT, 8], U32)
    idxf = sb(ctx, "idxf", [P, TT, 2])
    hot = sb(ctx, "hot", [P, 2, TT, E])
    gdiff, gexp = sb(ctx, "gdiff", [P, TT]), sb(ctx, "gexp", [P, TT])
    gden, gw, gsum = sb(ctx, "gden", [P, TT]), sb(ctx, "gw", [P, 2, TT]), sb(ctx, "gsum", [P, TT])
    ln = [dict(st=sb(ctx, f"ln_st{i}", [P, TT, 6]), mv=sb(ctx, f"ln_mv{i}", [P, TT, 2]),
               va=sb(ctx, f"ln_va{i}", [P, TT]), hb=sb(ctx, f"ln_hb{i}", [P, TT], I32),
               y=sb(ctx, f"ln_y{i}", [P, TT]), t=sb(ctx, f"ln_t{i}", [P, TT])) for i in range(3)]

    s_bank, st_bank, u_bank, f_bank, side = bank[0:2], bank[2:5], bank[5], bank[6], bank[7]

    x_loaded, t_loaded, outs_stored = sem("x_loaded"), sem("t_loaded"), sem("outs_stored")
    const_ready = sem("const_ready")
    stack_ready = [sem(f"stack_ready{c}") for c in range(NCH)]
    rows_ready = [sem(f"max_rows_ready{c}") for c in range(NCH)]
    xn_ready, xt_ready, hf_ready, h_ready = sem("xn_ready"), sem("xt_ready"), sem("hf_ready"), sem("h_ready")
    v_ready, v_used = sem("v_ready"), sem("v_used")
    f_ready, f_used = sem("f_ready"), sem("f_used")
    qh_ready, ksum_ready, kh_ready, kl_ready = sem("qh_ready"), sem("ksum_ready"), sem("kh_ready"), sem("kl_ready")
    s_ready, s_used = sem("s_ready"), sem("s_used")
    mt_ready, mh_ready, mt_used = sem("mt_ready"), sem("mh_ready"), sem("mt_used")
    st_ready, st_used = sem("st_ready"), sem("st_used")
    av_ready, u_copied = sem("av_ready"), sem("u_copied")
    ut_ready, ut_used = sem("ut_ready"), sem("ut_used")
    rden_ready = sem("rden_ready")
    yt_ready, yt_used = sem("yt_ready"), sem("yt_used")
    bcg_ready, xb_ready = sem("bcg_ready"), sem("xb_ready")
    proj_ready, x1_ready = sem("proj_ready"), sem("x1_ready")
    xn2_ready, h2m_ready, h2_ready = sem("xn2_ready"), sem("h2m_ready"), sem("h2_ready")
    held = sem("held")
    ht_ready, ht_used = sem("ht_ready"), sem("ht_used")
    xh_ready, gh_ready, base_ready = sem("xh_ready"), sem("gh_ready"), sem("base_ready")
    lg_ready, lg_used = sem("lg_ready"), sem("lg_used")
    gdiff_ready, gexp_ready, gate_ready = sem("gdiff_ready"), sem("gexp_ready"), sem("gate_ready")
    ln_step = [sem(f"ln_step{i}") for i in range(3)]
    rt_step = sem("router_step")
    RT_STEPS = 8

    def at(b, c, ahead):
        return b + (c + ahead) // NCH, (c + ahead) % NCH

    def exists(c, ahead, last):
        return not last or c + ahead < NCH

    def pe_scores(pe, stacks, out, h, tile, col, wide_queries):
        q, k = stacks
        o = h * T
        if wide_queries:
            n = T - P * tile
            pe.matmul(out[:, col:col + n], k[:, o + P * tile:o + P * tile + P], q[:, o + P * tile:o + T],
                      start=(col == 0), stop=False, skip_group_check=True)
            return col
        n = P * (tile + 1)
        pe.matmul(out[:, col:col + n], q[:, o + P * tile:o + P * tile + P], k[:, o:o + n],
                  start=(col == 0), stop=False, skip_group_check=True)
        return col + n - P

    def pe_piece(pe, c, p, out, wide_queries):
        kind, heads = piece(p)
        stacks = qs[c], ks[c]
        mask = v["mask_k"] if wide_queries else v["mask_q"]
        tiles = {0: [0], 1: [1, 3], 2: [2]} if wide_queries else {0: [3], 1: [2, 0], 2: [1]}
        diag, col = [], 0
        for h in heads:
            for tile in tiles[kind]:
                diag.append(pe_scores(pe, stacks, out, h, tile, col, wide_queries))
                col += T - P * tile if wide_queries else P * (tile + 1)
        if len(diag) == 1:
            return pe.matmul(out[:, diag[0]:diag[0] + P], v["ident_bf"][:], mask[:],
                             start=False, stop=True, skip_group_check=True)
        gap = diag[1] - diag[0]
        if gap == P:
            dst = out[:, diag[0]:diag[0] + 2 * P].rearrange("p (a q) -> p a q", a=2)
        elif diag[0] + 2 * gap <= 512:
            dst = out[:, diag[0]:diag[0] + 2 * gap].rearrange("p (a q) -> p a q", a=2)[:, :, 0:P]
        else:
            dst = None
        if dst is None:
            for d in diag:
                ins = pe.matmul(out[:, d:d + P], v["ident_bf"][:], mask[:], start=False, stop=True,
                                skip_group_check=True)
            return ins
        return pe.matmul(dst, v["ident_bf"][:], mask[:].unsqueeze(1).broadcast_to((P, 2, P)),
                         start=False, stop=True, skip_group_check=True)

    def pe_s(pe, b, c, p):
        n = NCH * b + c
        if p == 0:
            wait(pe, stack_ready[c], 112 * (b + 1))
        wait(pe, s_used, PIECES * n + p - 1)
        pe_piece(pe, c, p, s_bank[p % 2], False).then_inc(s_ready, 1)

    def pe_st(pe, b, c, p):
        n = NCH * b + c
        if p == 0:
            wait(pe, rows_ready[c], 32 * (b + 1))
        wait(pe, st_used, PIECES * n + p - ST_BACK[p] + 1)
        pe_piece(pe, c, p, st_bank[ST_BANK[p]], True).then_inc(st_ready, 1)

    def pe_av(pe, b, c, odd, j):
        n = NCH * b + c
        if j == 0:
            wait(pe, st_used, PIECES * (n + 1))
            wait(pe, v_ready, b + 1)
            wait(pe, u_copied, n)
        for h in range(HG):
            ins = pe.matmul(u_bank[L * h:L * h + VW, P * j:T], vx[odd][:, j, HG * c + h, :],
                            prob[c % 2][:, P_COLS * h + P_OFF[j]:P_COLS * h + P_OFF[j] + T - P * j],
                            start=(j == 0), stop=(j == TT - 1), skip_group_check=True)
        if j == TT - 1:
            ins.then_inc(av_ready, 1)

    def three(pe, out, w, x, start=True, stop=True):
        pe.matmul(out, w[0], x[0], start=start, stop=False)
        pe.matmul(out, w[0], x[1], start=False, stop=False)
        return pe.matmul(out, w[1], x[0], start=False, stop=stop)

    def pe_f(pe, b, c, part):
        n = NCH * b + c
        wait(pe, f_used, 4 * n + part)
        if part == 3:
            pe.matmul(f_bank[:], v["wqk_c"][:], q_cos[:], start=True, stop=False)
            ins = pe.matmul(f_bank[:], v["wqk_s"][:], q_sin[:], start=False, stop=True)
        else:
            wait(pe, h_ready, b + 1)
            w = (v["wq"], v["wk"], v["wkr"])[part]
            ins = three(pe, f_bank[:], [m[:, P * c:P * c + P] for m in w], [hh[:], hl[:]])
        ins.then_inc(f_ready, 1)

    side_last = [None]

    def side_take(pe):
        if side_last[0] is not None:
            wait(pe, *side_last[0])

    def pe_mt(pe, b, c):
        side_take(pe)
        n = NCH * b + c
        wait(pe, s_used, PIECES * (n + 1))
        pe.transpose(side[0:HG * TT, 0:P], mx[c % 2][:], ident[:]).then_inc(mt_ready, 1)
        side_last[0] = (mt_used, n + 1)

    def pe_xt(pe, b):
        side_take(pe)
        wait(pe, xn_ready, b + 1)
        for t in range(TT):
            ins = pe.transpose(side[:, P * t:P * t + P], xn[:, t, :], ident[:])
        ins.then_inc(xt_ready, 1)
        side_last[0] = (hf_ready, b + 1)

    def pe_v(pe, b):
        side_take(pe)
        wait(pe, h_ready, b + 1)
        for t in range(TT):
            s = slice(P * t, P * t + P)
            ins = three(pe, side[:, s], [hh[:, s], hl[:, s]], [v["wv"][0][:], v["wv"][1][:]])
        ins.then_inc(v_used, 1)
        side_last[0] = (v_ready, b + 1)

    def pe_ut(pe, b, t):
        side_take(pe)
        if t == 0:
            wait(pe, u_copied, NCH * (b + 1))
        for c in range(NCH):
            ins = pe.transpose(side[:, P * c:P * c + P], u_sb[:, c, P * t:P * t + P], ident[:])
        ins.then_inc(ut_ready, 1)
        side_last[0] = (ut_used, TT * b + t + 1)

    def pe_yt(pe, b):
        side_take(pe)
        for t in range(TT):
            ins = pe.transpose(side[:, P * t:P * t + P], y[:, t, :], ident[:])
        ins.then_inc(yt_ready, 1)
        side_last[0] = (yt_used, b + 1)

    def pe_proj(pe, b):
        side_take(pe)
        wait(pe, yt_used, b + 1)
        wait(pe, bcg_ready, b + 1)
        for t in range(TT):
            s = slice(P * t, P * t + P)
            ins = pe.matmul(side[:, s], y_t[:, s], wc_g[:], start=True, stop=True)
        ins.then_inc(proj_ready, 1)
        side_last[0] = (x1_ready, b + 1)

    def pe_ht(pe, b):
        side_take(pe)
        wait(pe, h2_ready, b + 1)
        for t in range(TT):
            ins = pe.transpose(side[:, P * t:P * t + P], h2[:, t, :], ident[:])
        ins.then_inc(ht_ready, 1)
        side_last[0] = (ht_used, b + 1)

    def pe_lg(pe, b):
        side_take(pe)
        wait(pe, ht_used, b + 1)
        for t in range(TT):
            ins = pe.matmul(side[:, E * t:E * t + E], h2_t[:, P * t:P * t + P], v["wr"][:], start=True, stop=True)
        ins.then_inc(lg_ready, 1)
        side_last[0] = (lg_used, b + 1)

    def pe_slot(pe, b, c, odd, first, last):
        for p in range(PIECES):
            pe_st(pe, b, c, p)
            if exists(c, 2, last):
                pe_s(pe, *at(b, c, 2), p)
            if 1 <= p <= 4 and not (first and c == 0):
                pe_av(pe, *at(b, c, -1), odd if c else 1 - odd, p - 1)
            if exists(c, 3, last) and p in (0, 1, 2, 4):
                pe_f(pe, *at(b, c, 3), (0, 1, 2, 4).index(p))
            if c == 3 and p == 0 and not first:
                pe_lg(pe, b - 1)
            if p == 1 and exists(c, 1, last):
                pe_mt(pe, *at(b, c, 1))
            if c == 0 and not last:
                if p == 5:
                    pe_xt(pe, b + 1)
                if p == 8:
                    pe_v(pe, b + 1)
            if c == 1 and not first:
                if p in (3, 5, 6, 7):
                    pe_ut(pe, b - 1, (3, 5, 6, 7).index(p))
                if p == 9:
                    pe_yt(pe, b - 1)
            if c == 2 and not first:
                if p == 3:
                    pe_proj(pe, b - 1)
                if p == 8:
                    pe_ht(pe, b - 1)

    def pe_open(pe):
        pe_xt(pe, 0)
        pe_v(pe, 0)
        for c in range(3):
            for part in range(4):
                pe_f(pe, 0, c, part)
            if c >= 1:
                for p in range(PIECES):
                    pe_s(pe, 0, c - 1, p)
            if c == 1:
                pe_mt(pe, 0, 0)

    def pe_close(pe, b):
        for j in range(TT):
            pe_av(pe, b, NCH - 1, b % 2, j)
        for t in range(TT):
            pe_ut(pe, b, t)
        pe_yt(pe, b)
        pe_proj(pe, b)
        pe_ht(pe, b)
        pe_lg(pe, b)

    def act_exp(act, b, c, p):
        n = NCH * b + c
        if p == 0:
            wait(act, av_ready, n - 1)
        wait(act, st_ready, PIECES * n + p + 1)
        kind, heads = piece(p)
        src, h = st_bank[ST_BANK[p]], heads[0]
        pb = prob[c % 2]
        if kind == 2:
            dst = pb[:, P_COLS * h:P_COLS * (h + 2)].rearrange("p (a n) -> p a n", a=2)[:, :, P_OFF[2]:P_OFF[2] + 2 * P]
            act.activation(dst, src[:].rearrange("p (a n) -> p a n", a=2), ACT.Exp, scale=SCALE).then_inc(st_used, 1)
        else:
            o = P_COLS * h + (P_OFF[0] if kind == 0 else P_OFF[1])
            act.activation(pb[:, o:o + T], src[:], ACT.Exp, scale=SCALE).then_inc(st_used, 1)

    def act_u(act, b, c, ut_done):
        n = NCH * b + c
        wait(act, av_ready, n + 1)
        wait(act, ut_ready, ut_done)
        act.activation(u_sb[:, c, :], u_bank[:], ACT.Copy).then_inc(u_copied, 1)

    def act_qh(act, b, c):
        n = NCH * b + c
        wait(act, f_ready, 4 * n + 4)
        pb, pc = at(b, c, -1)
        wait(act, stack_ready[pc], 112 * (pb + 1))
        act.activation(qh[:], f_bank[:], ACT.Identity, bias=v["param"]("wqk_b")).then_inc(qh_ready, 1)

    def act_kh(act, b, c):
        n = NCH * b + c
        wait(act, ksum_ready, n + 1)
        pb, pc = at(b, c, -1)
        wait(act, stack_ready[pc], 112 * (pb + 1))
        act.activation(kh[:], k_sum[:], ACT.Copy).then_inc(kh_ready, 1)

    def act_mh(act, b, c):
        n = NCH * b + c
        wait(act, mt_ready, n + 1)
        pb, pc = at(b, c, -1)
        wait(act, rows_ready[pc], 32 * (pb + 1))
        act.activation(mh[:], side[0:HG * TT, 0:P], ACT.Copy).then_inc(mh_ready, 1)

    def act_hf(act, b):
        wait(act, xt_ready, b + 1)
        wait(act, h_ready, b)
        wait(act, f_ready, 16 * b)
        wait(act, v_used, b)
        act.activation(hf[:], side[:], ACT.Identity, bias=col(v["mod_s"], b), scale=col(v["mod_c"], b))
        act.activation(hh[:], side[:], ACT.Identity, bias=col(v["mod_s"], b), scale=col(v["mod_c"], b))\
           .then_inc(hf_ready, 1)

    def col(t, b):
        return t[:, b:b + 1] if isinstance(b, int) else t[:, bass.ds(b, 1)]

    def act_yt(act, b):
        wait(act, yt_ready, b + 1)
        wait(act, proj_ready, b)
        act.activation(y_t[:], side[:], ACT.Copy).then_inc(yt_used, 1)

    def act_ht(act, b):
        wait(act, ht_ready, b + 1)
        wait(act, lg_ready, b)
        act.activation(h2_t[:], side[:], ACT.Copy).then_inc(ht_used, 1)

    def act_gexp(act, b):
        wait(act, gdiff_ready, b + 1)
        wait(act, gate_ready, b)
        act.activation(gexp[:], gdiff[:], ACT.Exp).then_inc(gexp_ready, 1)

    def act_slot(act, b, c, odd, first, last):
        for p in range(PIECES):
            act_exp(act, b, c, p)
            if exists(c, 3, last):
                if p == 4:
                    act_kh(act, *at(b, c, 3))
                    act_qh(act, *at(b, c, 3))
            if p == 1 and exists(c, 1, last):
                act_mh(act, *at(b, c, 1))
            if c == 0 and not last and p == 5:
                act_hf(act, b + 1)
            if p == 8 and not (first and c == 0):
                pb, pc = at(b, c, -1)
                act_u(act, pb, pc, TT * pb)
            if c == 1 and p == 9 and not first:
                act_yt(act, b - 1)
            if c == 2 and p == 9 and not first:
                act_ht(act, b - 1)
            if c == 3 and p == 3 and not first:
                act_gexp(act, b - 1)

    def act_open(act):
        act_hf(act, 0)
        for c in range(3):
            act_kh(act, 0, c)
            act_qh(act, 0, c)
            if c == 1:
                act_mh(act, 0, 0)

    def act_close(act, b):
        act_u(act, b, NCH - 1, TT * b)
        act_yt(act, b)
        act_ht(act, b)
        act_gexp(act, b)

    def dve_max(dve, b, c, p):
        n = NCH * b + c
        if p == 0:
            wait(dve, mt_ready, n - 1)
        wait(dve, s_ready, PIECES * n + p + 1)
        kind, heads = piece(p)
        src, h, m = s_bank[p % 2], heads[0], mx[c % 2]
        if kind == 0:
            ins = dve.tensor_reduce(m[:, TT * h + 3:TT * h + 4], src[:], AX.X, ALU.max, negate=True)
        elif kind == 1:
            dve.tensor_reduce(m[:, TT * h + 2:TT * h + 3], src[:, 0:3 * P], AX.X, ALU.max, negate=True)
            ins = dve.tensor_reduce(m[:, TT * h:TT * h + 1], src[:, 3 * P:4 * P], AX.X, ALU.max, negate=True)
        else:
            ins = dve.tensor_reduce(m[:, TT * h + 1:TT * h + 2 + TT:TT], src[:].rearrange("p (a n) -> p a n", a=2),
                                    AX.X, ALU.max, negate=True)
        ins.then_inc(s_used, 1)

    def dve_ml(dve, b, c):
        n = NCH * b + c
        wait(dve, mh_ready, n + 1)
        dve.tensor_tensor(ml[:], side[0:HG * TT, 0:P], mh[:].bitcast(F32), ALU.subtract).then_inc(mt_used, 1)

    def dve_f(dve, b, c, part):
        n = NCH * b + c
        wait(dve, f_ready, 4 * n + part + 1)
        if part == 0:
            dve.scalar_tensor_tensor(q_cos[:], f_bank[:], v["bias_q"][:, c:c + 1], v["cos_t"][:], ALU.add, ALU.mult)
            dve.scalar_tensor_tensor(q_sin[:], f_bank[:], v["bias_q"][:, c:c + 1], v["sin_t"][:], ALU.add, ALU.mult)\
               .then_inc(f_used, 1)
        elif part == 1:
            wait(dve, ksum_ready, n)
            dve.scalar_tensor_tensor(k_cos[:], f_bank[:], v["bias_k"][:, c:c + 1], v["cos_t"][:], ALU.add, ALU.mult)\
               .then_inc(f_used, 1)
        elif part == 2:
            dve.scalar_tensor_tensor(k_sin[:], f_bank[:], v["bias_kr"][:, c:c + 1], v["sin_t"][:], ALU.add, ALU.mult)\
               .then_inc(f_used, 1)
        else:
            wait(dve, qh_ready, n + 1)
            dve.scalar_tensor_tensor(ql[:], f_bank[:], v["param"]("wqk_b"), qh[:].bitcast(F32), ALU.add, ALU.subtract)\
               .then_inc(f_used, 1)

    def dve_norm(dve, b, i, src, dst, done):
        w = ln[i]
        at_step = [0]

        def link(ins):
            at_step[0] += 1
            ins.then_inc(ln_step[i], 1)
            wait(dve, ln_step[i], LN_STEPS * b + at_step[0])

        for t in range(TT):
            ins = dve.bn_stats(w["st"][:, t, :], src[:, t, :])
        link(ins)
        dve.sem_inc(held, 1)
        for t in range(TT):
            ins = dve.bn_aggr(w["mv"][:, t, :], w["st"][:, t, :])
        link(ins)
        link(dve.tensor_scalar(w["va"][:], w["mv"][:, :, 1], LN_EPS, None, ALU.add))
        link(dve.tensor_scalar(w["hb"][:], w["va"][:].bitcast(I32), 1, None, ALU.logical_shift_right))
        link(dve.tensor_scalar(w["y"][:].bitcast(I32), w["hb"][:], -1.0, float(RSQRT_MAGIC), ALU.mult, ALU.add))
        for _ in range(3):
            link(dve.scalar_tensor_tensor(w["t"][:], w["y"][:], -0.5, w["y"][:], ALU.mult, ALU.mult))
            link(dve.tensor_tensor(w["t"][:], w["t"][:], w["va"][:], ALU.mult))
            link(dve.scalar_tensor_tensor(w["y"][:], w["t"][:], 1.5, w["y"][:], ALU.add, ALU.mult))
        assert at_step[0] == LN_STEPS
        for t in range(TT):
            ins = dve.tensor_scalar(dst[:, t, :], src[:, t, :], w["mv"][:, t, 0:1], w["y"][:, t:t + 1],
                                    ALU.subtract, ALU.mult)
        ins.then_inc(done, 1)

    def dve_l(dve, b):
        wait(dve, x_loaded, 16 * (b + 1))
        wait(dve, xt_ready, b)
        dve_norm(dve, b, 0, x_in, xn, xn_ready)

    def dve_v(dve, b, odd):
        wait(dve, v_used, b + 1)
        wait(dve, av_ready, NCH * (b - 1))
        dve.tensor_tensor(vx[odd][:, :, :, 0:HD], side[:].rearrange("p (t h d) -> p t h d", t=TT, d=HD),
                          v["bias_v"][:].rearrange("p (h d) -> p h d", d=HD).unsqueeze(1).broadcast_to((P, TT, H, HD)),
                          ALU.add).then_inc(v_ready, 1)

    def dve_ut(dve, b, t):
        wait(dve, ut_ready, TT * b + t + 1)
        if t == 0:
            wait(dve, yt_ready, b)
        heads = side[:].rearrange("p (h l) -> p h l", l=L)
        dve.reciprocal(rden[:, t, :], heads[:, :, HD]).then_inc(rden_ready, 1)
        wait(dve, rden_ready, TT * b + t + 1)
        dve.tensor_tensor(y[:, t, :].rearrange("p (h d) -> p h d", d=HD), heads[:, :, 0:HD],
                          rden[:, t, :].unsqueeze(2).broadcast_to((P, H, HD)), ALU.mult).then_inc(ut_used, 1)

    def dve_x1(dve, b):
        wait(dve, proj_ready, b + 1)
        wait(dve, xb_ready, b + 1)
        dve.tensor_tensor(x1[:].rearrange("p t c -> p (t c)"), side[:], xb[:].rearrange("p t c -> p (t c)"), ALU.add)\
           .then_inc(x1_ready, 1)
        wait(dve, x1_ready, b + 1)
        dve_norm(dve, b, 1, x1, xn2, xn2_ready)

    def dve_xh(dve, b):
        wait(dve, h2_ready, b + 1)
        wait(dve, outs_stored, 48 * b)
        dve_norm(dve, b, 2, h2, xh, xh_ready)

    def dve_lg(dve, b):
        wait(dve, lg_ready, b + 1)
        dve.tensor_tensor(lg[:], side[:, 0:TT * E].rearrange("p (t e) -> p t e", e=E),
                          v["bias_r"][:].unsqueeze(1).broadcast_to((P, TT, E)), ALU.add).then_inc(lg_used, 1)

    def dve_router(dve, b):
        at_step = [0]

        def link(ins):
            at_step[0] += 1
            ins.then_inc(rt_step, 1)
            wait(dve, rt_step, RT_STEPS * b + at_step[0])

        wait(dve, lg_used, b + 1)
        dve.sem_inc(held, 1)
        for t in range(TT):
            ins = dve.max(top8[:, t, :], lg[:, t, :])
        link(ins)
        dve.tensor_tensor(gdiff[:], top8[:, :, 1], top8[:, :, 0], ALU.subtract).then_inc(gdiff_ready, 1)
        for t in range(TT):
            ins = dve.max_index(idx8[:, t, :], top8[:, t, :], lg[:, t, :])
        link(ins)
        link(dve.tensor_copy(idxf[:], idx8[:, :, 0:2]))
        for k in range(2):
            ins = dve.tensor_tensor(hot[:, k], v["iota_e"][:].unsqueeze(1).broadcast_to((P, TT, E)),
                                    idxf[:, :, k:k + 1].broadcast_to((P, TT, E)), ALU.is_equal)
        wait(dve, gexp_ready, b + 1)
        link(dve.tensor_scalar(gden[:], gexp[:], 1.0, None, ALU.add))
        link(dve.reciprocal(gw[:, 0], gden[:]))
        link(dve.tensor_tensor(gw[:, 1], gw[:, 0], gexp[:], ALU.mult))
        link(dve.tensor_tensor(gsum[:], gw[:, 0], gw[:, 1], ALU.add))
        for k in range(2):
            ins = dve.tensor_tensor(hot[:, k], hot[:, k], gw[:, k].unsqueeze(2).broadcast_to((P, TT, E)), ALU.mult)
        link(ins)
        wait(dve, outs_stored, 48 * b)
        dve.tensor_tensor(gate[:], hot[:, 0], hot[:, 1], ALU.add).then_inc(gate_ready, 1)
        wait(dve, gh_ready, b + 1)
        for t in range(TT):
            ins = dve.scalar_tensor_tensor(base[:, t, :], xn2[:, t, :], gsum[:, t:t + 1], x1[:, t, :], ALU.mult, ALU.add)
        ins.then_inc(base_ready, 1)

    def dve_slot(dve, b, c, odd, first, last):
        for p in range(PIECES):
            if exists(c, 2, last):
                dve_max(dve, *at(b, c, 2), p)
            if exists(c, 3, last) and p in (0, 1, 2, 4):
                dve_f(dve, *at(b, c, 3), (0, 1, 2, 4).index(p))
            if p == 1 and exists(c, 1, last):
                dve_ml(dve, *at(b, c, 1))
            if c == 0 and not last:
                if p == 3:
                    dve_l(dve, b + 1)
                if p == 8:
                    dve_v(dve, b + 1, 1 - odd)
            if c == 1 and not first and p in (3, 5, 6, 7):
                dve_ut(dve, b - 1, (3, 5, 6, 7).index(p))
            if c == 2 and not first:
                if p == 3:
                    dve_x1(dve, b - 1)
                if p == 9:
                    dve_xh(dve, b - 1)
            if c == 3 and not first and p == 0:
                dve_lg(dve, b - 1)
            if c == 3 and not first and p == 3:
                dve_router(dve, b - 1)

    def dve_open(dve):
        dve.memset(zero2[:].bitcast(F32), 0.0)
        for i in range(2):
            dve.memset(vx[i][:], 1.0)
        for c in range(NCH):
            dve.memset(qs[c][ROW_MAX:P, :].bitcast(F32), 0.0)
            dve.memset(ks[c][ROW_MAX:P, :].bitcast(F32), 0.0)
        dve.memset(u_bank[:], 0.0)
        dve.memset(ml[:].bitcast(F32), 0.0).then_inc(const_ready, 1)
        wait(dve, const_ready, 1)
        for c in range(NCH):
            ins = dve.memset(ks[c][ROW_MAX:ROW_MAX + 2, :].bitcast(F32), 1.0)
        ins.then_inc(const_ready, 1)
        dve_l(dve, 0)
        dve_v(dve, 0, 0)
        for c in range(3):
            for part in range(4):
                dve_f(dve, 0, c, part)
            if c >= 1:
                for p in range(PIECES):
                    dve_max(dve, 0, c - 1, p)
            if c == 1:
                dve_ml(dve, 0, 0)

    def dve_close(dve, b):
        for t in range(TT):
            dve_ut(dve, b, t)
        dve_x1(dve, b)
        dve_xh(dve, b)
        dve_lg(dve, b)
        dve_router(dve, b)

    def pool_k(pool, b, c):
        n = NCH * b + c
        wait(pool, f_used, 4 * n + 3)
        wait(pool, kl_ready, n)
        pool.tensor_tensor(k_sum[:], k_cos[:], k_sin[:], ALU.add).then_inc(ksum_ready, 1)
        wait(pool, kh_ready, n + 1)
        pool.tensor_tensor(kl[:], k_sum[:], kh[:].bitcast(F32), ALU.subtract).then_inc(kl_ready, 1)

    def pool_h(pool, b):
        wait(pool, hf_ready, b + 1)
        pool.tensor_tensor(hl[:], hf[:], hh[:].bitcast(F32), ALU.subtract).then_inc(h_ready, 1)

    def pool_xb(pool, b):
        wait(pool, t_loaded, 32 * (b + 1))
        wait(pool, proj_ready, b)
        wait(pool, x1_ready, b)
        pool.tensor_tensor(wc_g[:], v["param"]("cproj_t"), mod_b[:, 0, :], ALU.mult)
        pool.tensor_tensor(bias_cg[:], v["bias_c"][:], mod_b[:, 0, :], ALU.mult).then_inc(bcg_ready, 1)
        wait(pool, bcg_ready, b + 1)
        pool.tensor_tensor(xb[:], x_res[:], bias_cg[:].unsqueeze(1).broadcast_to((P, TT, C)), ALU.add).then_inc(xb_ready, 1)

    def pool_h2(pool, b):
        wait(pool, xn2_ready, b + 1)
        wait(pool, ht_ready, b)
        wait(pool, xh_ready, b)
        pool.tensor_tensor(h2[:], xn2[:], mod_b[:, 2, :].unsqueeze(1).broadcast_to((P, TT, C)), ALU.mult).then_inc(h2m_ready, 1)
        wait(pool, h2m_ready, b + 1)
        pool.tensor_tensor(h2[:], h2[:], mod_b[:, 1, :].unsqueeze(1).broadcast_to((P, TT, C)), ALU.add).then_inc(h2_ready, 1)
        wait(pool, h2_ready, b + 1)
        pool.tensor_tensor(xn2[:], h2[:], mod_b[:, 3, :].unsqueeze(1).broadcast_to((P, TT, C)), ALU.mult).then_inc(gh_ready, 1)

    def pool_slot(pool, b, c, odd, first, last):
        if c == 1 and not first:
            pool_xb(pool, b - 1)
        if exists(c, 3, last):
            pool_k(pool, *at(b, c, 3))
        if c == 0 and not last:
            pool_h(pool, b + 1)
        if c == 2 and not first:
            pool_h2(pool, b - 1)

    def pool_open(pool):
        pool_h(pool, 0)
        for c in range(3):
            pool_k(pool, 0, c)

    def pool_close(pool, b):
        pool_xb(pool, b)
        pool_h2(pool, b)

    def sp_wait(sp, semaphore, n):
        if isinstance(n, int) and n <= 0:
            return
        sp.wait_ge(semaphore, n)
        sp.sem_inc(held, 1)

    def tokens(ap, b, width):
        t = ap.rearrange("(b t p) c -> b p t c", p=P, t=TT)
        return t[b] if isinstance(b, int) else t[bass.ds(b, 1)].rearrange("a p t c -> (a p) t c")

    x_rows = v["x"].rearrange("b t c -> (b t) c")

    def sp_x(sp, b):
        sp_wait(sp, xn_ready, b)
        sp.dma_start(x_in[:], tokens(x_rows, b, C)).then_inc(x_loaded, 16)

    def sp_t(sp, b):
        sp_wait(sp, xb_ready, b)
        sp_wait(sp, gh_ready, b)
        sp.dma_start(x_res[:], tokens(x_rows, b, C)).then_inc(t_loaded, 16)
        m = v["d_mod"]
        row = m[b:b + 1, :] if isinstance(b, int) else m[bass.ds(b, 1), :]
        sp.dma_start(mod_b[:].rearrange("p m c -> p (m c)"), row.broadcast_to((P, 4 * C))).then_inc(t_loaded, 16)

    def sp_stack(sp, b, c):
        n = NCH * b + c
        if isinstance(b, int) and b == 0:
            sp_wait(sp, const_ready, 2)
        sp_wait(sp, st_ready, PIECES * (n - NCH + 1))
        sp_wait(sp, kh_ready, n + 1)
        sp_wait(sp, kl_ready, n + 1)
        sp_wait(sp, qh_ready, n + 1)
        sp_wait(sp, f_used, 4 * n + 4)
        for r, src in ((0, kh), (L, kl), (2 * L, kh)):
            sp.dma_start(ks[c][r:r + L, :].bitcast(F32), src[:].bitcast(F32)).then_inc(stack_ready[c], 16)
        for r, src in ((0, qh), (L, qh), (2 * L, ql)):
            sp.dma_start(qs[c][r:r + L, :].bitcast(F32), src[:].bitcast(F32)).then_inc(stack_ready[c], 16)
        sp.dma_start(qs[c][ROW_MAX:ROW_MAX + 2, :].bitcast(F32), zero2[:].bitcast(F32)).then_inc(stack_ready[c], 16)

    def sp_rows(sp, b, c):
        n = NCH * b + c
        sp_wait(sp, mt_used, n + 1)
        sp_wait(sp, mh_ready, n + 1)
        for r, src in ((ROW_MAX, mh), (ROW_MAX + 1, ml)):
            sp.dma_start(qs[c][r:r + 1, :].bitcast(F32), src[:].bitcast(F32)).then_inc(rows_ready[c], 16)

    def sp_out(sp, b):
        sp_wait(sp, xh_ready, b + 1)
        sp_wait(sp, gate_ready, b + 1)
        sp_wait(sp, base_ready, b + 1)
        sp.dma_start(tokens(v["d_xh"], b, C), xh[:]).then_inc(outs_stored, 16)
        sp.dma_start(tokens(v["d_gate"], b, E), gate[:]).then_inc(outs_stored, 16)
        sp.dma_start(tokens(v["d_base"], b, C), base[:]).then_inc(outs_stored, 16)

    def sp_slot(sp, b, c, odd, first, last):
        if c == 0 and not last:
            sp_x(sp, b + 1)
        if exists(c, 1, last):
            sp_rows(sp, *at(b, c, 1))
        if exists(c, 3, last):
            sp_stack(sp, *at(b, c, 3))
        if c == 0 and not first:
            sp_t(sp, b - 1)
        if c == 3 and not first:
            sp_out(sp, b - 1)

    def sp_open(sp):
        sp_x(sp, 0)
        sp_stack(sp, 0, 0)
        sp_stack(sp, 0, 1)
        sp_rows(sp, 0, 0)
        sp_stack(sp, 0, 2)

    def sp_close(sp, b):
        sp_t(sp, b)
        sp_out(sp, b)
        sp.wait_ge(outs_stored, 48 * B)

    def run(eng, opening, slot, closing):
        side_last[0] = None
        opening(eng)
        for b in (0, 1):
            for c in range(NCH):
                slot(eng, b, c, b, b == 0, False)
        with eng.Fori(2, B - 3, 2) as i:
            for odd in (0, 1):
                for c in range(NCH):
                    slot(eng, i + 1 if odd else i, c, odd, False, False)
        for b in (B - 2, B - 1):
            for c in range(NCH):
                slot(eng, b, c, b % 2, False, b == B - 1)
        closing(eng, B - 1)

    with nc.Block() as block:
        @block.sync
        def _(sp):
            run(sp, sp_open, sp_slot, sp_close)

        @block.gpsimd
        def _(pool):
            run(pool, pool_open, pool_slot, pool_close)

        @block.scalar
        def _(act):
            run(act, act_open, act_slot, act_close)

        @block.vector
        def _(dve):
            run(dve, dve_open, dve_slot, dve_close)

        @block.tensor
        def _(pe):
            run(pe, pe_open, pe_slot, pe_close)


def feed_forward(nc, ctx, sb, sem, bank, v):
    NF = FF // P
    ident = v["ident"]
    w1 = sb(ctx, "w1", [P, E, FF])
    w2 = sb(ctx, "w2", [P, E, NF, C])
    g, bl, b1c = v["param"]("ln_g_t"), v["param"]("ln_b_t"), v["param"]("b1_t")
    b1f = sb(ctx, "b1f", [P, E, NF])
    b2r = sb(ctx, "b2r", [1, E, C])
    ones = sb(ctx, "ones", [1, P])
    xh = sb(ctx, "f_xh", [P, TT, C])
    xt = sb(ctx, "f_xt", [P, T])
    gate = sb(ctx, "f_gate", [P, TT, E])
    base = sb(ctx, "f_base", [P, TT, C])
    gb = sb(ctx, "f_gb", [P, C])
    a = [sb(ctx, f"f_a{i}", [P, NF, T]) for i in range(2)]
    acc = sb(ctx, "f_acc", [P, TT, C])
    o = sb(ctx, "f_o", [P, TT, C])

    w_loaded, folded, w_ready = sem("w_loaded"), sem("fw_folded"), sem("fw_ready")
    in_loaded, xt_ready, xt_copied = sem("in_loaded"), sem("fxt_ready"), sem("fxt_copied")
    h_ready, a_ready = sem("fh_ready"), sem("fa_ready")
    y_ready, y_used = sem("fy_ready"), sem("fy_used")
    acc_free, o_free = sem("acc_free"), sem("o_free")
    gacc_ready, o_ready, o_stored = sem("gacc_ready"), sem("fo_ready"), sem("o_stored")
    held = sem("f_held")
    h_bank, y_bank, x_bank = bank[0:4], bank[4:6], bank[6]

    def rows_of(ap, b):
        return ap.rearrange("(b t p) c -> b p t c", p=P, t=TT)[bass.ds(b, 1)].rearrange("a p t c -> (a p) t c")

    with nc.Block() as block:
        @block.sync
        def _(sp):
            sp.dma_start(w1[:], v["w1"].rearrange("e p f -> p e f")).then_inc(w_loaded, 16)
            for e in range(E):
                sp.dma_start(w2[:, e], v["w2"][e].rearrange("(f p) c -> p f c", p=P)).then_inc(w_loaded, 16)
            sp.dma_start(b2r[:], v["b2"].rearrange("(a e) c -> a e c", a=1)).then_inc(w_loaded, 16)
            with sp.Fori(0, B) as i:
                sp.wait_ge(acc_free, i + 1)
                sp.sem_inc(held, 1)
                sp.dma_start(xh[:], rows_of(v["d_xh"], i)).then_inc(in_loaded, 16)
                sp.dma_start(gate[:], rows_of(v["d_gate"], i)).then_inc(in_loaded, 16)
                sp.dma_start(base[:], rows_of(v["d_base"], i)).then_inc(in_loaded, 16)
                sp.dma_start(gb[:], v["d_mod"][bass.ds(i, 1), 3 * C:4 * C].broadcast_to((P, C))).then_inc(in_loaded, 16)
                sp.wait_ge(o_ready, i + 1)
                sp.sem_inc(held, 1)
                sp.dma_start(rows_of(v["out"].rearrange("b t c -> (b t) c"), i), o[:]).then_inc(o_stored, 16)
            sp.wait_ge(o_stored, 16 * B)

        @block.scalar
        def _(act):
            with act.Fori(0, B) as i:
                act.wait_ge(xt_ready, i + 1)
                act.activation(xt[:], x_bank[:], ACT.Copy).then_inc(xt_copied, 1)
                for e in range(E):
                    for f in range(NF):
                        act.wait_ge(h_ready, i * (E * NF) + (e * NF + f + 1))
                        act.activation(a[e % 2][:, f], h_bank[f][:], ACT.Gelu, bias=b1f[:, e, f:f + 1]).then_inc(a_ready, 1)

        @block.vector
        def _(dve):
            dve.memset(ones[:], 1.0)
            dve.wait_ge(w_loaded, 16 * (E + 2))
            dve.wait_ge(folded, 1)
            dve.tensor_tensor(b1f[:].rearrange("p e f -> p (e f)"), bank[7][:, 0:E * NF],
                              b1c, ALU.add)
            for e in range(E):
                ins = dve.tensor_scalar(w1[:, e], w1[:, e], g[:, e:e + 1], None, ALU.mult)
            ins.then_inc(w_ready, 1)
            dve.wait_ge(w_ready, 1)
            dve.sem_inc(acc_free, 1)
            with dve.Fori(0, B) as i:
                for e in range(E):
                    dve.wait_ge(y_ready, i * E + (e + 1))
                    for t in range(TT):
                        src = y_bank[e % 2][:, P * t:P * t + P]
                        if e == 0:
                            ins = dve.tensor_scalar(acc[:, t], src, gate[:, t, e:e + 1], None, ALU.mult)
                        else:
                            ins = dve.scalar_tensor_tensor(acc[:, t], src, gate[:, t, e:e + 1], acc[:, t], ALU.mult, ALU.add)
                    ins.then_inc(y_used, 1)
                    dve.wait_ge(y_used, i * E + (e + 1))
                dve.tensor_tensor(acc[:], acc[:], gb[:].unsqueeze(1).broadcast_to((P, TT, C)), ALU.mult).then_inc(gacc_ready, 1)
                dve.wait_ge(gacc_ready, i + 1)
                dve.wait_ge(o_free, i + 1)
                dve.tensor_tensor(o[:], acc[:], base[:], ALU.add).then_inc(o_ready, 1)
                dve.wait_ge(o_ready, i + 1)
                dve.sem_inc(acc_free, 1)

        @block.gpsimd
        def _(pool):
            pool.sem_inc(o_free, 1)
            with pool.Fori(0, B) as i:
                pool.wait_ge(o_stored, i * 16 + 16)
                pool.sem_inc(o_free, 1)

        @block.tensor
        def _(pe):
            pe.wait_ge(w_loaded, 16 * (E + 2))
            for e in range(E):
                for f in range(NF):
                    ins = pe.matmul(bank[7][:, e * NF + f:e * NF + f + 1], w1[:, e, P * f:P * f + P], bl[:, e:e + 1],
                                    start=True, stop=True)
            ins.then_inc(folded, 1)
            pe.wait_ge(w_ready, 1)
            with pe.Fori(0, B) as i:
                pe.wait_ge(in_loaded, i * 64 + 64)
                for t in range(TT):
                    ins = pe.transpose(x_bank[:, P * t:P * t + P], xh[:, t, :], ident[:])
                ins.then_inc(xt_ready, 1)
                pe.wait_ge(xt_copied, i + 1)

                def up(e):
                    for f in range(NF):
                        if e:
                            pe.wait_ge(a_ready, i * (E * NF) + ((e - 1) * NF + f + 1))
                        pe.matmul(h_bank[f][:], w1[:, e, P * f:P * f + P], xt[:], start=True, stop=True).then_inc(h_ready, 1)

                def down(e):
                    pe.wait_ge(a_ready, i * (E * NF) + (e + 1) * NF)
                    if e >= 2:
                        pe.wait_ge(y_used, i * E + (e - 1))
                    for t in range(TT):
                        out = y_bank[e % 2][:, P * t:P * t + P]
                        pe.matmul(out, ones[:], b2r[:, e, :], start=True, stop=False, skip_group_check=True)
                        for f in range(NF):
                            ins = pe.matmul(out, a[e % 2][:, f, P * t:P * t + P], w2[:, e, f, :],
                                            start=False, stop=(f == NF - 1), skip_group_check=True)
                    ins.then_inc(y_ready, 1)

                up(0)
                for e in range(1, E):
                    up(e)
                    down(e - 1)
                down(E - 1)
                pe.wait_ge(y_used, i * E + E)


_INS = ['attn_x', 'attn_c_attn_w', 'attn_c_attn_b', 'attn_q2l_w', 'attn_q2l_b', 'attn_kv2l_w', 'attn_kv2l_b',
        'attn_l2o_w', 'attn_l2o_b', 'attn_wqk_w', 'attn_wqk_b', 'attn_cproj_w', 'attn_cproj_b',
        'ffn_router_W', 'ffn_router_b', 'ffn_ln_g', 'ffn_ln_b', 'ffn_W1', 'ffn_b1', 'ffn_W2', 'ffn_b2', 'c', 'wmod']
_OUTS = [((16, 512, 128), 'float32')]


def _constants():
    import numpy as np
    latent, heads = np.arange(P) // HG, np.arange(P) % HG
    inv = (np.float32(1.0) / np.float32(10000.0) ** (np.arange(0, L, 2, dtype=np.float32) / np.float32(L))).astype(np.float32)
    angle = np.outer(np.arange(T, dtype=np.float32), inv).astype(np.float32)
    cos = np.cos(angle).astype(np.float32).T[latent // 2]
    sin = np.sin(angle).astype(np.float32).T[latent // 2]
    rot = np.zeros((P, P), np.float32)
    for r in range(P):
        other = r + HG if latent[r] % 2 == 0 else r - HG
        rot[r, other] = -1.0 if latent[r] % 2 == 0 else 1.0
    mats = np.concatenate([np.eye(P, dtype=np.float32), rot], 1)
    q, k = np.meshgrid(np.arange(P), np.arange(P), indexing="ij")
    hide = np.where(k > q, np.float32(-1e30), np.float32(0))
    sel = np.concatenate([(np.arange(P)[:, None] // HD == np.arange(H)), (heads[:, None] == np.arange(HG)),
                          np.broadcast_to(np.arange(E), (P, E))], 1)
    masks = np.concatenate([hide, hide.T, sel], 1).astype(np.float32)
    return {"c_cos": np.ascontiguousarray(cos), "c_sin": np.ascontiguousarray(sin), "c_mats": mats, "c_masks": masks}


def _small(w):
    import numpy as np
    latent_col = lambda b: np.repeat(b, HG)[:, None]
    parts = {"b_attn": w["attn_c_attn_b"].reshape(3, C).T, "q2l_b": latent_col(w["attn_q2l_b"]),
             "kv2l_b": latent_col(w["attn_kv2l_b"]), "wqk_b": latent_col(w["attn_wqk_b"]),
             "q2l_t": np.tile(w["attn_q2l_w"].T, (H, 1)), "kv2l_t": np.tile(w["attn_kv2l_w"].T, (H, 1)),
             "wqk_t": np.repeat(w["attn_wqk_w"].T, HG, axis=0), "cproj_t": w["attn_cproj_w"].T,
             "ln_g_t": w["ffn_ln_g"].T, "ln_b_t": w["ffn_ln_b"].T,
             "b1_t": w["ffn_b1"].reshape(E * FF // P, P).T, "cond_t": w["c"].T}
    return np.ascontiguousarray(np.concatenate([parts[name] for name, _ in SMALL], 1))


def kernel(**inputs):
    import numpy as _np
    import concourse.bacc as _bacc
    from concourse import mybir as _mybir
    from concourse.bass_utils import run_bass_kernel_spmd as _run

    nc = _bacc.Bacc("TRN2", target_bir_lowering=False, num_devices=1)
    w = {name: _np.ascontiguousarray(inputs["L0_" + name]) for name in _INS}
    arrays = {"x": w["attn_x"], "w_attn": w["attn_c_attn_w"], "kv2l_h": _np.tile(w["attn_kv2l_w"], (1, H)),
              "kvb_col": w["attn_kv2l_b"][:, None], "l2o_t": _np.ascontiguousarray(w["attn_l2o_w"].T),
              "l2o_b": w["attn_l2o_b"][None], "cproj_b": w["attn_cproj_b"][None], "router_w": w["ffn_router_W"],
              "router_b": w["ffn_router_b"][None], "w1": w["ffn_W1"], "w2": w["ffn_W2"], "b2": w["ffn_b2"],
              "wmod": w["wmod"], "small": _small(w), **_constants()}
    arrays = {"in_" + name: _np.ascontiguousarray(a) for name, a in arrays.items()}
    args = [nc.dram_tensor(name, a.shape, _mybir.dt.from_np(a.dtype), kind="ExternalInput").ap()
            for name, a in arrays.items()]
    for i, (shape, dtype) in enumerate(_OUTS):
        dt = _mybir.dt.from_np(_np.dtype(dtype))
        args.append(nc.dram_tensor(f"out_{i}", shape, dt, kind="ExternalOutput").ap())
    adaln_block(nc, *args)
    r = _run(nc, [arrays], core_ids=[0])
    return r.results[0]["out_0"]
```

```python
import concourse.bass as bass
from concourse import mybir
from contextlib import ExitStack

F32 = mybir.dt.float32
F32R = mybir.dt.float32r
BF16 = mybir.dt.bfloat16
U32 = mybir.dt.uint32
I32 = mybir.dt.int32
ALU = mybir.AluOpType
ACT = mybir.ActivationFunctionType
AX = mybir.AxisListType

B, T, C = 16, 512, 128
H, HD, L = 16, 8, 32
E, FF = 8, 512
P = 128
HG = P // L
NCH = H // HG
TT = T // P
VW = HD + 1
SCALE = float(L) ** -0.5
LN_EPS = 1e-5
RSQRT_MAGIC = 0x5F3759DF
MOD_SA, MOD_CA, MOD_GA, MOD_SB, MOD_CB, MOD_GB = range(6)

ROW_MAX = 3 * L

P_OFF = [0, 512, 1024, 896]
P_COLS = 1280
PIECES = 10
ST_BANK = [0, 1, 2, 0, 1, 2, 0, 1, 2, 1]
ST_BACK = [4, 2, 4, 3, 3, 3, 3, 3, 3, 2]
LN_STEPS = 14

N_TOK = B * T
TOP = 2
ROW = C + 2
REGION = N_TOK + P
TILES = TOP * N_TOK // P + E
RING = 8


def wait(eng, sem, n):
    if isinstance(n, int) and n <= 0:
        return
    eng.wait_ge(sem, n)


def piece(p):
    pair, q = divmod(p, 5)
    h = 2 * pair
    return [(0, [h]), (0, [h + 1]), (1, [h]), (1, [h + 1]), (2, [h, h + 1])][q]


SMALL = [("b_attn", 3), ("q2l_b", 1), ("kv2l_b", 1), ("wqk_b", 1), ("q2l_t", L), ("kv2l_t", L), ("wqk_t", L),
         ("cproj_t", C), ("ln_g_t", E), ("ln_b_t", E), ("b1_t", E * FF // P), ("cond_t", B)]
ROUTE_TOKEN = P
ROUTE_FILL = ROUTE_TOKEN + TOP * TT
ROUTE_TILE = ROUTE_FILL + 2 * E
ROUTE_COLS = ROUTE_TILE + TILES
SMALL_AT = {name: (sum(w for _, w in SMALL[:n]), width) for n, (name, width) in enumerate(SMALL)}


def adaln_block(nc, x, w_attn, kv2l_h_d, kvb_col, l2o_t, l2o_b, cproj_b, router_w, router_b, w1, w2, b2, wmod,
                small, c_cos, c_sin, c_mats, c_masks, c_route, out):
    top = ExitStack()
    with top:
        def sb(ctx, name, shape, dt=F32):
            return ctx.enter_context(nc.sbuf_tensor(name, shape, dt))

        def sem(name):
            return top.enter_context(nc.semaphore(name))

        bank = [top.enter_context(nc.psum_tensor(f"bank{i}", [P, 512], F32)) for i in range(8)]

        d_mod = nc.dram_tensor("d_mod", [B, 4 * C], F32, kind="Internal").ap()
        d_base = nc.dram_tensor("d_base", [B * T, C], F32, kind="Internal").ap()
        d_queue = nc.dram_tensor("d_queue", [E * REGION + E * P, ROW], F32, kind="Internal").ap()
        d_y = nc.dram_tensor("d_y", [TOP * N_TOK + 2 * E * P, C], F32, kind="Internal").ap()

        par = sb(top, "par", [P, sum(w for _, w in SMALL)])

        def param(name):
            at, width = SMALL_AT[name]
            return par[:, at:at + width]

        route = sb(top, "route", [P, ROUTE_COLS])
        end_row = sb(top, "end_row", [P, E])
        iota_e = sb(top, "iota_e", [P, E])
        tile_no, fill_target = route[:, ROUTE_TILE:ROUTE_COLS], route[:, ROUTE_FILL:ROUTE_TILE]

        attn = ExitStack()
        ident = sb(top, "ident", [P, P])
        cos_t = sb(attn, "cos_t", [P, T])
        sin_t = sb(attn, "sin_t", [P, T])
        ident_bf = sb(attn, "ident_bf", [P, P], BF16)
        mask_q = sb(attn, "mask_q", [P, P], BF16)
        mask_k = sb(attn, "mask_k", [P, P], BF16)
        before = sb(attn, "before", [P, P], BF16)
        ones_bf = sb(attn, "ones_bf", [P, P], BF16)
        token = sb(attn, "token", [P, TOP, TT])
        wq = [sb(attn, f"wq{i}", [P, H * L], F32R) for i in range(2)]
        wk = [sb(attn, f"wk{i}", [P, H * L], F32R) for i in range(2)]
        wkr = [sb(attn, f"wkr{i}", [P, H * L], F32R) for i in range(2)]
        wv = [sb(attn, f"wv{i}", [P, C], F32R) for i in range(2)]
        wqk_c = sb(attn, "wqk_c", [P, P])
        wqk_s = sb(attn, "wqk_s", [P, P])
        bias_q = sb(attn, "bias_q", [P, NCH])
        bias_k = sb(attn, "bias_k", [P, NCH])
        bias_kr = sb(attn, "bias_kr", [P, NCH])
        bias_v = sb(attn, "bias_v", [P, C])
        bias_c = sb(attn, "bias_c", [P, C])
        wr = sb(attn, "wr", [P, E])
        bias_r = sb(attn, "bias_r", [P, E])
        mod_s = sb(attn, "mod_s", [P, B])
        mod_c = sb(attn, "mod_c", [P, B])

        setup = ExitStack()
        with attn:
            with setup:
                prepare(nc, setup, sb, sem, bank, locals())
            attention(nc, attn, sb, sem, bank, locals())
        with ExitStack() as experts:
            feed_forward(nc, experts, sb, sem, bank, locals())
        with ExitStack() as sums:
            combine(nc, sums, sb, sem, locals())


def prepare(nc, ctx, sb, sem, bank, v):
    mats = sb(ctx, "mats", [P, 2 * P])
    rot = mats[:, P:2 * P]
    masks = sb(ctx, "masks", [P, 2 * P])
    sel = sb(ctx, "sel", [P, H + HG + E])
    wa = sb(ctx, "wa", [P, 3, C])
    par, param = v["par"], v["param"]
    ba = param("b_attn")
    q2l_r, kv2l_r = param("q2l_t"), param("kv2l_t")
    kv2l_h = sb(ctx, "kv2l_h", [L, H, HD])
    l2o_t = sb(ctx, "l2o_t", [L, HD])
    l2o_br = sb(ctx, "l2o_br", [P, HD])
    kvb = sb(ctx, "kvb", [L, 1])
    qbc, kbc, wqk_rep = param("q2l_b"), param("kv2l_b"), param("wqk_t")
    wqk_bd = sb(ctx, "wqk_bd", [P, L, HG])
    eq = sb(ctx, "eq", [P, NCH, L, HG])
    ek = sb(ctx, "ek", [P, NCH, L, HG])
    er = sb(ctx, "er", [P, NCH, L, HG])
    g_bd = sb(ctx, "g_bd", [P, H, HD])
    g_small = sb(ctx, "g_small", [P, HD])
    bv_rep = sb(ctx, "bv_rep", [P, P])
    kvb_rep = sb(ctx, "kvb_rep", [L, P])
    l2o_rep = sb(ctx, "l2o_rep", [L, H, HD])
    cin = param("cond_t")
    ce, cs, cst = sb(ctx, "ce", [P, B]), sb(ctx, "cs", [P, B]), sb(ctx, "cst", [P, B])
    wm = sb(ctx, "wm", [P, 6, C])
    rows = sb(ctx, "rows", [B, 4, C])
    absr = sb(ctx, "absr", [B, 2, C])
    sgn = sb(ctx, "sgn", [B, 2, C])
    full = sb(ctx, "full", [P, H * L])

    loaded = sem("setup_loaded")
    step = sem("setup_step")
    spread_ready, folded, folded_bias = sem("spread_ready"), sem("folded"), sem("folded_bias")
    bias_ready, wqk_ready, rotated = sem("bias_ready"), sem("wqk_ready"), sem("rotated")
    value_folded, g_ready = sem("value_folded"), sem("g_ready")
    exp_ready, silu_ready = sem("exp_ready"), sem("silu_ready")
    modulated, rows_ready, stored = sem("modulated"), sem("rows_ready"), sem("mod_rows_stored")
    n_loads = 0

    with nc.Block() as block:
        @block.sync
        def _(sp):
            nonlocal n_loads

            def load(dst, src):
                nonlocal n_loads
                sp.dma_start(dst, src).then_inc(loaded, 16)
                n_loads += 1

            load(mats[:], v["c_mats"])
            load(masks[:], v["c_masks"][:, 0:2 * P])
            load(sel[:], v["c_masks"][:, 2 * P:2 * P + H + HG + E])
            load(v["cos_t"][:], v["c_cos"])
            load(v["sin_t"][:], v["c_sin"])
            load(par[:], v["small"])
            load(v["route"][:], v["c_route"])
            load(wa[:], v["w_attn"].rearrange("(a p) c -> p a c", p=P))
            load(kv2l_h[:].rearrange("l h d -> l (h d)"), v["kv2l_h_d"])
            load(l2o_t[:], v["l2o_t"])
            load(l2o_br[:], v["l2o_b"].broadcast_to((P, HD)))
            load(kvb[:], v["kvb_col"])
            load(v["bias_c"][:], v["cproj_b"].broadcast_to((P, C)))
            load(v["wr"][:], v["router_w"])
            load(v["bias_r"][:], v["router_b"].broadcast_to((P, E)))
            load(wm[:], v["wmod"].rearrange("p (m c) -> p m c", c=C))
            sp.wait_ge(rows_ready, 1)
            sp.dma_start(v["d_mod"], rows[:].rearrange("b m c -> b (m c)")).then_inc(stored, 16)
            sp.wait_ge(stored, 16)

        head_of_row = sel[:, 0:H]
        head_in_chunk = sel[:, H:H + HG]
        flat = lambda ap: ap.rearrange("p c l h -> p (c l h)")

        @block.tensor
        def _(pe):
            pe.wait_ge(loaded, 16 * n_loads)
            for n, (rows_of, spread_w) in enumerate(((0, eq), (1, ek), (1, er))):
                pe.wait_ge(spread_ready, n + 1)
                pe.matmul(bank[n][:], wa[:, rows_of, :], flat(spread_w[:]), start=True, stop=True).then_inc(folded, 1)
            for n, spread_w in ((0, eq), (1, ek)):
                for c in range(NCH):
                    last = pe.matmul(bank[3][:, NCH * n + c:NCH * n + c + 1], spread_w[:, c].rearrange("p l h -> p (l h)"),
                                     ba[:, n:n + 1], start=True, stop=True)
            last.then_inc(folded_bias, 1)
            pe.wait_ge(bias_ready, 1)
            pe.matmul(bank[4][:, 0:NCH], rot, v["bias_k"][:], start=True, stop=True).then_inc(rotated, 1)
            pe.wait_ge(wqk_ready, 1)
            pe.matmul(bank[5][:, 0:P], rot, v["wqk_c"][:], start=True, stop=True).then_inc(rotated, 1)
            pe.matmul(bank[6][:, 0:HD], kv2l_h[:].rearrange("l h d -> l (h d)"), l2o_t[:],
                      start=True, stop=True).then_inc(value_folded, 1)
            pe.wait_ge(g_ready, 1)
            pe.matmul(bank[6][:, 0:C], wa[:, 2, :], g_bd[:].rearrange("p h d -> p (h d)"), start=True, stop=True)
            pe.matmul(bank[7][:, 0:C], bv_rep[:], g_bd[:].rearrange("p h d -> p (h d)"), start=True, stop=False)
            pe.matmul(bank[7][:, 0:C], kvb_rep[:], l2o_rep[:].rearrange("l h d -> l (h d)"),
                      start=False, stop=True).then_inc(value_folded, 1)
            pe.wait_ge(silu_ready, 1)
            pe.matmul(bank[0][:, 0:B], wm[:, MOD_SA, :], cst[:], start=True, stop=True)
            pe.matmul(bank[1][:, 0:B], wm[:, MOD_CA, :], cst[:], start=True, stop=True)
            pe.matmul(bank[2][0:B, :], cst[:], wm[:, MOD_GA:, :].rearrange("p m c -> p (m c)"),
                      start=True, stop=True).then_inc(modulated, 1)

        @block.scalar
        def _(act):
            act.wait_ge(loaded, 16 * n_loads)
            act.activation(ce[:], cin, ACT.Exp, scale=-1.0).then_inc(exp_ready, 1)

        @block.vector
        def _(dve):
            steps = 0

            def link(ins):
                nonlocal steps
                steps += 1
                ins.then_inc(step, 1)
                dve.wait_ge(step, steps)

            dve.wait_ge(loaded, 16 * n_loads)
            dve.tensor_copy(v["ident"][:], mats[:, 0:P])
            dve.tensor_copy(v["ident_bf"][:], mats[:, 0:P])
            dve.tensor_copy(v["mask_q"][:], masks[:, 0:P])
            dve.tensor_copy(v["mask_k"][:], masks[:, P:2 * P])
            dve.tensor_copy(v["iota_e"][:], sel[:, H + HG:H + HG + E])
            dve.tensor_copy(v["before"][:], v["route"][:, 0:P])
            dve.memset(v["ones_bf"][:], 1.0)
            dve.tensor_copy(v["token"][:].rearrange("p k t -> p (k t)"), v["route"][:, ROUTE_TOKEN:ROUTE_FILL])
            dve.tensor_scalar(v["end_row"][:], sel[:, H + HG:H + HG + E], float(REGION), None, ALU.mult)
            for dst, src in ((eq, q2l_r), (ek, kv2l_r)):
                for c in range(NCH):
                    ins = dve.tensor_tensor(
                        dst[:, c], src.unsqueeze(2).broadcast_to((P, L, HG)),
                        head_of_row[:, HG * c:HG * c + HG].unsqueeze(1).broadcast_to((P, L, HG)), ALU.mult)
                link(ins)
                dve.sem_inc(spread_ready, 1)
            for c in range(NCH):
                dve.tensor_scalar(er[:, c, 0:L:2, :], ek[:, c, 1:L:2, :], -1.0, None, ALU.mult)
                ins = dve.tensor_copy(er[:, c, 1:L:2, :], ek[:, c, 0:L:2, :])
            ins.then_inc(spread_ready, 1)
            link(dve.tensor_tensor(wqk_bd[:], wqk_rep.unsqueeze(2).broadcast_to((P, L, HG)),
                                   head_in_chunk.unsqueeze(1).broadcast_to((P, L, HG)), ALU.mult))
            dve.tensor_copy(v["wqk_c"][:], wqk_bd[:].rearrange("p l h -> p (l h)")).then_inc(wqk_ready, 1)
            dve.tensor_copy(bv_rep[:], ba[:, 2:3].broadcast_to((P, P)))
            dve.tensor_copy(kvb_rep[:], kvb[:].broadcast_to((L, P)))
            dve.tensor_copy(l2o_rep[:], l2o_t[:].unsqueeze(1).broadcast_to((L, H, HD)))
            for n, dst in enumerate((v["wq"], v["wk"], v["wkr"])):
                dve.wait_ge(folded, n + 1)
                link(dve.tensor_copy(full[:], bank[n][:]))
                link(dve.tensor_copy(dst[0][:], full[:]))
                link(dve.tensor_tensor(dst[1][:], full[:], dst[0][:].bitcast(F32), ALU.subtract))
            dve.wait_ge(folded_bias, 1)
            dve.tensor_scalar(v["bias_q"][:], bank[3][:, 0:NCH], qbc, None, ALU.add)
            dve.tensor_scalar(v["bias_k"][:], bank[3][:, NCH:2 * NCH], kbc, None, ALU.add).then_inc(bias_ready, 1)
            dve.wait_ge(rotated, 2)
            dve.tensor_scalar(v["bias_kr"][:], bank[4][:, 0:NCH], -1.0, None, ALU.mult)
            dve.tensor_copy(v["wqk_s"][:], bank[5][:, 0:P])
            dve.wait_ge(value_folded, 1)
            link(dve.tensor_copy(g_small[:], bank[6][:, 0:HD]))
            dve.tensor_tensor(g_bd[:], g_small[:].unsqueeze(1).broadcast_to((P, H, HD)),
                              head_of_row.unsqueeze(2).broadcast_to((P, H, HD)), ALU.mult).then_inc(g_ready, 1)
            dve.wait_ge(value_folded, 2)
            link(dve.tensor_copy(full[:, 0:C], bank[6][:, 0:C]))
            link(dve.tensor_copy(v["wv"][0][:], full[:, 0:C]))
            dve.tensor_tensor(v["wv"][1][:], full[:, 0:C], v["wv"][0][:].bitcast(F32), ALU.subtract)
            dve.tensor_tensor(v["bias_v"][:].rearrange("p (h d) -> p h d", d=HD),
                              bank[7][:, 0:C].rearrange("p (h d) -> p h d", d=HD),
                              l2o_br[:].unsqueeze(1).broadcast_to((P, H, HD)), ALU.add)
            dve.wait_ge(exp_ready, 1)
            link(dve.tensor_scalar(ce[:], ce[:], 1.0, None, ALU.add))
            link(dve.reciprocal(cs[:], ce[:]))
            dve.tensor_tensor(cst[:], cs[:], cin, ALU.mult).then_inc(silu_ready, 1)
            dve.wait_ge(modulated, 1)
            dve.tensor_copy(v["mod_s"][:], bank[0][:, 0:B])
            dve.tensor_scalar(v["mod_c"][:], bank[1][:, 0:B], 1.0, None, ALU.add)
            link(dve.tensor_copy(rows[:], bank[2][0:B, :].rearrange("b (m c) -> b m c", c=C)))
            link(dve.tensor_scalar(rows[:, 2, :], rows[:, 2, :], 1.0, None, ALU.add))
            link(dve.tensor_scalar(absr[:], rows[:, 0:4:3, :], -1.0, None, ALU.mult))
            link(dve.tensor_tensor(absr[:], absr[:], rows[:, 0:4:3, :], ALU.max))
            link(dve.tensor_scalar(absr[:], absr[:], 0.25, None, ALU.max))
            link(dve.tensor_scalar(sgn[:], rows[:, 0:4:3, :], 0.0, None, ALU.is_ge))
            link(dve.tensor_scalar(sgn[:], sgn[:], 2.0, -1.0, ALU.mult, ALU.add))
            dve.tensor_tensor(rows[:, 0:4:3, :], absr[:], sgn[:], ALU.mult).then_inc(rows_ready, 1)


def attention(nc, ctx, sb, sem, bank, v):
    ident = v["ident"]
    qs = [sb(ctx, f"q_stack{c}", [P, HG * T], F32R) for c in range(NCH)]
    ks = [sb(ctx, f"k_stack{c}", [P, HG * T], F32R) for c in range(NCH)]
    zero2 = sb(ctx, "zero2", [2, HG * T], F32R)
    prob = [sb(ctx, f"prob{i}", [P, HG * P_COLS]) for i in range(2)]
    u_sb = sb(ctx, "u_sb", [P, NCH, T])
    x_in = sb(ctx, "x_in", [P, TT, C])
    xn = sb(ctx, "xn", [P, TT, C])
    hf = sb(ctx, "hf", [P, T])
    hh, hl = sb(ctx, "hh", [P, T], F32R), sb(ctx, "hl", [P, T], F32R)
    q_cos, q_sin = sb(ctx, "q_cos", [P, T]), sb(ctx, "q_sin", [P, T])
    k_cos, k_sin, k_sum = sb(ctx, "k_cos", [P, T]), sb(ctx, "k_sin", [P, T]), sb(ctx, "k_sum", [P, T])
    qf = sb(ctx, "qf", [P, T])
    qh, ql = sb(ctx, "qh", [P, T], F32R), sb(ctx, "ql", [P, T], F32R)
    kh, kl = sb(ctx, "kh", [P, T], F32R), sb(ctx, "kl", [P, T], F32R)
    vx = [sb(ctx, f"vx{i}", [P, TT, H, VW]) for i in range(2)]
    mx = [sb(ctx, f"mx{i}", [P, HG * TT]) for i in range(2)]
    mh, ml = sb(ctx, "mh", [HG * TT, P], F32R), sb(ctx, "ml", [HG * TT, P], F32R)
    y = sb(ctx, "y", [P, TT, C])
    rden = sb(ctx, "rden", [P, TT, H])
    y_t = sb(ctx, "y_t", [P, T])
    x_res = sb(ctx, "x_res", [P, TT, C])
    mod_b = sb(ctx, "mod_b", [P, 4, C])
    wc_g, bias_cg = sb(ctx, "wc_g", [P, C]), sb(ctx, "bias_cg", [P, C])
    xb = sb(ctx, "xb", [P, TT, C])
    x1 = sb(ctx, "x1", [P, TT, C])
    xn2 = sb(ctx, "xn2", [P, TT, C])
    h2 = sb(ctx, "h2", [P, TT, C])
    h2_t = sb(ctx, "h2_t", [P, T])
    queued = sb(ctx, "queued", [P, TOP, TT, ROW])
    base = sb(ctx, "base", [P, TT, C])
    lg = sb(ctx, "lg", [P, TT, E])
    top8 = sb(ctx, "top8", [P, TT, 8])
    idx8 = sb(ctx, "idx8", [P, TT, 8], U32)
    idxf = sb(ctx, "idxf", [P, TT, 2])
    hot = sb(ctx, "hot", [P, 2, TT, E])
    gdiff, gexp = sb(ctx, "gdiff", [P, TT]), sb(ctx, "gexp", [P, TT])
    both = sb(ctx, "both", [P, TT, E], BF16)
    rank, rank_k = sb(ctx, "rank", [P, TT, E]), sb(ctx, "rank_k", [P, TOP, TT, E])
    pos_f, pos = sb(ctx, "pos_f", [P, TOP, TT]), sb(ctx, "pos", [P, TOP, TT], U32)
    gden, gw, gsum = sb(ctx, "gden", [P, TT]), sb(ctx, "gw", [P, 2, TT]), sb(ctx, "gsum", [P, TT])
    ln = [dict(st=sb(ctx, f"ln_st{i}", [P, TT, 6]), mv=sb(ctx, f"ln_mv{i}", [P, TT, 2]),
               va=sb(ctx, f"ln_va{i}", [P, TT]), hb=sb(ctx, f"ln_hb{i}", [P, TT], I32),
               y=sb(ctx, f"ln_y{i}", [P, TT]), t=sb(ctx, f"ln_t{i}", [P, TT])) for i in range(3)]

    s_bank, st_bank, u_bank, f_bank, side = bank[0:2], bank[2:5], bank[5], bank[6], bank[7]

    x_loaded, t_loaded, outs_stored = sem("x_loaded"), sem("t_loaded"), sem("outs_stored")
    const_ready = sem("const_ready")
    stack_ready = [sem(f"stack_ready{c}") for c in range(NCH)]
    rows_ready = [sem(f"max_rows_ready{c}") for c in range(NCH)]
    xn_ready, xt_ready, hf_ready, h_ready = sem("xn_ready"), sem("xt_ready"), sem("hf_ready"), sem("h_ready")
    v_ready, v_used = sem("v_ready"), sem("v_used")
    f_ready, f_used = sem("f_ready"), sem("f_used")
    ksum_ready, kh_ready, kl_ready = sem("ksum_ready"), sem("kh_ready"), sem("kl_ready")
    krope_ready, ql_ready = sem("krope_ready"), sem("ql_ready")
    s_ready, s_used = sem("s_ready"), sem("s_used")
    mt_ready, mh_ready, mt_used = sem("mt_ready"), sem("mh_ready"), sem("mt_used")
    st_ready, st_used = sem("st_ready"), sem("st_used")
    av_ready, u_copied = sem("av_ready"), sem("u_copied")
    ut_ready, ut_used = sem("ut_ready"), sem("ut_used")
    rden_ready = sem("rden_ready")
    yt_ready, yt_used = sem("yt_ready"), sem("yt_used")
    bcg_ready, xb_ready = sem("bcg_ready"), sem("xb_ready")
    proj_ready, x1_ready = sem("proj_ready"), sem("x1_ready")
    xn2_ready, h2m_ready, h2_ready = sem("xn2_ready"), sem("h2m_ready"), sem("h2_ready")
    held = sem("held")
    ht_ready, ht_used = sem("ht_ready"), sem("ht_used")
    xh_ready, gh_ready, base_ready = sem("xh_ready"), sem("gh_ready"), sem("base_ready")
    lg_ready, lg_used = sem("lg_ready"), sem("lg_used")
    gdiff_ready, gexp_ready, gsum_ready = sem("gdiff_ready"), sem("gexp_ready"), sem("gsum_ready")
    both_ready, rank_ready, rank_used = sem("both_ready"), sem("rank_ready"), sem("rank_used")
    pos_ready, copy_ready, scattered = sem("pos_ready"), sem("copy_ready"), sem("scattered")
    ln_step = [sem(f"ln_step{i}") for i in range(3)]
    rt_step = sem("router_step")
    RT_STEPS = 13
    SCATTERED = 16 * TOP * TT

    def at(b, c, ahead):
        return b + (c + ahead) // NCH, (c + ahead) % NCH

    def exists(c, ahead, last):
        return not last or c + ahead < NCH

    def pe_scores(pe, stacks, out, h, tile, col, wide_queries):
        q, k = stacks
        o = h * T
        if wide_queries:
            n = T - P * tile
            pe.matmul(out[:, col:col + n], k[:, o + P * tile:o + P * tile + P], q[:, o + P * tile:o + T],
                      start=(col == 0), stop=False, skip_group_check=True)
            return col
        n = P * (tile + 1)
        pe.matmul(out[:, col:col + n], q[:, o + P * tile:o + P * tile + P], k[:, o:o + n],
                  start=(col == 0), stop=False, skip_group_check=True)
        return col + n - P

    def pe_piece(pe, c, p, out, wide_queries):
        kind, heads = piece(p)
        stacks = qs[c], ks[c]
        mask = v["mask_k"] if wide_queries else v["mask_q"]
        tiles = {0: [0], 1: [1, 3], 2: [2]} if wide_queries else {0: [3], 1: [2, 0], 2: [1]}
        diag, col = [], 0
        for h in heads:
            for tile in tiles[kind]:
                diag.append(pe_scores(pe, stacks, out, h, tile, col, wide_queries))
                col += T - P * tile if wide_queries else P * (tile + 1)
        if len(diag) == 1:
            return pe.matmul(out[:, diag[0]:diag[0] + P], v["ident_bf"][:], mask[:],
                             start=False, stop=True, skip_group_check=True)
        gap = diag[1] - diag[0]
        if gap == P:
            dst = out[:, diag[0]:diag[0] + 2 * P].rearrange("p (a q) -> p a q", a=2)
        elif diag[0] + 2 * gap <= 512:
            dst = out[:, diag[0]:diag[0] + 2 * gap].rearrange("p (a q) -> p a q", a=2)[:, :, 0:P]
        else:
            dst = None
        if dst is None:
            for d in diag:
                ins = pe.matmul(out[:, d:d + P], v["ident_bf"][:], mask[:], start=False, stop=True,
                                skip_group_check=True)
            return ins
        return pe.matmul(dst, v["ident_bf"][:], mask[:].unsqueeze(1).broadcast_to((P, 2, P)),
                         start=False, stop=True, skip_group_check=True)

    def pe_s(pe, b, c, p):
        n = NCH * b + c
        if p == 0:
            wait(pe, stack_ready[c], 112 * (b + 1))
        wait(pe, s_used, PIECES * n + p - 1)
        pe_piece(pe, c, p, s_bank[p % 2], False).then_inc(s_ready, 1)

    def pe_st(pe, b, c, p):
        n = NCH * b + c
        if p == 0:
            wait(pe, rows_ready[c], 32 * (b + 1))
        wait(pe, st_used, PIECES * n + p - ST_BACK[p] + 1)
        pe_piece(pe, c, p, st_bank[ST_BANK[p]], True).then_inc(st_ready, 1)

    def pe_av(pe, b, c, odd, j):
        n = NCH * b + c
        if j == 0:
            wait(pe, st_used, PIECES * (n + 1))
            wait(pe, v_ready, b + 1)
            wait(pe, u_copied, n)
        for h in range(HG):
            ins = pe.matmul(u_bank[L * h:L * h + VW, P * j:T], vx[odd][:, j, HG * c + h, :],
                            prob[c % 2][:, P_COLS * h + P_OFF[j]:P_COLS * h + P_OFF[j] + T - P * j],
                            start=(j == 0), stop=(j == TT - 1), skip_group_check=True)
        if j == TT - 1:
            ins.then_inc(av_ready, 1)

    def three(pe, out, w, x, start=True, stop=True):
        pe.matmul(out, w[0], x[0], start=start, stop=False)
        pe.matmul(out, w[0], x[1], start=False, stop=False)
        return pe.matmul(out, w[1], x[0], start=False, stop=stop)

    def pe_f(pe, b, c, part):
        n = NCH * b + c
        wait(pe, f_used, 4 * n + part)
        if part == 3:
            pe.matmul(f_bank[:], v["wqk_c"][:], q_cos[:], start=True, stop=False)
            ins = pe.matmul(f_bank[:], v["wqk_s"][:], q_sin[:], start=False, stop=True)
        else:
            wait(pe, h_ready, b + 1)
            w = (v["wk"], v["wkr"], v["wq"])[part]
            ins = three(pe, f_bank[:], [m[:, P * c:P * c + P] for m in w], [hh[:], hl[:]])
        ins.then_inc(f_ready, 1)

    side_last = [None]

    def side_take(pe):
        if side_last[0] is not None:
            wait(pe, *side_last[0])

    def pe_mt(pe, b, c):
        side_take(pe)
        n = NCH * b + c
        wait(pe, s_used, PIECES * (n + 1))
        pe.transpose(side[0:HG * TT, 0:P], mx[c % 2][:], ident[:]).then_inc(mt_ready, 1)
        side_last[0] = (mt_used, n + 1)

    def pe_xt(pe, b):
        side_take(pe)
        wait(pe, xn_ready, b + 1)
        for t in range(TT):
            ins = pe.transpose(side[:, P * t:P * t + P], xn[:, t, :], ident[:])
        ins.then_inc(xt_ready, 1)
        side_last[0] = (hf_ready, b + 1)

    def pe_v(pe, b):
        side_take(pe)
        wait(pe, h_ready, b + 1)
        for t in range(TT):
            s = slice(P * t, P * t + P)
            ins = three(pe, side[:, s], [hh[:, s], hl[:, s]], [v["wv"][0][:], v["wv"][1][:]])
        ins.then_inc(v_used, 1)
        side_last[0] = (v_ready, b + 1)

    def pe_ut(pe, b, t):
        side_take(pe)
        if t == 0:
            wait(pe, u_copied, NCH * (b + 1))
        for c in range(NCH):
            ins = pe.transpose(side[:, P * c:P * c + P], u_sb[:, c, P * t:P * t + P], ident[:])
        ins.then_inc(ut_ready, 1)
        side_last[0] = (ut_used, TT * b + t + 1)

    def pe_yt(pe, b):
        side_take(pe)
        for t in range(TT):
            ins = pe.transpose(side[:, P * t:P * t + P], y[:, t, :], ident[:])
        ins.then_inc(yt_ready, 1)
        side_last[0] = (yt_used, b + 1)

    def pe_proj(pe, b):
        side_take(pe)
        wait(pe, yt_used, b + 1)
        wait(pe, bcg_ready, b + 1)
        for t in range(TT):
            s = slice(P * t, P * t + P)
            ins = pe.matmul(side[:, s], y_t[:, s], wc_g[:], start=True, stop=True)
        ins.then_inc(proj_ready, 1)
        side_last[0] = (x1_ready, b + 1)

    def pe_ht(pe, b):
        side_take(pe)
        wait(pe, h2_ready, b + 1)
        for t in range(TT):
            ins = pe.transpose(side[:, P * t:P * t + P], h2[:, t, :], ident[:])
        ins.then_inc(ht_ready, 1)
        side_last[0] = (ht_used, b + 1)

    def pe_lg(pe, b):
        side_take(pe)
        wait(pe, ht_used, b + 1)
        for t in range(TT):
            ins = pe.matmul(side[:, E * t:E * t + E], h2_t[:, P * t:P * t + P], v["wr"][:], start=True, stop=True)
        ins.then_inc(lg_ready, 1)
        side_last[0] = (lg_used, b + 1)

    def pe_rank(pe, b):
        side_take(pe)
        wait(pe, both_ready, b + 1)
        pe.matmul(side[:, 0:TT * E], v["before"][:], both[:].rearrange("p t e -> p (t e)"),
                  start=True, stop=False, skip_group_check=True)
        for t in range(TT):
            later = TT - t
            ins = pe.matmul(side[:, E * (t + 1):E * (TT + 1)].rearrange("p (a e) -> p a e", e=E), v["ones_bf"][:],
                            both[:, t:t + 1, :].broadcast_to((P, later, E)), start=False, stop=(later == 1),
                            skip_group_check=True)
        ins.then_inc(rank_ready, 1)
        side_last[0] = (rank_used, b + 1)

    def pe_slot(pe, b, c, odd, first, last):
        for p in range(PIECES):
            pe_st(pe, b, c, p)
            if exists(c, 2, last):
                pe_s(pe, *at(b, c, 2), p)
            if 1 <= p <= 4 and not (first and c == 0):
                pe_av(pe, *at(b, c, -1), odd if c else 1 - odd, p - 1)
            if exists(c, 3, last) and p in (0, 1, 2, 4):
                pe_f(pe, *at(b, c, 3), (0, 1, 2, 4).index(p))
            if c == 3 and p == 1 and not first:
                pe_lg(pe, b - 1)
            if c == 3 and p == 5 and not first:
                pe_rank(pe, b - 1)
            if p == (2 if c == 3 else 1) and exists(c, 1, last):
                pe_mt(pe, *at(b, c, 1))
            if c == 0 and not last:
                if p == 6:
                    pe_xt(pe, b + 1)
                if p == 9:
                    pe_v(pe, b + 1)
            if c == 1 and not first:
                if p in (3, 5, 6, 7):
                    pe_ut(pe, b - 1, (3, 5, 6, 7).index(p))
                if p == 9:
                    pe_yt(pe, b - 1)
            if c == 2 and not first:
                if p == 2:
                    pe_proj(pe, b - 1)
                if p == 9:
                    pe_ht(pe, b - 1)

    def pe_open(pe):
        pe_xt(pe, 0)
        pe_v(pe, 0)
        for c in range(3):
            for part in range(4):
                pe_f(pe, 0, c, part)
            if c >= 1:
                for p in range(PIECES):
                    pe_s(pe, 0, c - 1, p)
            if c == 1:
                pe_mt(pe, 0, 0)

    def pe_close(pe, b):
        for j in range(TT):
            pe_av(pe, b, NCH - 1, b % 2, j)
        for t in range(TT):
            pe_ut(pe, b, t)
        pe_yt(pe, b)
        pe_proj(pe, b)
        pe_ht(pe, b)
        pe_lg(pe, b)
        pe_rank(pe, b)

    def act_exp(act, b, c, p):
        n = NCH * b + c
        if p == 0:
            wait(act, av_ready, n - 1)
        wait(act, st_ready, PIECES * n + p + 1)
        kind, heads = piece(p)
        src, h = st_bank[ST_BANK[p]], heads[0]
        pb = prob[c % 2]
        if kind == 2:
            dst = pb[:, P_COLS * h:P_COLS * (h + 2)].rearrange("p (a n) -> p a n", a=2)[:, :, P_OFF[2]:P_OFF[2] + 2 * P]
            act.activation(dst, src[:].rearrange("p (a n) -> p a n", a=2), ACT.Exp, scale=SCALE).then_inc(st_used, 1)
        else:
            o = P_COLS * h + (P_OFF[0] if kind == 0 else P_OFF[1])
            act.activation(pb[:, o:o + T], src[:], ACT.Exp, scale=SCALE).then_inc(st_used, 1)

    def act_u(act, b, c, ut_done):
        n = NCH * b + c
        wait(act, av_ready, n + 1)
        wait(act, ut_ready, ut_done)
        act.activation(u_sb[:, c, :], u_bank[:], ACT.Copy).then_inc(u_copied, 1)

    def act_k(act, b, c, part):
        n = NCH * b + c
        wait(act, f_ready, 4 * n + part + 1)
        wait(act, ksum_ready, n)
        dst, bias = ((k_cos, "bias_k"), (k_sin, "bias_kr"))[part]
        act.activation(dst[:], f_bank[:], ACT.Identity, bias=v[bias][:, c:c + 1]).then_inc(f_used, 1)

    def act_qh(act, b, c):
        n = NCH * b + c
        wait(act, f_ready, 4 * n + 4)
        wait(act, ql_ready, n)
        act.activation(qf[:], f_bank[:], ACT.Identity, bias=v["param"]("wqk_b"))
        pb, pc = at(b, c, -1)
        wait(act, stack_ready[pc], 112 * (pb + 1))
        act.activation(qh[:], f_bank[:], ACT.Identity, bias=v["param"]("wqk_b")).then_inc(f_used, 1)

    def act_kh(act, b, c):
        n = NCH * b + c
        wait(act, ksum_ready, n + 1)
        pb, pc = at(b, c, -1)
        wait(act, stack_ready[pc], 112 * (pb + 1))
        act.activation(kh[:], k_sum[:], ACT.Copy).then_inc(kh_ready, 1)

    def act_mh(act, b, c):
        n = NCH * b + c
        wait(act, mt_ready, n + 1)
        pb, pc = at(b, c, -1)
        wait(act, rows_ready[pc], 32 * (pb + 1))
        act.activation(mh[:], side[0:HG * TT, 0:P], ACT.Copy).then_inc(mh_ready, 1)

    def act_hf(act, b):
        wait(act, xt_ready, b + 1)
        wait(act, h_ready, b)
        wait(act, f_ready, 16 * b)
        wait(act, v_used, b)
        act.activation(hf[:], side[:], ACT.Identity, bias=col(v["mod_s"], b), scale=col(v["mod_c"], b))
        act.activation(hh[:], side[:], ACT.Identity, bias=col(v["mod_s"], b), scale=col(v["mod_c"], b))\
           .then_inc(hf_ready, 1)

    def col(t, b):
        return t[:, b:b + 1] if isinstance(b, int) else t[:, bass.ds(b, 1)]

    def act_yt(act, b):
        wait(act, yt_ready, b + 1)
        wait(act, proj_ready, b)
        act.activation(y_t[:], side[:], ACT.Copy).then_inc(yt_used, 1)

    def act_ht(act, b):
        wait(act, ht_ready, b + 1)
        wait(act, lg_ready, b)
        act.activation(h2_t[:], side[:], ACT.Copy).then_inc(ht_used, 1)

    def act_gexp(act, b):
        wait(act, gdiff_ready, b + 1)
        wait(act, gsum_ready, b)
        act.activation(gexp[:], gdiff[:], ACT.Exp).then_inc(gexp_ready, 1)

    def act_slot(act, b, c, odd, first, last):
        for p in range(PIECES):
            act_exp(act, b, c, p)
            if exists(c, 3, last):
                if p in (0, 1):
                    act_k(act, *at(b, c, 3), p)
                if p == 3:
                    act_kh(act, *at(b, c, 3))
                if p == 4:
                    act_qh(act, *at(b, c, 3))
            if p == (2 if c == 3 else 1) and exists(c, 1, last):
                act_mh(act, *at(b, c, 1))
            if c == 0 and not last and p == 6:
                act_hf(act, b + 1)
            if p == 8 and not (first and c == 0):
                pb, pc = at(b, c, -1)
                act_u(act, pb, pc, TT * pb)
            if c == 1 and p == 9 and not first:
                act_yt(act, b - 1)
            if c == 2 and p == 9 and not first:
                act_ht(act, b - 1)
            if c == 3 and p == 3 and not first:
                act_gexp(act, b - 1)

    def act_open(act):
        act_hf(act, 0)
        for c in range(3):
            act_k(act, 0, c, 0)
            act_k(act, 0, c, 1)
            act_kh(act, 0, c)
            act_qh(act, 0, c)
            if c == 1:
                act_mh(act, 0, 0)

    def act_close(act, b):
        act_u(act, b, NCH - 1, TT * b)
        act_yt(act, b)
        act_ht(act, b)
        act_gexp(act, b)

    def dve_max(dve, b, c, p):
        n = NCH * b + c
        if p == 0:
            wait(dve, mt_ready, n - 1)
        wait(dve, s_ready, PIECES * n + p + 1)
        kind, heads = piece(p)
        src, h, m = s_bank[p % 2], heads[0], mx[c % 2]
        if kind == 0:
            ins = dve.tensor_reduce(m[:, TT * h + 3:TT * h + 4], src[:], AX.X, ALU.max, negate=True)
        elif kind == 1:
            dve.tensor_reduce(m[:, TT * h + 2:TT * h + 3], src[:, 0:3 * P], AX.X, ALU.max, negate=True)
            ins = dve.tensor_reduce(m[:, TT * h:TT * h + 1], src[:, 3 * P:4 * P], AX.X, ALU.max, negate=True)
        else:
            ins = dve.tensor_reduce(m[:, TT * h + 1:TT * h + 2 + TT:TT], src[:].rearrange("p (a n) -> p a n", a=2),
                                    AX.X, ALU.max, negate=True)
        ins.then_inc(s_used, 1)

    def dve_ml(dve, b, c):
        n = NCH * b + c
        wait(dve, mh_ready, n + 1)
        dve.tensor_tensor(ml[:], side[0:HG * TT, 0:P], mh[:].bitcast(F32), ALU.subtract).then_inc(mt_used, 1)

    def dve_q(dve, b, c):
        n = NCH * b + c
        wait(dve, f_ready, 4 * n + 3)
        dve.scalar_tensor_tensor(q_cos[:], f_bank[:], v["bias_q"][:, c:c + 1], v["cos_t"][:], ALU.add, ALU.mult)
        dve.scalar_tensor_tensor(q_sin[:], f_bank[:], v["bias_q"][:, c:c + 1], v["sin_t"][:], ALU.add, ALU.mult)\
           .then_inc(f_used, 1)

    def dve_ksum(dve, b, c):
        n = NCH * b + c
        wait(dve, krope_ready, n + 1)
        wait(dve, kl_ready, n)
        dve.tensor_tensor(k_sum[:], k_cos[:], k_sin[:], ALU.add).then_inc(ksum_ready, 1)

    def dve_kl(dve, b, c):
        n = NCH * b + c
        wait(dve, kh_ready, n + 1)
        dve.tensor_tensor(kl[:], k_sum[:], kh[:].bitcast(F32), ALU.subtract).then_inc(kl_ready, 1)

    def dve_norm(dve, b, i, part, src, dst, done):
        w = ln[i]
        at_step = [(0, 5, 11, 14)[part]]

        def link(ins):
            at_step[0] += 1
            ins.then_inc(ln_step[i], 1)
            wait(dve, ln_step[i], LN_STEPS * b + at_step[0])

        def newton():
            link(dve.scalar_tensor_tensor(w["t"][:], w["y"][:], -0.5, w["y"][:], ALU.mult, ALU.mult))
            link(dve.tensor_tensor(w["t"][:], w["t"][:], w["va"][:], ALU.mult))
            link(dve.scalar_tensor_tensor(w["y"][:], w["t"][:], 1.5, w["y"][:], ALU.add, ALU.mult))

        if part == 0:
            for t in range(TT):
                ins = dve.bn_stats(w["st"][:, t, :], src[:, t, :])
            link(ins)
            dve.sem_inc(held, 1)
            for t in range(TT):
                ins = dve.bn_aggr(w["mv"][:, t, :], w["st"][:, t, :])
            link(ins)
            link(dve.tensor_scalar(w["va"][:], w["mv"][:, :, 1], LN_EPS, None, ALU.add))
            link(dve.tensor_scalar(w["hb"][:], w["va"][:].bitcast(I32), 1, None, ALU.logical_shift_right))
            link(dve.tensor_scalar(w["y"][:].bitcast(I32), w["hb"][:], -1.0, float(RSQRT_MAGIC), ALU.mult, ALU.add))
        elif part == 1:
            newton()
            newton()
        elif part == 2:
            newton()
        for t in {2: (0, 1), 3: (2, 3)}.get(part, ()):
            ins = dve.tensor_scalar(dst[:, t, :], src[:, t, :], w["mv"][:, t, 0:1], w["y"][:, t:t + 1],
                                    ALU.subtract, ALU.mult)
        if part == 3:
            ins.then_inc(done, 1)

    def dve_l(dve, b, part):
        if part == 0:
            wait(dve, x_loaded, 16 * (b + 1))
            wait(dve, xt_ready, b)
        dve_norm(dve, b, 0, part, x_in, xn, xn_ready)

    def dve_v(dve, b, odd):
        wait(dve, v_used, b + 1)
        wait(dve, av_ready, NCH * (b - 1))
        dve.tensor_tensor(vx[odd][:, :, :, 0:HD], side[:].rearrange("p (t h d) -> p t h d", t=TT, d=HD),
                          v["bias_v"][:].rearrange("p (h d) -> p h d", d=HD).unsqueeze(1).broadcast_to((P, TT, H, HD)),
                          ALU.add).then_inc(v_ready, 1)

    def dve_ut(dve, b, t):
        wait(dve, ut_ready, TT * b + t + 1)
        if t == 0:
            wait(dve, yt_ready, b)
        heads = side[:].rearrange("p (h l) -> p h l", l=L)
        dve.reciprocal(rden[:, t, :], heads[:, :, HD]).then_inc(rden_ready, 1)
        wait(dve, rden_ready, TT * b + t + 1)
        dve.tensor_tensor(y[:, t, :].rearrange("p (h d) -> p h d", d=HD), heads[:, :, 0:HD],
                          rden[:, t, :].unsqueeze(2).broadcast_to((P, H, HD)), ALU.mult).then_inc(ut_used, 1)

    def dve_x1(dve, b):
        wait(dve, proj_ready, b + 1)
        wait(dve, xb_ready, b + 1)
        dve.tensor_tensor(x1[:].rearrange("p t c -> p (t c)"), side[:], xb[:].rearrange("p t c -> p (t c)"), ALU.add)\
           .then_inc(x1_ready, 1)

    def dve_xn2(dve, b, part):
        if part == 0:
            wait(dve, x1_ready, b + 1)
        dve_norm(dve, b, 1, part, x1, xn2, xn2_ready)

    def dve_xh(dve, b, part):
        if part == 0:
            wait(dve, h2_ready, b + 1)
            wait(dve, scattered, SCATTERED * b)
        dve_norm(dve, b, 2, part, h2, queued[:, 0, :, 0:C], xh_ready)

    def dve_lg(dve, b):
        wait(dve, lg_ready, b + 1)
        dve.tensor_tensor(lg[:], side[:, 0:TT * E].rearrange("p (t e) -> p t e", e=E),
                          v["bias_r"][:].unsqueeze(1).broadcast_to((P, TT, E)), ALU.add).then_inc(lg_used, 1)

    def dve_router(dve, b, part):
        at_step = [(0, 3, 4, 8, 13)[part]]

        def link(ins):
            at_step[0] += 1
            ins.then_inc(rt_step, 1)
            wait(dve, rt_step, RT_STEPS * b + at_step[0])

        if part == 0:
            wait(dve, lg_used, b + 1)
            dve.sem_inc(held, 1)
            for t in range(TT):
                ins = dve.max(top8[:, t, :], lg[:, t, :])
            link(ins)
            dve.tensor_tensor(gdiff[:], top8[:, :, 1], top8[:, :, 0], ALU.subtract).then_inc(gdiff_ready, 1)
            for t in range(TT):
                ins = dve.max_index(idx8[:, t, :], top8[:, t, :], lg[:, t, :])
            link(ins)
            link(dve.tensor_copy(idxf[:], idx8[:, :, 0:TOP]))
        elif part == 1:
            for k in range(TOP):
                ins = dve.tensor_tensor(hot[:, k], v["iota_e"][:].unsqueeze(1).broadcast_to((P, TT, E)),
                                        idxf[:, :, k:k + 1].broadcast_to((P, TT, E)), ALU.is_equal)
            link(ins)
            wait(dve, rank_used, b)
            dve.tensor_tensor(both[:], hot[:, 0], hot[:, 1], ALU.add).then_inc(both_ready, 1)
        elif part == 2:
            wait(dve, gexp_ready, b + 1)
            link(dve.tensor_scalar(gden[:], gexp[:], 1.0, None, ALU.add))
            link(dve.reciprocal(gw[:, 0], gden[:]))
            link(dve.tensor_tensor(gw[:, 1], gw[:, 0], gexp[:], ALU.mult))
            wait(dve, scattered, SCATTERED * b)
            dve.tensor_scalar(queued[:, :, :, C], gw[:], 1.0, None, ALU.mult)
            link(dve.tensor_tensor(gsum[:], gw[:, 0], gw[:, 1], ALU.add))
            dve.sem_inc(gsum_ready, 1)
        elif part == 3:
            wait(dve, rank_ready, b + 1)
            link(dve.tensor_tensor(rank[:], side[:, 0:TT * E].rearrange("p (t e) -> p t e", e=E),
                                   v["end_row"][:].unsqueeze(1).broadcast_to((P, TT, E)), ALU.add))
            dve.tensor_tensor(v["end_row"][:], v["end_row"][:], side[:, TT * E:(TT + 1) * E], ALU.add)\
               .then_inc(rank_used, 1)
            for k in range(TOP):
                ins = dve.tensor_tensor(rank_k[:, k], rank[:], hot[:, k], ALU.mult)
            link(ins)
            link(dve.tensor_reduce(pos_f[:], rank_k[:], AX.X, ALU.add))
            link(dve.tensor_scalar(queued[:, :, :, C + 1].bitcast(U32), v["token"][:], 1.0, None, ALU.mult))
            link(dve.tensor_scalar(v["token"][:], v["token"][:], float(T), None, ALU.add))
            dve.tensor_scalar(pos[:], pos_f[:], 1.0, None, ALU.mult).then_inc(pos_ready, 1)
        else:
            wait(dve, gh_ready, b + 1)
            wait(dve, outs_stored, 16 * b)
            for t in range(TT):
                ins = dve.scalar_tensor_tensor(base[:, t, :], xn2[:, t, :], gsum[:, t:t + 1], x1[:, t, :], ALU.mult, ALU.add)
            ins.then_inc(base_ready, 1)

    def dve_slot(dve, b, c, odd, first, last):
        for p in range(PIECES):
            if exists(c, 2, last):
                dve_max(dve, *at(b, c, 2), p)
            if exists(c, 3, last):
                if p == 2:
                    dve_q(dve, *at(b, c, 3))
                if p == 3:
                    dve_ksum(dve, *at(b, c, 3))
                if p == 4:
                    dve_kl(dve, *at(b, c, 3))
            if p == (2 if c == 3 else 1) and exists(c, 1, last):
                dve_ml(dve, *at(b, c, 1))
            if c == 0 and not last:
                if p in (2, 3, 4, 5):
                    dve_l(dve, b + 1, p - 2)
                if p == 9:
                    dve_v(dve, b + 1, 1 - odd)
            if c == 1 and not first and p in (3, 5, 6, 7):
                dve_ut(dve, b - 1, (3, 5, 6, 7).index(p))
            if c == 2 and not first:
                if p == 2:
                    dve_x1(dve, b - 1)
                if p in (3, 4, 5, 6):
                    dve_xn2(dve, b - 1, p - 3)
            if c == 3 and not first:
                if p == 1:
                    dve_lg(dve, b - 1)
                if p in (5, 6, 7, 8):
                    dve_xh(dve, b - 1, p - 5)
                if p in (2, 3, 4, 6, 9):
                    dve_router(dve, b - 1, (2, 3, 4, 6, 9).index(p))

    def dve_open(dve):
        dve.memset(zero2[:].bitcast(F32), 0.0)
        for i in range(2):
            dve.memset(vx[i][:], 1.0)
        for c in range(NCH):
            dve.memset(qs[c][ROW_MAX:P, :].bitcast(F32), 0.0)
            dve.memset(ks[c][ROW_MAX:P, :].bitcast(F32), 0.0)
        dve.memset(u_bank[:], 0.0)
        dve.memset(ml[:].bitcast(F32), 0.0).then_inc(const_ready, 1)
        wait(dve, const_ready, 1)
        for c in range(NCH):
            ins = dve.memset(ks[c][ROW_MAX:ROW_MAX + 2, :].bitcast(F32), 1.0)
        ins.then_inc(const_ready, 1)
        for part in range(4):
            dve_l(dve, 0, part)
        dve_v(dve, 0, 0)
        for c in range(3):
            dve_q(dve, 0, c)
            dve_ksum(dve, 0, c)
            dve_kl(dve, 0, c)
            if c >= 1:
                for p in range(PIECES):
                    dve_max(dve, 0, c - 1, p)
            if c == 1:
                dve_ml(dve, 0, 0)

    def dve_close(dve, b):
        for t in range(TT):
            dve_ut(dve, b, t)
        dve_x1(dve, b)
        for part in range(4):
            dve_xn2(dve, b, part)
        for part in range(4):
            dve_xh(dve, b, part)
        dve_lg(dve, b)
        for part in range(5):
            dve_router(dve, b, part)

    def pool_k(pool, b, c):
        n = NCH * b + c
        wait(pool, f_used, 4 * n + 1)
        pool.tensor_tensor(k_cos[:], k_cos[:], v["cos_t"][:], ALU.mult)
        wait(pool, f_used, 4 * n + 2)
        pool.tensor_tensor(k_sin[:], k_sin[:], v["sin_t"][:], ALU.mult).then_inc(krope_ready, 1)
        wait(pool, f_used, 4 * n + 4)
        pool.tensor_tensor(ql[:], qf[:], qh[:].bitcast(F32), ALU.subtract).then_inc(ql_ready, 1)

    def pool_h(pool, b):
        wait(pool, hf_ready, b + 1)
        pool.tensor_tensor(hl[:], hf[:], hh[:].bitcast(F32), ALU.subtract).then_inc(h_ready, 1)

    def pool_xb(pool, b):
        wait(pool, t_loaded, 32 * (b + 1))
        wait(pool, proj_ready, b)
        wait(pool, x1_ready, b)
        pool.tensor_tensor(wc_g[:], v["param"]("cproj_t"), mod_b[:, 0, :], ALU.mult)
        pool.tensor_tensor(bias_cg[:], v["bias_c"][:], mod_b[:, 0, :], ALU.mult).then_inc(bcg_ready, 1)
        wait(pool, bcg_ready, b + 1)
        pool.tensor_tensor(xb[:], x_res[:], bias_cg[:].unsqueeze(1).broadcast_to((P, TT, C)), ALU.add).then_inc(xb_ready, 1)

    def pool_h2(pool, b):
        wait(pool, xn2_ready, b + 1)
        wait(pool, ht_ready, b)
        wait(pool, xh_ready, b)
        pool.tensor_tensor(h2[:], xn2[:], mod_b[:, 2, :].unsqueeze(1).broadcast_to((P, TT, C)), ALU.mult).then_inc(h2m_ready, 1)
        wait(pool, h2m_ready, b + 1)
        pool.tensor_tensor(h2[:], h2[:], mod_b[:, 1, :].unsqueeze(1).broadcast_to((P, TT, C)), ALU.add).then_inc(h2_ready, 1)
        wait(pool, h2_ready, b + 1)
        pool.tensor_tensor(xn2[:], h2[:], mod_b[:, 3, :].unsqueeze(1).broadcast_to((P, TT, C)), ALU.mult).then_inc(gh_ready, 1)

    def pool_scatter(pool, b, tiles):
        if 0 in tiles:
            wait(pool, xh_ready, b + 1)
            wait(pool, pos_ready, b + 1)
            pool.sem_inc(held, 1)
            pool.tensor_copy(queued[:, 1, :, 0:C], queued[:, 0, :, 0:C]).then_inc(copy_ready, 1)
        wait(pool, copy_ready, b + 1)
        pool.sem_inc(held, 1)
        for t in tiles:
            for k in range(TOP):
                pool.indirect_dma_start(v["d_queue"], bass.IndirectOffsetOnAxis(pos[:, k, t:t + 1], 0),
                                        queued[:, k, t, :], None).then_inc(scattered, 16)

    def pool_slot(pool, b, c, odd, first, last):
        if c == 1 and not first:
            pool_xb(pool, b - 1)
        if exists(c, 3, last):
            pool_k(pool, *at(b, c, 3))
        if c == 0 and not last:
            pool_h(pool, b + 1)
        if c == 2 and not first:
            pool_h2(pool, b - 1)
        if c in (0, 1) and not first and not (isinstance(b, int) and b == 1):
            pool_scatter(pool, b - 2, (2 * c, 2 * c + 1))

    def pool_open(pool):
        pool_h(pool, 0)
        for c in range(3):
            pool_k(pool, 0, c)

    def pool_close(pool, b):
        pool_scatter(pool, b - 1, range(TT))
        pool_xb(pool, b)
        pool_h2(pool, b)
        pool_scatter(pool, b, range(TT))

    def sp_wait(sp, semaphore, n):
        if isinstance(n, int) and n <= 0:
            return
        sp.wait_ge(semaphore, n)
        sp.sem_inc(held, 1)

    def tokens(ap, b, width):
        t = ap.rearrange("(b t p) c -> b p t c", p=P, t=TT)
        return t[b] if isinstance(b, int) else t[bass.ds(b, 1)].rearrange("a p t c -> (a p) t c")

    x_rows = v["x"].rearrange("b t c -> (b t) c")

    def sp_x(sp, b):
        sp_wait(sp, xn_ready, b)
        sp.dma_start(x_in[:], tokens(x_rows, b, C)).then_inc(x_loaded, 16)

    def sp_t(sp, b):
        sp_wait(sp, xb_ready, b)
        sp_wait(sp, gh_ready, b)
        sp.dma_start(x_res[:], tokens(x_rows, b, C)).then_inc(t_loaded, 16)
        m = v["d_mod"]
        row = m[b:b + 1, :] if isinstance(b, int) else m[bass.ds(b, 1), :]
        sp.dma_start(mod_b[:].rearrange("p m c -> p (m c)"), row.broadcast_to((P, 4 * C))).then_inc(t_loaded, 16)

    def sp_stack(sp, b, c):
        n = NCH * b + c
        if isinstance(b, int) and b == 0:
            sp_wait(sp, const_ready, 2)
        sp_wait(sp, st_ready, PIECES * (n - NCH + 1))
        sp.dma_start(qs[c][ROW_MAX:ROW_MAX + 2, :].bitcast(F32), zero2[:].bitcast(F32)).then_inc(stack_ready[c], 16)
        sp_wait(sp, kh_ready, n + 1)
        for r, src in ((0, kh), (L, kh)):
            sp.dma_start(ks[c][r:r + L, :].bitcast(F32), src[:].bitcast(F32)).then_inc(stack_ready[c], 16)
        sp_wait(sp, kl_ready, n + 1)
        sp.dma_start(ks[c][2 * L:3 * L, :].bitcast(F32), kl[:].bitcast(F32)).then_inc(stack_ready[c], 16)
        sp_wait(sp, ql_ready, n + 1)
        for r, src in ((0, qh), (2 * L, qh), (L, ql)):
            sp.dma_start(qs[c][r:r + L, :].bitcast(F32), src[:].bitcast(F32)).then_inc(stack_ready[c], 16)

    def sp_rows(sp, b, c):
        n = NCH * b + c
        sp_wait(sp, mt_used, n + 1)
        sp_wait(sp, mh_ready, n + 1)
        for r, src in ((ROW_MAX, mh), (ROW_MAX + 1, ml)):
            sp.dma_start(qs[c][r:r + 1, :].bitcast(F32), src[:].bitcast(F32)).then_inc(rows_ready[c], 16)

    def sp_out(sp, b):
        sp_wait(sp, base_ready, b + 1)
        sp.dma_start(tokens(v["d_base"], b, C), base[:]).then_inc(outs_stored, 16)

    def sp_slot(sp, b, c, odd, first, last):
        if c == 0 and not last:
            sp_x(sp, b + 1)
        if exists(c, 1, last):
            sp_rows(sp, *at(b, c, 1))
        if exists(c, 3, last):
            sp_stack(sp, *at(b, c, 3))
        if c == 0 and not first:
            sp_t(sp, b - 1)
        if c == 3 and not first:
            sp_out(sp, b - 1)

    def sp_open(sp):
        sp_x(sp, 0)
        sp_stack(sp, 0, 0)
        sp_stack(sp, 0, 1)
        sp_rows(sp, 0, 0)
        sp_stack(sp, 0, 2)

    def sp_close(sp, b):
        sp_t(sp, b)
        sp_out(sp, b)
        sp.wait_ge(outs_stored, 16 * B)
        sp.wait_ge(scattered, SCATTERED * B)

    def run(eng, opening, slot, closing):
        side_last[0] = None
        opening(eng)
        for b in (0, 1):
            for c in range(NCH):
                slot(eng, b, c, b, b == 0, False)
        with eng.Fori(2, B - 3, 2) as i:
            for odd in (0, 1):
                for c in range(NCH):
                    slot(eng, i + 1 if odd else i, c, odd, False, False)
        for b in (B - 2, B - 1):
            for c in range(NCH):
                slot(eng, b, c, b % 2, False, b == B - 1)
        closing(eng, B - 1)

    with nc.Block() as block:
        @block.sync
        def _(sp):
            run(sp, sp_open, sp_slot, sp_close)

        @block.gpsimd
        def _(pool):
            run(pool, pool_open, pool_slot, pool_close)

        @block.scalar
        def _(act):
            run(act, act_open, act_slot, act_close)

        @block.vector
        def _(dve):
            run(dve, dve_open, dve_slot, dve_close)

        @block.tensor
        def _(pe):
            run(pe, pe_open, pe_slot, pe_close)


def feed_forward(nc, ctx, sb, sem, bank, v):
    NF = FF // P
    LAST = TILES - 1
    ident = v["ident"]
    g, bl, b1c = v["param"]("ln_g_t"), v["param"]("ln_b_t"), v["param"]("b1_t")
    w1h, w1l = sb(ctx, "w1h", [P, E * FF], F32R), sb(ctx, "w1l", [P, E * FF], F32R)
    w2h, w2l = sb(ctx, "w2h", [P, E * FF], F32R), sb(ctx, "w2l", [P, E * FF], F32R)
    b1_rows = sb(ctx, "b1_rows", [P, E * FF], F32R)
    b2_rows = sb(ctx, "b2_rows", [P, E * C], F32R)
    ones = sb(ctx, "ones", [P, P], F32R)
    w1 = sb(ctx, "w1", [P, E * FF])
    w2 = sb(ctx, "w2", [P, E * FF])
    b1f, b1fh, b1hl = sb(ctx, "b1f", [P, E * NF]), sb(ctx, "b1fh", [P, E * NF], F32R), sb(ctx, "b1hl", [P, 2 * E * NF])
    b1t = sb(ctx, "b1t", [E * NF, 2, P])
    b2f, b2h, b2l = sb(ctx, "b2f", [E, C]), sb(ctx, "b2h", [E, C], F32R), sb(ctx, "b2l", [E, C], F32R)
    fill = sb(ctx, "fill", [P, 2 * E, ROW])
    count, count_i, tiles_e = sb(ctx, "count", [1, E]), sb(ctx, "count_i", [1, E], I32), sb(ctx, "tiles_e", [1, E])
    ends, skip = sb(ctx, "ends", [1, E]), sb(ctx, "skip", [1, E])
    past, past_skip = sb(ctx, "past", [1, TILES, E]), sb(ctx, "past_skip", [1, TILES, E])
    sum_past, sum_skip, row_f = sb(ctx, "sum_past", [1, TILES]), sb(ctx, "sum_skip", [1, TILES]), sb(ctx, "row_f", [1, TILES])
    expert_of, row_of = sb(ctx, "expert_of", [1, TILES], U32), sb(ctx, "row_of", [1, TILES], U32)
    fill_at = sb(ctx, "fill_at", [1, E], U32)
    xq = [sb(ctx, f"xq{r}", [P, ROW]) for r in range(RING)]
    z = [sb(ctx, f"z{r}", [P, C]) for r in range(RING)]
    xth = [sb(ctx, f"xth{i}", [P, P], F32R) for i in range(2)]
    xtl = [sb(ctx, f"xtl{i}", [P, P], F32R) for i in range(2)]
    a = [sb(ctx, f"a{i}", [P, FF]) for i in range(2)]
    ah = [sb(ctx, f"ah{i}", [P, FF], F32R) for i in range(2)]
    al = [sb(ctx, f"al{i}", [P, FF], F32R) for i in range(2)]

    w_loaded, b_loaded, fill_stored, b_stored = sem("w_loaded"), sem("b_loaded"), sem("fill_stored"), sem("b_rows_stored")
    tab_step, tables_ready, fill_ready = sem("tab_step"), sem("tables_ready"), sem("fill_ready")
    b1_folded, b1_split, b1_turned = sem("b1_folded"), sem("b1_split"), sem("b1_turned")
    bias_out, zeroed = sem("bias_out"), sem("rows_zeroed")
    wh_ready, wl_ready = sem("wh_ready"), sem("wl_ready")
    x_loaded = [sem(f"xq_loaded{r}") for r in range(RING)]
    z_stored = [sem(f"z_stored{r}") for r in range(RING)]
    xt_ready, xh_ready, xl_ready = sem("q_xt_ready"), sem("q_xh_ready"), sem("q_xl_ready")
    hid_ready, a_ready, at_ready = sem("hid_ready"), sem("a_ready"), sem("at_ready")
    ah_ready, al_ready, y_ready, z_ready = sem("ah_ready"), sem("al_ready"), sem("y_ready"), sem("z_ready")
    held = sem("f_held")
    h_bank, at_bank, x_bank, y_bank = bank[0:2], bank[2:4], bank[4:6], bank[6:8]

    def round_of(base, j, per_round):
        return base * (per_round // RING) + per_round

    def hold(eng, semaphore, n):
        if isinstance(n, int) and n <= 0:
            return
        eng.wait_ge(semaphore, n)
        eng.sem_inc(held, 1)

    def tiles(step, eng):
        for r in range(RING):
            step(0, r)
        with eng.Fori(RING, TILES - RING, RING) as i:
            for r in range(RING):
                step(i, r)
        for r in range(RING):
            step(TILES - RING, r)

    def early(base, r, n):
        return isinstance(base, int) and base + r < n

    def final(base, r):
        return isinstance(base, int) and base + r == LAST

    def entry(table, base, r):
        j = base + r
        return table[0:1, j:j + 1] if isinstance(j, int) else table[0:1, bass.ds(j, 1)]

    with nc.Block() as block:
        @block.sync
        def _(sp):
            sp.dma_start(w1[:].rearrange("p (e f) -> p e f", e=E), v["w1"].rearrange("e p f -> p e f")).then_inc(w_loaded, 16)
            for e in range(E):
                sp.dma_start(w2[:, FF * e:FF * e + FF].rearrange("p (f c) -> p f c", c=C),
                             v["w2"][e].rearrange("(f p) c -> p f c", p=P)).then_inc(w_loaded, 16)
            sp.dma_start(b2f[:], v["b2"]).then_inc(b_loaded, 16)
            sp.wait_ge(fill_ready, 1)
            sp.dma_start(v["d_queue"][E * REGION:, :].rearrange("(g p) c -> p g c", p=P), fill[:, E:, :])\
              .then_inc(fill_stored, 16)
            sp.wait_ge(tables_ready, 1)
            for e in range(E):
                row = sp.value_load(fill_at[0:1, e:e + 1], min_val=e * REGION, max_val=e * REGION + N_TOK)
                sp.dma_start(v["d_queue"][bass.ds(row, P), :], fill[:, e, :]).then_inc(fill_stored, 16)
            sp.wait_ge(zeroed, 1)
            sp.wait_ge(bias_out, 2)
            for k, part in ((0, b2h), (1, b2l)):
                sp.dma_start(b1_rows[k:k + 1, :].bitcast(F32), b1t[:, k, :]).then_inc(b_stored, 16)
                sp.dma_start(b2_rows[k:k + 1, :].bitcast(F32), part[:].bitcast(F32)).then_inc(b_stored, 16)
            sp.wait_ge(fill_stored, 16 * (E + 1))

            def step(base, r):
                row = sp.value_load(entry(row_of, base, r), min_val=0, max_val=E * REGION + (E - 1) * P)
                hold(sp, z_stored[r], round_of(base, r, 16) - 16)
                sp.dma_start(xq[r][:], v["d_queue"][bass.ds(row, P), :]).then_inc(x_loaded[r], 16)

            tiles(step, sp)
            for r in range(RING):
                sp.wait_ge(z_stored[r], 16 * (TILES // RING))

        @block.gpsimd
        def _(pool):
            pool.memset(b1_rows[:].bitcast(F32), 0.0)
            pool.memset(b2_rows[:].bitcast(F32), 0.0)
            pool.memset(ones[:].bitcast(F32), 1.0).then_inc(zeroed, 1)

            def step(base, r):
                hold(pool, z_ready, base + (r + 1))
                pool.indirect_dma_start(v["d_y"], bass.IndirectOffsetOnAxis(xq[r][:, C + 1:C + 2].bitcast(U32), 0),
                                        z[r][:], None).then_inc(z_stored[r], 16)

            tiles(step, pool)

        @block.scalar
        def _(act):
            act.wait_ge(w_loaded, 16 * (E + 1))
            for e in range(E):
                s = slice(FF * e, FF * e + FF)
                act.activation(w1h[:, s], w1[:, s], ACT.Copy, scale=g[:, e:e + 1]).then_inc(wh_ready, 1)
            for e in range(E):
                s = slice(FF * e, FF * e + FF)
                act.activation(w2h[:, s], w2[:, s], ACT.Copy).then_inc(wh_ready, 1)

            def x_hi(base, r):
                act.wait_ge(xt_ready, base + (r + 1))
                act.activation(xth[r % 2][:], x_bank[r % 2][:, 0:P], ACT.Copy).then_inc(xh_ready, 1)

            def a_hi(base, r):
                act.wait_ge(at_ready, base + (r + 1))
                if not early(base, r, 2):
                    act.wait_ge(y_ready, base + (r - 1))
                act.activation(ah[r % 2][:], at_bank[r % 2][:], ACT.Copy).then_inc(ah_ready, 1)

            x_hi(0, 0)

            def step(base, r):
                act.wait_ge(hid_ready, base + (r + 1))
                if not early(base, r, 2):
                    act.wait_ge(at_ready, base + (r - 1))
                act.activation(a[r % 2][:], h_bank[r % 2][:], ACT.Gelu).then_inc(a_ready, 1)
                if not final(base, r):
                    x_hi(base, r + 1)
                if not early(base, r, 1):
                    a_hi(base, r - 1)

            tiles(step, act)
            a_hi(TILES, -1)

        @block.vector
        def _(dve):
            steps = 0

            def link(ins):
                nonlocal steps
                steps += 1
                ins.then_inc(tab_step, 1)
                dve.wait_ge(tab_step, steps)

            link(dve.memset(fill[:], 0.0))
            dve.tensor_copy(fill[:, :, C + 1].bitcast(U32), v["fill_target"]).then_inc(fill_ready, 1)
            dve.tensor_copy(fill_at[:], v["end_row"][0:1, :])
            link(dve.scalar_tensor_tensor(count[:], v["iota_e"][0:1, :], -float(REGION), v["end_row"][0:1, :],
                                          ALU.mult, ALU.add))
            link(dve.tensor_scalar(count_i[:], count[:], float(P - 1), None, ALU.add))
            link(dve.tensor_scalar(count_i[:], count_i[:], P.bit_length() - 1, None, ALU.logical_shift_right))
            link(dve.tensor_copy(tiles_e[:], count_i[:]))
            link(dve.tensor_copy(ends[:], tiles_e[:]))
            for e in range(1, E):
                link(dve.tensor_tensor(ends[:, e:e + 1], ends[:, e - 1:e], tiles_e[:, e:e + 1], ALU.add))
            link(dve.tensor_scalar(skip[:], tiles_e[:], -float(P), float(REGION), ALU.mult, ALU.add))
            number = v["tile_no"][0:1, :]
            link(dve.tensor_tensor(past[:], number.unsqueeze(2).broadcast_to((1, TILES, E)),
                                   ends[:].unsqueeze(1).broadcast_to((1, TILES, E)), ALU.is_ge))
            dve.tensor_reduce(sum_past[:], past[:], AX.X, ALU.add)
            link(dve.tensor_tensor(past_skip[:], past[:], skip[:].unsqueeze(1).broadcast_to((1, TILES, E)), ALU.mult))
            link(dve.tensor_reduce(sum_skip[:], past_skip[:], AX.X, ALU.add))
            dve.tensor_scalar(expert_of[:], sum_past[:], float(E - 1), None, ALU.min)
            link(dve.scalar_tensor_tensor(row_f[:], number, float(P), sum_skip[:], ALU.mult, ALU.add))
            dve.tensor_copy(row_of[:], row_f[:]).then_inc(tables_ready, 1)
            dve.wait_ge(b_loaded, 16)
            link(dve.tensor_copy(b2h[:], b2f[:]))
            dve.tensor_tensor(b2l[:], b2f[:], b2h[:].bitcast(F32), ALU.subtract).then_inc(bias_out, 1)
            dve.wait_ge(b1_folded, 1)
            link(dve.tensor_tensor(b1f[:], bank[7][:, 0:E * NF], b1c, ALU.add))
            link(dve.tensor_copy(b1fh[:], b1f[:]))
            dve.tensor_copy(b1hl[:, 0:E * NF], b1fh[:].bitcast(F32))
            dve.tensor_tensor(b1hl[:, E * NF:], b1f[:], b1fh[:].bitcast(F32), ALU.subtract).then_inc(b1_split, 1)
            dve.wait_ge(b1_turned, 1)
            dve.tensor_copy(b1t[:], bank[6][0:E * NF, 0:2 * P].rearrange("r (k p) -> r k p", k=2)).then_inc(bias_out, 1)
            for e in range(E):
                s = slice(FF * e, FF * e + FF)
                dve.wait_ge(wh_ready, e + 1)
                dve.scalar_tensor_tensor(w1l[:, s], w1[:, s], g[:, e:e + 1], w1h[:, s].bitcast(F32), ALU.mult, ALU.subtract)
            for e in range(E):
                s = slice(FF * e, FF * e + FF)
                dve.wait_ge(wh_ready, E + e + 1)
                ins = dve.tensor_tensor(w2l[:, s], w2[:, s], w2h[:, s].bitcast(F32), ALU.subtract)
            ins.then_inc(wl_ready, 1)

            def x_lo(base, r):
                dve.wait_ge(xh_ready, base + (r + 1))
                dve.tensor_tensor(xtl[r % 2][:], x_bank[r % 2][:, 0:P], xth[r % 2][:].bitcast(F32), ALU.subtract)\
                   .then_inc(xl_ready, 1)

            def a_lo(base, r):
                dve.wait_ge(ah_ready, base + (r + 1))
                dve.tensor_tensor(al[r % 2][:], at_bank[r % 2][:], ah[r % 2][:].bitcast(F32), ALU.subtract)\
                   .then_inc(al_ready, 1)

            def out(base, r, place):
                dve.wait_ge(y_ready, base + (r + 1))
                dve.tensor_scalar(z[place][:], y_bank[place % 2][:, 0:C], xq[place][:, C:C + 1], None, ALU.mult)\
                   .then_inc(z_ready, 1)

            x_lo(0, 0)

            def step(base, r):
                if not final(base, r):
                    x_lo(base, r + 1)
                if not early(base, r, 1):
                    a_lo(base, r - 1)
                if not early(base, r, 2):
                    out(base, r - 2, (r - 2) % RING)

            tiles(step, dve)
            a_lo(TILES, -1)
            out(TILES, -2, RING - 2)
            out(TILES, -1, RING - 1)

        @block.tensor
        def _(pe):
            pe.wait_ge(w_loaded, 16 * (E + 1))
            for q in range(E * NF):
                ins = pe.matmul(bank[7][:, q:q + 1], w1[:, P * q:P * q + P], bl[:, q // NF:q // NF + 1], start=True, stop=True)
            ins.then_inc(b1_folded, 1)
            pe.wait_ge(b1_split, 1)
            for k in range(2):
                ins = pe.transpose(bank[6][0:E * NF, P * k:P * k + P], b1hl[:, E * NF * k:E * NF * (k + 1)], ident[:])
            ins.then_inc(b1_turned, 1)

            def turn_x(base, r):
                place = r % RING
                if r < RING:
                    pe.wait_ge(x_loaded[place], round_of(base, place, 16))
                else:
                    pe.wait_ge(x_loaded[place], round_of(base, place, 16) + 16)
                pe.transpose(x_bank[r % 2][:, 0:P], xq[place][:, 0:C], ident[:]).then_inc(xt_ready, 1)

            def hidden(base, r):
                n = pe.value_load(entry(expert_of, base, r), min_val=0, max_val=E - 1)
                pe.wait_ge(xl_ready, base + (r + 1))
                if not early(base, r, 2):
                    pe.wait_ge(a_ready, base + (r - 1))
                h = h_bank[r % 2][:]
                s = bass.ds(n * FF, FF)
                pe.matmul(h, xth[r % 2][:], w1h[:, s], start=True, stop=False)
                pe.matmul(h, xth[r % 2][:], w1l[:, s], start=False, stop=False)
                pe.matmul(h, xtl[r % 2][:], w1h[:, s], start=False, stop=False)
                pe.matmul(h, ones[:], b1_rows[:, s], start=False, stop=True).then_inc(hid_ready, 1)

            def turn_a(base, r):
                pe.wait_ge(a_ready, base + (r + 1))
                if not early(base, r, 2):
                    pe.wait_ge(al_ready, base + (r - 1))
                for f in range(NF):
                    ins = pe.transpose(at_bank[r % 2][:, P * f:P * f + P], a[r % 2][:, P * f:P * f + P], ident[:])
                ins.then_inc(at_ready, 1)

            def output(base, r):
                n = pe.value_load(entry(expert_of, base, r), min_val=0, max_val=E - 1)
                pe.wait_ge(al_ready, base + (r + 1))
                if not early(base, r, 2):
                    pe.wait_ge(z_ready, base + (r - 1))
                y = y_bank[r % 2][:, 0:C]
                pe.matmul(y, ones[:], b2_rows[:, bass.ds(n * C, C)], start=True, stop=False)
                for f in range(NF):
                    s = slice(P * f, P * f + P)
                    w = bass.ds(n * FF + P * f, C)
                    pe.matmul(y, ah[r % 2][:, s], w2h[:, w], start=False, stop=False)
                    pe.matmul(y, ah[r % 2][:, s], w2l[:, w], start=False, stop=False)
                    ins = pe.matmul(y, al[r % 2][:, s], w2h[:, w], start=False, stop=(f == NF - 1))
                ins.then_inc(y_ready, 1)

            pe.wait_ge(wl_ready, 1)
            pe.wait_ge(zeroed, 1)
            pe.wait_ge(b_stored, 64)
            pe.wait_ge(tables_ready, 1)
            turn_x(0, 0)

            def step(base, r):
                hidden(base, r)
                if not final(base, r):
                    turn_x(base, r + 1)
                if not early(base, r, 1):
                    turn_a(base, r - 1)
                if not early(base, r, 2):
                    output(base, r - 2)

            tiles(step, pe)
            turn_a(TILES, -1)
            output(TILES, -2)
            output(TILES, -1)


def combine(nc, ctx, sb, sem, v):
    PLACES = 4
    gb = sb(ctx, "gb", [P, B, C])
    base = [sb(ctx, f"c_base{r}", [P, TT, C]) for r in range(PLACES)]
    y = [[sb(ctx, f"c_y{k}_{r}", [P, TT, C]) for r in range(PLACES)] for k in range(TOP)]
    o = [sb(ctx, f"c_out{r}", [P, TT, C]) for r in range(PLACES)]
    gb_loaded = sem("gb_loaded")
    loaded = [sem(f"c_loaded{r}") for r in range(PLACES)]
    stored = [sem(f"c_stored{r}") for r in range(PLACES)]
    added, scaled, out_ready, held = sem("c_added"), sem("c_scaled"), sem("c_out_ready"), sem("c_held")

    def tokens(ap, b):
        t = ap.rearrange("(b t p) c -> b p t c", p=P, t=TT)
        return t[b] if isinstance(b, int) else t[bass.ds(b, 1)].rearrange("a p t c -> (a p) t c")

    def batches(eng, step):
        for r in range(PLACES):
            step(r, r, 0)
        with eng.Fori(PLACES, B - PLACES + 1, PLACES) as i:
            for r in range(PLACES):
                step(i + r, r, i * (16 // PLACES))

    with nc.Block() as block:
        @block.sync
        def _(sp):
            sp.dma_start(gb[:], v["d_mod"][:, 3 * C:4 * C].rearrange("(a b) c -> a b c", a=1).broadcast_to((P, B, C)))\
              .then_inc(gb_loaded, 16)

            def step(b, r, before):
                if not isinstance(before, int):
                    sp.wait_ge(stored[r], before)
                    sp.sem_inc(held, 1)
                sp.dma_start(y[0][r][:], tokens(v["d_y"][0:N_TOK, :], b)).then_inc(loaded[r], 16)
                sp.dma_start(y[1][r][:], tokens(v["d_y"][N_TOK:TOP * N_TOK, :], b)).then_inc(loaded[r], 16)
                sp.dma_start(base[r][:], tokens(v["d_base"], b)).then_inc(loaded[r], 16)

            batches(sp, step)
            for r in range(PLACES):
                sp.wait_ge(stored[r], 16 * (B // PLACES))

        @block.scalar
        def _(act):
            def step(b, r, before):
                act.wait_ge(out_ready, b + 1)
                act.sem_inc(held, 1)
                act.dma_start(tokens(v["out"].rearrange("b t c -> (b t) c"), b), o[r][:]).then_inc(stored[r], 16)

            batches(act, step)

        @block.vector
        def _(dve):
            dve.wait_ge(gb_loaded, 16)

            def step(b, r, before):
                dve.wait_ge(loaded[r], before * 3 + 48)
                dve.tensor_tensor(y[0][r][:], y[0][r][:], y[1][r][:], ALU.add).then_inc(added, 1)
                row = gb[:, b:b + 1, :] if isinstance(b, int) else gb[:, bass.ds(b, 1), :]
                dve.wait_ge(added, b + 1)
                dve.tensor_tensor(y[0][r][:], y[0][r][:], row.broadcast_to((P, TT, C)), ALU.mult).then_inc(scaled, 1)
                dve.wait_ge(scaled, b + 1)
                dve.tensor_tensor(o[r][:], y[0][r][:], base[r][:], ALU.add).then_inc(out_ready, 1)

            batches(dve, step)


_INS = ['attn_x', 'attn_c_attn_w', 'attn_c_attn_b', 'attn_q2l_w', 'attn_q2l_b', 'attn_kv2l_w', 'attn_kv2l_b',
        'attn_l2o_w', 'attn_l2o_b', 'attn_wqk_w', 'attn_wqk_b', 'attn_cproj_w', 'attn_cproj_b',
        'ffn_router_W', 'ffn_router_b', 'ffn_ln_g', 'ffn_ln_b', 'ffn_W1', 'ffn_b1', 'ffn_W2', 'ffn_b2', 'c', 'wmod']
_OUTS = [((16, 512, 128), 'float32')]


def _constants():
    import numpy as np
    latent, heads = np.arange(P) // HG, np.arange(P) % HG
    inv = (np.float32(1.0) / np.float32(10000.0) ** (np.arange(0, L, 2, dtype=np.float32) / np.float32(L))).astype(np.float32)
    angle = np.outer(np.arange(T, dtype=np.float32), inv).astype(np.float32)
    cos = np.cos(angle).astype(np.float32).T[latent // 2]
    sin = np.sin(angle).astype(np.float32).T[latent // 2]
    rot = np.zeros((P, P), np.float32)
    for r in range(P):
        other = r + HG if latent[r] % 2 == 0 else r - HG
        rot[r, other] = -1.0 if latent[r] % 2 == 0 else 1.0
    mats = np.concatenate([np.eye(P, dtype=np.float32), rot], 1)
    q, k = np.meshgrid(np.arange(P), np.arange(P), indexing="ij")
    hide = np.where(k > q, np.float32(-1e30), np.float32(0))
    sel = np.concatenate([(np.arange(P)[:, None] // HD == np.arange(H)), (heads[:, None] == np.arange(HG)),
                          np.broadcast_to(np.arange(E), (P, E))], 1)
    masks = np.concatenate([hide, hide.T, sel], 1).astype(np.float32)
    p = np.arange(P)[:, None]
    route = np.concatenate([k > q, (np.arange(TOP)[:, None] * N_TOK + np.arange(TT) * P).reshape(1, -1) + p,
                            TOP * N_TOK + np.arange(2 * E) * P + p,
                            np.broadcast_to(np.arange(TILES), (P, TILES))], 1).astype(np.float32)
    return {"c_cos": np.ascontiguousarray(cos), "c_sin": np.ascontiguousarray(sin), "c_mats": mats, "c_masks": masks,
            "c_route": route}


def _small(w):
    import numpy as np
    latent_col = lambda b: np.repeat(b, HG)[:, None]
    parts = {"b_attn": w["attn_c_attn_b"].reshape(3, C).T, "q2l_b": latent_col(w["attn_q2l_b"]),
             "kv2l_b": latent_col(w["attn_kv2l_b"]), "wqk_b": latent_col(w["attn_wqk_b"]),
             "q2l_t": np.tile(w["attn_q2l_w"].T, (H, 1)), "kv2l_t": np.tile(w["attn_kv2l_w"].T, (H, 1)),
             "wqk_t": np.repeat(w["attn_wqk_w"].T, HG, axis=0), "cproj_t": w["attn_cproj_w"].T,
             "ln_g_t": w["ffn_ln_g"].T, "ln_b_t": w["ffn_ln_b"].T,
             "b1_t": w["ffn_b1"].reshape(E * FF // P, P).T, "cond_t": w["c"].T}
    return np.ascontiguousarray(np.concatenate([parts[name] for name, _ in SMALL], 1))


def kernel(**inputs):
    import numpy as _np
    import concourse.bacc as _bacc
    from concourse import mybir as _mybir
    from concourse.bass_utils import run_bass_kernel_spmd as _run

    nc = _bacc.Bacc("TRN2", target_bir_lowering=False, num_devices=1)
    w = {name: _np.ascontiguousarray(inputs["L0_" + name]) for name in _INS}
    arrays = {"x": w["attn_x"], "w_attn": w["attn_c_attn_w"], "kv2l_h": _np.tile(w["attn_kv2l_w"], (1, H)),
              "kvb_col": w["attn_kv2l_b"][:, None], "l2o_t": _np.ascontiguousarray(w["attn_l2o_w"].T),
              "l2o_b": w["attn_l2o_b"][None], "cproj_b": w["attn_cproj_b"][None], "router_w": w["ffn_router_W"],
              "router_b": w["ffn_router_b"][None], "w1": w["ffn_W1"], "w2": w["ffn_W2"], "b2": w["ffn_b2"],
              "wmod": w["wmod"], "small": _small(w), **_constants()}
    arrays = {"in_" + name: _np.ascontiguousarray(a) for name, a in arrays.items()}
    args = [nc.dram_tensor(name, a.shape, _mybir.dt.from_np(a.dtype), kind="ExternalInput").ap()
            for name, a in arrays.items()]
    for i, (shape, dtype) in enumerate(_OUTS):
        dt = _mybir.dt.from_np(_np.dtype(dtype))
        args.append(nc.dram_tensor(f"out_{i}", shape, dt, kind="ExternalOutput").ap())
    adaln_block(nc, *args)
    r = _run(nc, [arrays], core_ids=[0])
    return r.results[0]["out_0"]
```

```python
import concourse.bass as bass
from concourse import mybir
from contextlib import ExitStack

F32 = mybir.dt.float32
F32R = mybir.dt.float32r
BF16 = mybir.dt.bfloat16
U32 = mybir.dt.uint32
I32 = mybir.dt.int32
ALU = mybir.AluOpType
ACT = mybir.ActivationFunctionType
AX = mybir.AxisListType

B, T, C = 16, 512, 128
H, HD, L = 16, 8, 32
E, FF = 8, 512
P = 128
HG = P // L
NCH = H // HG
TT = T // P
VW = HD + 1
SCALE = float(L) ** -0.5
LN_EPS = 1e-5
RSQRT_MAGIC = 0x5F3759DF
MOD_SA, MOD_CA, MOD_GA, MOD_SB, MOD_CB, MOD_GB = range(6)

ROW_MAX = 3 * L

P_OFF = [0, 512, 1024, 896]
P_COLS = 1280
PIECES = 10
ST_BANK = [0, 1, 2, 0, 1, 2, 0, 1, 2, 1]
ST_BACK = [4, 2, 4, 3, 3, 3, 3, 3, 3, 2]
LN_STEPS = 14

AT = {
    "av": (1, 2, 3, 5), "f": (0, 1, 2, 4), "mt": (0, 1, 1, 1),
    "xt": 6, "v": 9, "ut": (3, 6, 8, 9), "yt": 0, "proj": 4, "ht": 2, "lg": 4, "rank": 8,
    "k_copy": (0, 1), "qh": 3, "kh": 2, "mh": (0, 1, 2, 1), "u": 9,
    "hf": 6, "yt_copy": 0, "ht_copy": 3, "gexp": 6,
    "q": 2, "ksum": 2, "kl": 4, "ml": (0, 0, 1, 1),
    "l": (0, 4, 5), "v_add": 8, "ut_div": (3, 6, 7, 8), "x1": 4, "xn2": (5, 8, 9),
    "xh": (1, 4, 5), "lg_add": 4, "router": (5, 6, 7, 8, 9),
    "rsqrt": (1, 2, 1), "xb": 0, "scatter": (2, 2),
    "s_first": (0, 0, 0, 1, 1, 0, 1, 1, 0, 1), "max_last": (0, 0, 0, 0, 0, 1, 0, 0, 0, 0),
}

N_TOK = B * T
TOP = 2
ROW = C + 2
REGION = N_TOK + P
TILES = TOP * N_TOK // P + E
RING = 8


def wait(eng, sem, n):
    if isinstance(n, int) and n <= 0:
        return
    eng.wait_ge(sem, n)


def piece(p):
    pair, q = divmod(p, 5)
    h = 2 * pair
    return [(0, [h]), (0, [h + 1]), (1, [h]), (1, [h + 1]), (2, [h, h + 1])][q]


SMALL = [("b_attn", 3), ("q2l_b", 1), ("kv2l_b", 1), ("wqk_b", 1), ("q2l_t", L), ("kv2l_t", L), ("wqk_t", L),
         ("cproj_t", C), ("ln_g_t", E), ("ln_b_t", E), ("b1_t", E * FF // P), ("cond_t", B)]
ROUTE_TOKEN = P
ROUTE_FILL = ROUTE_TOKEN + TOP * TT
ROUTE_TILE = ROUTE_FILL + 2 * E
ROUTE_COLS = ROUTE_TILE + TILES
SMALL_AT = {name: (sum(w for _, w in SMALL[:n]), width) for n, (name, width) in enumerate(SMALL)}


def adaln_block(nc, x, w_attn, kv2l_h_d, kvb_col, l2o_t, l2o_b, cproj_b, router_w, router_b, w1, w2, b2, wmod,
                small, c_cos, c_sin, c_mats, c_masks, c_route, out):
    top = ExitStack()
    with top:
        def sb(ctx, name, shape, dt=F32):
            return ctx.enter_context(nc.sbuf_tensor(name, shape, dt))

        def sem(name):
            return top.enter_context(nc.semaphore(name))

        bank = [top.enter_context(nc.psum_tensor(f"bank{i}", [P, 512], F32)) for i in range(8)]

        d_mod = nc.dram_tensor("d_mod", [B, 4 * C], F32, kind="Internal").ap()
        d_base = nc.dram_tensor("d_base", [B * T, C], F32, kind="Internal").ap()
        d_queue = nc.dram_tensor("d_queue", [E * REGION + E * P, ROW], F32, kind="Internal").ap()
        d_y = nc.dram_tensor("d_y", [TOP * N_TOK + 2 * E * P, C], F32, kind="Internal").ap()

        par = sb(top, "par", [P, sum(w for _, w in SMALL)])

        def param(name):
            at, width = SMALL_AT[name]
            return par[:, at:at + width]

        route = sb(top, "route", [P, ROUTE_COLS])
        b1t = sb(top, "b1t", [E * FF // P, 2, P])
        end_row = sb(top, "end_row", [P, E])
        iota_e = sb(top, "iota_e", [P, E])
        tile_no, fill_target = route[:, ROUTE_TILE:ROUTE_COLS], route[:, ROUTE_FILL:ROUTE_TILE]

        attn = ExitStack()
        ident = sb(top, "ident", [P, P])
        cos_t = sb(attn, "cos_t", [P, T])
        sin_t = sb(attn, "sin_t", [P, T])
        ident_bf = sb(attn, "ident_bf", [P, P], BF16)
        mask_q = sb(attn, "mask_q", [P, P], BF16)
        mask_k = sb(attn, "mask_k", [P, P], BF16)
        before = sb(attn, "before", [P, P], BF16)
        ones_bf = sb(attn, "ones_bf", [P, P], BF16)
        token = sb(attn, "token", [P, TOP, TT])
        wq = [sb(attn, f"wq{i}", [P, H * L], F32R) for i in range(2)]
        wk = [sb(attn, f"wk{i}", [P, H * L], F32R) for i in range(2)]
        wkr = [sb(attn, f"wkr{i}", [P, H * L], F32R) for i in range(2)]
        wv = [sb(attn, f"wv{i}", [P, C], F32R) for i in range(2)]
        wqk_c = sb(attn, "wqk_c", [P, P])
        wqk_s = sb(attn, "wqk_s", [P, P])
        bias_q = sb(attn, "bias_q", [P, NCH])
        bias_k = sb(attn, "bias_k", [P, NCH])
        bias_kr = sb(attn, "bias_kr", [P, NCH])
        bias_v = sb(attn, "bias_v", [P, C])
        bias_c = sb(attn, "bias_c", [P, C])
        wr = sb(attn, "wr", [P, E])
        bias_r = sb(attn, "bias_r", [P, E])
        mod_s = sb(attn, "mod_s", [P, B])
        mod_c = sb(attn, "mod_c", [P, B])

        qs = [sb(attn, f"q_stack{c}", [P, HG * T], F32R) for c in range(NCH)]
        ks = [sb(attn, f"k_stack{c}", [P, HG * T], F32R) for c in range(NCH)]

        setup = ExitStack()
        with attn:
            with setup:
                prepare(nc, setup, sb, sem, bank, locals())
            attention(nc, attn, sb, sem, bank, locals())
        base_all = sb(top, "base_all", [P, B * TT, C])
        gb_all = sb(top, "gb_all", [P, B, C])
        with ExitStack() as experts:
            feed_forward(nc, experts, sb, sem, bank, locals())
        with ExitStack() as sums:
            combine(nc, sums, sb, sem, locals())


def prepare(nc, ctx, sb, sem, bank, v):
    NF = FF // P
    mats = sb(ctx, "mats", [P, 2 * P])
    rot = mats[:, P:2 * P]
    masks = sb(ctx, "masks", [P, 2 * P])
    sel = sb(ctx, "sel", [P, H + HG + E])
    wa = sb(ctx, "wa", [P, 3, C])
    par, param = v["par"], v["param"]
    ba = param("b_attn")
    q2l_r, kv2l_r = param("q2l_t"), param("kv2l_t")
    kv2l_h = sb(ctx, "kv2l_h", [L, H, HD])
    l2o_t = sb(ctx, "l2o_t", [L, HD])
    l2o_br = sb(ctx, "l2o_br", [P, HD])
    kvb = sb(ctx, "kvb", [L, 1])
    qbc, kbc, wqk_rep = param("q2l_b"), param("kv2l_b"), param("wqk_t")
    wqk_bd = sb(ctx, "wqk_bd", [P, L, HG])
    eq = sb(ctx, "eq", [P, NCH, L, HG])
    ek = sb(ctx, "ek", [P, NCH, L, HG])
    er = sb(ctx, "er", [P, NCH, L, HG])
    g_bd = sb(ctx, "g_bd", [P, H, HD])
    g_small = sb(ctx, "g_small", [P, HD])
    bv_rep = sb(ctx, "bv_rep", [P, P])
    kvb_rep = sb(ctx, "kvb_rep", [L, P])
    l2o_rep = sb(ctx, "l2o_rep", [L, H, HD])
    cin = param("cond_t")
    ce, cs, cst = sb(ctx, "ce", [P, B]), sb(ctx, "cs", [P, B]), sb(ctx, "cst", [P, B])
    wm = sb(ctx, "wm", [P, 6, C])
    rows = sb(ctx, "rows", [B, 4, C])
    absr = sb(ctx, "absr", [B, 2, C])
    sgn = sb(ctx, "sgn", [B, 2, C])
    full = sb(ctx, "full", [P, H * L])
    w1 = sb(ctx, "w1_raw", [P, E, FF])
    b1f, b1fh, b1hl = sb(ctx, "b1f", [P, E * NF]), sb(ctx, "b1fh", [P, E * NF], F32R), sb(ctx, "b1hl", [P, 2 * E * NF])

    loaded = sem("setup_loaded")
    step = sem("setup_step")
    spread_ready, folded, folded_bias = sem("spread_ready"), sem("folded"), sem("folded_bias")
    bias_ready, wqk_ready, rotated = sem("bias_ready"), sem("wqk_ready"), sem("rotated")
    value_folded, g_ready = sem("value_folded"), sem("g_ready")
    exp_ready, silu_ready = sem("exp_ready"), sem("silu_ready")
    modulated, rows_ready, stored = sem("modulated"), sem("rows_ready"), sem("mod_rows_stored")
    w1_loaded, b1_folded, b1_split, b1_turned = sem("w1_loaded"), sem("b1_folded"), sem("b1_split"), sem("b1_turned")
    cleared = sem("stacks_cleared")
    n_loads = 0
    bl, b1c = param("ln_b_t"), param("b1_t")

    with nc.Block() as block:
        @block.sync
        def _(sp):
            nonlocal n_loads

            def load(dst, src):
                nonlocal n_loads
                sp.dma_start(dst, src).then_inc(loaded, 16)
                n_loads += 1

            load(mats[:], v["c_mats"])
            load(masks[:], v["c_masks"][:, 0:2 * P])
            load(sel[:], v["c_masks"][:, 2 * P:2 * P + H + HG + E])
            load(v["cos_t"][:], v["c_cos"])
            load(v["sin_t"][:], v["c_sin"])
            load(par[:], v["small"])
            load(v["route"][:], v["c_route"])
            load(wa[:], v["w_attn"].rearrange("(a p) c -> p a c", p=P))
            load(kv2l_h[:].rearrange("l h d -> l (h d)"), v["kv2l_h_d"])
            load(l2o_t[:], v["l2o_t"])
            load(l2o_br[:], v["l2o_b"].broadcast_to((P, HD)))
            load(kvb[:], v["kvb_col"])
            load(v["bias_c"][:], v["cproj_b"].broadcast_to((P, C)))
            load(v["wr"][:], v["router_w"])
            load(v["bias_r"][:], v["router_b"].broadcast_to((P, E)))
            load(wm[:], v["wmod"].rearrange("p (m c) -> p m c", c=C))
            sp.dma_start(w1[:], v["w1"].rearrange("e p f -> p e f")).then_inc(w1_loaded, 16)
            sp.wait_ge(rows_ready, 1)
            sp.dma_start(v["d_mod"], rows[:].rearrange("b m c -> b (m c)")).then_inc(stored, 16)
            sp.wait_ge(stored, 16)

        @block.gpsimd
        def _(pool):
            for c in range(NCH):
                pool.memset(v["qs"][c][ROW_MAX:P, :].bitcast(F32), 0.0)
                ins = pool.memset(v["ks"][c][ROW_MAX:P, :].bitcast(F32), 0.0)
            ins.then_inc(cleared, 1)
            pool.wait_ge(cleared, 1)
            for c in range(NCH):
                pool.memset(v["ks"][c][ROW_MAX:ROW_MAX + 2, :].bitcast(F32), 1.0)

        head_of_row = sel[:, 0:H]
        head_in_chunk = sel[:, H:H + HG]
        flat = lambda ap: ap.rearrange("p c l h -> p (c l h)")

        @block.tensor
        def _(pe):
            pe.wait_ge(loaded, 16 * n_loads)
            for n, (rows_of, spread_w) in enumerate(((0, eq), (1, ek), (1, er))):
                pe.wait_ge(spread_ready, n + 1)
                pe.matmul(bank[n][:], wa[:, rows_of, :], flat(spread_w[:]), start=True, stop=True).then_inc(folded, 1)
            for n, spread_w in ((0, eq), (1, ek)):
                for c in range(NCH):
                    last = pe.matmul(bank[3][:, NCH * n + c:NCH * n + c + 1], spread_w[:, c].rearrange("p l h -> p (l h)"),
                                     ba[:, n:n + 1], start=True, stop=True)
            last.then_inc(folded_bias, 1)
            pe.wait_ge(bias_ready, 1)
            pe.matmul(bank[4][:, 0:NCH], rot, v["bias_k"][:], start=True, stop=True).then_inc(rotated, 1)
            pe.wait_ge(wqk_ready, 1)
            pe.matmul(bank[5][:, 0:P], rot, v["wqk_c"][:], start=True, stop=True).then_inc(rotated, 1)
            pe.matmul(bank[6][:, 0:HD], kv2l_h[:].rearrange("l h d -> l (h d)"), l2o_t[:],
                      start=True, stop=True).then_inc(value_folded, 1)
            pe.wait_ge(g_ready, 1)
            pe.matmul(bank[6][:, 0:C], wa[:, 2, :], g_bd[:].rearrange("p h d -> p (h d)"), start=True, stop=True)
            pe.matmul(bank[7][:, 0:C], bv_rep[:], g_bd[:].rearrange("p h d -> p (h d)"), start=True, stop=False)
            pe.matmul(bank[7][:, 0:C], kvb_rep[:], l2o_rep[:].rearrange("l h d -> l (h d)"),
                      start=False, stop=True).then_inc(value_folded, 1)
            pe.wait_ge(silu_ready, 1)
            pe.matmul(bank[0][:, 0:B], wm[:, MOD_SA, :], cst[:], start=True, stop=True)
            pe.matmul(bank[1][:, 0:B], wm[:, MOD_CA, :], cst[:], start=True, stop=True)
            pe.matmul(bank[2][0:B, :], cst[:], wm[:, MOD_GA:, :].rearrange("p m c -> p (m c)"),
                      start=True, stop=True).then_inc(modulated, 1)
            pe.wait_ge(w1_loaded, 16)
            for e in range(E):
                for f in range(NF):
                    ins = pe.matmul(bank[5][:, NF * e + f:NF * e + f + 1], w1[:, e, P * f:P * f + P], bl[:, e:e + 1],
                                    start=True, stop=True)
            ins.then_inc(b1_folded, 1)
            pe.wait_ge(b1_split, 1)
            for k in range(2):
                ins = pe.transpose(bank[4][0:E * NF, P * k:P * k + P], b1hl[:, E * NF * k:E * NF * (k + 1)], v["ident"][:])
            ins.then_inc(b1_turned, 1)

        @block.scalar
        def _(act):
            act.wait_ge(loaded, 16 * n_loads)
            act.activation(ce[:], cin, ACT.Exp, scale=-1.0).then_inc(exp_ready, 1)

        @block.vector
        def _(dve):
            steps = 0

            def link(ins):
                nonlocal steps
                steps += 1
                ins.then_inc(step, 1)
                dve.wait_ge(step, steps)

            dve.wait_ge(loaded, 16 * n_loads)
            dve.tensor_copy(v["ident"][:], mats[:, 0:P])
            dve.tensor_copy(v["ident_bf"][:], mats[:, 0:P])
            dve.tensor_copy(v["mask_q"][:], masks[:, 0:P])
            dve.tensor_copy(v["mask_k"][:], masks[:, P:2 * P])
            dve.tensor_copy(v["iota_e"][:], sel[:, H + HG:H + HG + E])
            dve.tensor_copy(v["before"][:], v["route"][:, 0:P])
            dve.memset(v["ones_bf"][:], 1.0)
            dve.tensor_copy(v["token"][:].rearrange("p k t -> p (k t)"), v["route"][:, ROUTE_TOKEN:ROUTE_FILL])
            dve.tensor_scalar(v["end_row"][:], sel[:, H + HG:H + HG + E], float(REGION), None, ALU.mult)
            for dst, src in ((eq, q2l_r), (ek, kv2l_r)):
                for c in range(NCH):
                    ins = dve.tensor_tensor(
                        dst[:, c], src.unsqueeze(2).broadcast_to((P, L, HG)),
                        head_of_row[:, HG * c:HG * c + HG].unsqueeze(1).broadcast_to((P, L, HG)), ALU.mult)
                link(ins)
                dve.sem_inc(spread_ready, 1)
            for c in range(NCH):
                dve.tensor_scalar(er[:, c, 0:L:2, :], ek[:, c, 1:L:2, :], -1.0, None, ALU.mult)
                ins = dve.tensor_copy(er[:, c, 1:L:2, :], ek[:, c, 0:L:2, :])
            ins.then_inc(spread_ready, 1)
            link(dve.tensor_tensor(wqk_bd[:], wqk_rep.unsqueeze(2).broadcast_to((P, L, HG)),
                                   head_in_chunk.unsqueeze(1).broadcast_to((P, L, HG)), ALU.mult))
            dve.tensor_copy(v["wqk_c"][:], wqk_bd[:].rearrange("p l h -> p (l h)")).then_inc(wqk_ready, 1)
            dve.tensor_copy(bv_rep[:], ba[:, 2:3].broadcast_to((P, P)))
            dve.tensor_copy(kvb_rep[:], kvb[:].broadcast_to((L, P)))
            dve.tensor_copy(l2o_rep[:], l2o_t[:].unsqueeze(1).broadcast_to((L, H, HD)))
            for n, dst in enumerate((v["wq"], v["wk"], v["wkr"])):
                dve.wait_ge(folded, n + 1)
                link(dve.tensor_copy(full[:], bank[n][:]))
                link(dve.tensor_copy(dst[0][:], full[:]))
                link(dve.tensor_tensor(dst[1][:], full[:], dst[0][:].bitcast(F32), ALU.subtract))
            dve.wait_ge(folded_bias, 1)
            dve.tensor_scalar(v["bias_q"][:], bank[3][:, 0:NCH], qbc, None, ALU.add)
            dve.tensor_scalar(v["bias_k"][:], bank[3][:, NCH:2 * NCH], kbc, None, ALU.add).then_inc(bias_ready, 1)
            dve.wait_ge(rotated, 2)
            dve.tensor_scalar(v["bias_kr"][:], bank[4][:, 0:NCH], -1.0, None, ALU.mult)
            dve.tensor_copy(v["wqk_s"][:], bank[5][:, 0:P])
            dve.wait_ge(value_folded, 1)
            link(dve.tensor_copy(g_small[:], bank[6][:, 0:HD]))
            dve.tensor_tensor(g_bd[:], g_small[:].unsqueeze(1).broadcast_to((P, H, HD)),
                              head_of_row.unsqueeze(2).broadcast_to((P, H, HD)), ALU.mult).then_inc(g_ready, 1)
            dve.wait_ge(value_folded, 2)
            link(dve.tensor_copy(full[:, 0:C], bank[6][:, 0:C]))
            link(dve.tensor_copy(v["wv"][0][:], full[:, 0:C]))
            dve.tensor_tensor(v["wv"][1][:], full[:, 0:C], v["wv"][0][:].bitcast(F32), ALU.subtract)
            dve.tensor_tensor(v["bias_v"][:].rearrange("p (h d) -> p h d", d=HD),
                              bank[7][:, 0:C].rearrange("p (h d) -> p h d", d=HD),
                              l2o_br[:].unsqueeze(1).broadcast_to((P, H, HD)), ALU.add)
            dve.wait_ge(exp_ready, 1)
            link(dve.tensor_scalar(ce[:], ce[:], 1.0, None, ALU.add))
            link(dve.reciprocal(cs[:], ce[:]))
            dve.tensor_tensor(cst[:], cs[:], cin, ALU.mult).then_inc(silu_ready, 1)
            dve.wait_ge(modulated, 1)
            dve.tensor_copy(v["mod_s"][:], bank[0][:, 0:B])
            dve.tensor_scalar(v["mod_c"][:], bank[1][:, 0:B], 1.0, None, ALU.add)
            link(dve.tensor_copy(rows[:], bank[2][0:B, :].rearrange("b (m c) -> b m c", c=C)))
            link(dve.tensor_scalar(rows[:, 2, :], rows[:, 2, :], 1.0, None, ALU.add))
            link(dve.tensor_scalar(absr[:], rows[:, 0:4:3, :], -1.0, None, ALU.mult))
            link(dve.tensor_tensor(absr[:], absr[:], rows[:, 0:4:3, :], ALU.max))
            link(dve.tensor_scalar(absr[:], absr[:], 0.25, None, ALU.max))
            link(dve.tensor_scalar(sgn[:], rows[:, 0:4:3, :], 0.0, None, ALU.is_ge))
            link(dve.tensor_scalar(sgn[:], sgn[:], 2.0, -1.0, ALU.mult, ALU.add))
            dve.tensor_tensor(rows[:, 0:4:3, :], absr[:], sgn[:], ALU.mult).then_inc(rows_ready, 1)
            dve.wait_ge(b1_folded, 1)
            link(dve.tensor_tensor(b1f[:], bank[5][:, 0:E * NF], b1c, ALU.add))
            link(dve.tensor_copy(b1fh[:], b1f[:]))
            dve.tensor_copy(b1hl[:, 0:E * NF], b1fh[:].bitcast(F32))
            dve.tensor_tensor(b1hl[:, E * NF:], b1f[:], b1fh[:].bitcast(F32), ALU.subtract).then_inc(b1_split, 1)
            dve.wait_ge(b1_turned, 1)
            dve.tensor_copy(v["b1t"][:], bank[4][0:E * NF, 0:2 * P].rearrange("r (k p) -> r k p", k=2))


def attention(nc, ctx, sb, sem, bank, v):
    ident = v["ident"]
    qs, ks = v["qs"], v["ks"]
    prob = [sb(ctx, f"prob{i}", [P, HG * P_COLS]) for i in range(2)]
    u_sb = sb(ctx, "u_sb", [P, NCH, T])
    x_in = sb(ctx, "x_in", [P, TT, C])
    xn = sb(ctx, "xn", [P, TT, C])
    hf = sb(ctx, "hf", [P, T])
    hh, hl = sb(ctx, "hh", [P, T], F32R), sb(ctx, "hl", [P, T], F32R)
    q_cos, q_sin = sb(ctx, "q_cos", [P, T]), sb(ctx, "q_sin", [P, T])
    k_cos, k_sin, k_sum = sb(ctx, "k_cos", [P, T]), sb(ctx, "k_sin", [P, T]), sb(ctx, "k_sum", [P, T])
    qf = sb(ctx, "qf", [P, T])
    qh, ql = ([sb(ctx, f"{n}{i}", [P, T], F32R) for i in range(2)] for n in ("qh", "ql"))
    kh, kl = ([sb(ctx, f"{n}{i}", [P, T], F32R) for i in range(2)] for n in ("kh", "kl"))
    vx = [sb(ctx, f"vx{i}", [P, TT, H, VW]) for i in range(2)]
    mx = [sb(ctx, f"mx{i}", [P, HG * TT]) for i in range(2)]
    consts = sb(ctx, "consts", [P, 3, TT])
    mh, ml = sb(ctx, "mh", [HG * TT, P], F32R), sb(ctx, "ml", [HG * TT, P], F32R)
    y = sb(ctx, "y", [P, TT, C])
    rden = sb(ctx, "rden", [P, TT, H])
    y_t = sb(ctx, "y_t", [P, T])
    x_res = sb(ctx, "x_res", [P, TT, C])
    mod_b = sb(ctx, "mod_b", [P, 4, C])
    wc_g, bias_cg = sb(ctx, "wc_g", [P, C]), sb(ctx, "bias_cg", [P, C])
    xb = sb(ctx, "xb", [P, TT, C])
    x1 = sb(ctx, "x1", [P, TT, C])
    xn2 = sb(ctx, "xn2", [P, TT, C])
    h2 = sb(ctx, "h2", [P, TT, C])
    h2_t = sb(ctx, "h2_t", [P, T])
    queued = sb(ctx, "queued", [P, TOP, TT, ROW])
    base = sb(ctx, "base", [P, TT, C])
    lg = sb(ctx, "lg", [P, TT, E])
    top8 = sb(ctx, "top8", [P, TT, 8])
    idx8 = sb(ctx, "idx8", [P, TT, 8], U32)
    idxf = sb(ctx, "idxf", [P, TT, 2])
    hot = sb(ctx, "hot", [P, 2, TT, E])
    gdiff, gexp = sb(ctx, "gdiff", [P, TT]), sb(ctx, "gexp", [P, TT])
    both = sb(ctx, "both", [P, TT, E], BF16)
    rank, rank_k = sb(ctx, "rank", [P, TT, E]), sb(ctx, "rank_k", [P, TOP, TT, E])
    pos_f, pos = sb(ctx, "pos_f", [P, TOP, TT]), sb(ctx, "pos", [P, TOP, TT], U32)
    gden, gw, gsum = sb(ctx, "gden", [P, TT]), sb(ctx, "gw", [P, 2, TT]), sb(ctx, "gsum", [P, TT])
    ln = [dict(st=sb(ctx, f"ln_st{i}", [P, TT, 6]), mv=sb(ctx, f"ln_mv{i}", [P, TT, 2]),
               va=sb(ctx, f"ln_va{i}", [P, TT]), y=sb(ctx, f"ln_y{i}", [P, TT]), t=sb(ctx, f"ln_t{i}", [P, TT])) for i in range(3)]

    s_bank, st_bank, u_bank, f_bank, side = bank[0:2], bank[2:5], bank[5], bank[6], bank[7]

    x_loaded, t_loaded, outs_stored = sem("x_loaded"), sem("t_loaded"), sem("outs_stored")
    stack_ready = [sem(f"stack_ready{c}") for c in range(NCH)]
    rows_ready = [sem(f"max_rows_ready{c}") for c in range(NCH)]
    xn_ready, xt_ready, hf_ready, h_ready = sem("xn_ready"), sem("xt_ready"), sem("hf_ready"), sem("h_ready")
    v_ready, v_used = sem("v_ready"), sem("v_used")
    f_ready, f_used = sem("f_ready"), sem("f_used")
    ksum_ready, kh_ready, kl_ready = sem("ksum_ready"), sem("kh_ready"), sem("kl_ready")
    krope_ready, ql_ready = sem("krope_ready"), sem("ql_ready")
    s_ready, s_used = sem("s_ready"), sem("s_used")
    mt_ready, mh_ready, mt_used = sem("mt_ready"), sem("mh_ready"), sem("mt_used")
    st_ready, st_used = sem("st_ready"), sem("st_used")
    av_ready, u_copied = sem("av_ready"), sem("u_copied")
    ut_ready, ut_used = sem("ut_ready"), sem("ut_used")
    rden_ready = sem("rden_ready")
    yt_ready, yt_used = sem("yt_ready"), sem("yt_used")
    bcg_ready, xb_ready = sem("bcg_ready"), sem("xb_ready")
    proj_ready, x1_ready = sem("proj_ready"), sem("x1_ready")
    xn2_ready, h2m_ready, h2_ready = sem("xn2_ready"), sem("h2m_ready"), sem("h2_ready")
    held, consts_ready = sem("held"), sem("consts_ready")
    ht_ready, ht_used = sem("ht_ready"), sem("ht_used")
    xh_ready, gh_ready, base_ready = sem("xh_ready"), sem("gh_ready"), sem("base_ready")
    lg_ready, lg_used = sem("lg_ready"), sem("lg_used")
    gdiff_ready, gexp_ready, gsum_ready = sem("gdiff_ready"), sem("gexp_ready"), sem("gsum_ready")
    both_ready, rank_ready, rank_used = sem("both_ready"), sem("rank_ready"), sem("rank_used")
    pos_ready, copy_ready, scattered = sem("pos_ready"), sem("copy_ready"), sem("scattered")
    ln_step = [sem(f"ln_step{i}") for i in range(3)]
    st_step = [sem(f"stats_ready{i}") for i in range(3)]
    mv_ready = [sem(f"mean_ready{i}") for i in range(3)]
    rs_ready = [sem(f"rsqrt_ready{i}") for i in range(3)]
    rt_step = sem("router_step")
    RT_STEPS = 13
    SCATTERED = 16 * TOP * TT

    def at(b, c, ahead):
        return b + (c + ahead) // NCH, (c + ahead) % NCH

    def exists(c, ahead, last):
        return not last or c + ahead < NCH

    def pe_scores(pe, stacks, out, h, tile, col, wide_queries):
        q, k = stacks
        o = h * T
        if wide_queries:
            n = T - P * tile
            pe.matmul(out[:, col:col + n], k[:, o + P * tile:o + P * tile + P], q[:, o + P * tile:o + T],
                      start=(col == 0), stop=False, skip_group_check=True)
            return col
        n = P * (tile + 1)
        pe.matmul(out[:, col:col + n], q[:, o + P * tile:o + P * tile + P], k[:, o:o + n],
                  start=(col == 0), stop=False, skip_group_check=True)
        return col + n - P

    def pe_piece(pe, c, p, out, wide_queries):
        kind, heads = piece(p)
        stacks = qs[c], ks[c]
        mask = v["mask_k"] if wide_queries else v["mask_q"]
        tiles = {0: [0], 1: [1, 3], 2: [2]} if wide_queries else {0: [3], 1: [2, 0], 2: [1]}
        diag, col = [], 0
        for h in heads:
            for tile in tiles[kind]:
                diag.append(pe_scores(pe, stacks, out, h, tile, col, wide_queries))
                col += T - P * tile if wide_queries else P * (tile + 1)
        if len(diag) == 1:
            return pe.matmul(out[:, diag[0]:diag[0] + P], v["ident_bf"][:], mask[:],
                             start=False, stop=True, skip_group_check=True)
        gap = diag[1] - diag[0]
        if gap == P:
            dst = out[:, diag[0]:diag[0] + 2 * P].rearrange("p (a q) -> p a q", a=2)
        elif diag[0] + 2 * gap <= 512:
            dst = out[:, diag[0]:diag[0] + 2 * gap].rearrange("p (a q) -> p a q", a=2)[:, :, 0:P]
        else:
            dst = None
        if dst is None:
            for d in diag:
                ins = pe.matmul(out[:, d:d + P], v["ident_bf"][:], mask[:], start=False, stop=True,
                                skip_group_check=True)
            return ins
        return pe.matmul(dst, v["ident_bf"][:], mask[:].unsqueeze(1).broadcast_to((P, 2, P)),
                         start=False, stop=True, skip_group_check=True)

    def pe_s(pe, b, c, p):
        n = NCH * b + c
        if p == 0:
            wait(pe, stack_ready[c], 112 * (b + 1))
        wait(pe, s_used, PIECES * n + p - 1)
        pe_piece(pe, c, p, s_bank[p % 2], False).then_inc(s_ready, 1)

    def pe_st(pe, b, c, p):
        n = NCH * b + c
        if p == 0:
            wait(pe, rows_ready[c], 32 * (b + 1))
        wait(pe, st_used, PIECES * n + p - ST_BACK[p] + 1)
        pe_piece(pe, c, p, st_bank[ST_BANK[p]], True).then_inc(st_ready, 1)

    def pe_av(pe, b, c, odd, j):
        n = NCH * b + c
        if j == 0:
            wait(pe, st_used, PIECES * (n + 1))
            wait(pe, v_ready, b + 1)
            wait(pe, u_copied, n)
        for h in range(HG):
            ins = pe.matmul(u_bank[L * h:L * h + VW, P * j:T], vx[odd][:, j, HG * c + h, :],
                            prob[c % 2][:, P_COLS * h + P_OFF[j]:P_COLS * h + P_OFF[j] + T - P * j],
                            start=(j == 0), stop=(j == TT - 1), skip_group_check=True)
        if j == TT - 1:
            ins.then_inc(av_ready, 1)

    def three(pe, out, w, x, start=True, stop=True):
        pe.matmul(out, w[0], x[0], start=start, stop=False)
        pe.matmul(out, w[0], x[1], start=False, stop=False)
        return pe.matmul(out, w[1], x[0], start=False, stop=stop)

    def pe_f(pe, b, c, part):
        n = NCH * b + c
        wait(pe, f_used, 4 * n + part)
        if part == 3:
            pe.matmul(f_bank[:], v["wqk_c"][:], q_cos[:], start=True, stop=False)
            ins = pe.matmul(f_bank[:], v["wqk_s"][:], q_sin[:], start=False, stop=True)
        else:
            wait(pe, h_ready, b + 1)
            w = (v["wk"], v["wkr"], v["wq"])[part]
            ins = three(pe, f_bank[:], [m[:, P * c:P * c + P] for m in w], [hh[:], hl[:]])
        ins.then_inc(f_ready, 1)

    side_last = [None]

    def side_take(pe):
        if side_last[0] is not None:
            wait(pe, *side_last[0])

    def pe_mt(pe, b, c):
        side_take(pe)
        n = NCH * b + c
        wait(pe, s_used, PIECES * (n + 1))
        pe.transpose(side[0:HG * TT, 0:P], mx[c % 2][:], ident[:]).then_inc(mt_ready, 1)
        side_last[0] = (mt_used, n + 1)

    def pe_xt(pe, b):
        side_take(pe)
        wait(pe, xn_ready, b + 1)
        for t in range(TT):
            ins = pe.transpose(side[:, P * t:P * t + P], xn[:, t, :], ident[:])
        ins.then_inc(xt_ready, 1)
        side_last[0] = (hf_ready, b + 1)

    def pe_v(pe, b):
        side_take(pe)
        wait(pe, h_ready, b + 1)
        for t in range(TT):
            s = slice(P * t, P * t + P)
            ins = three(pe, side[:, s], [hh[:, s], hl[:, s]], [v["wv"][0][:], v["wv"][1][:]])
        ins.then_inc(v_used, 1)
        side_last[0] = (v_ready, b + 1)

    def pe_ut(pe, b, t):
        side_take(pe)
        if t == 0:
            wait(pe, u_copied, NCH * (b + 1))
        for c in range(NCH):
            ins = pe.transpose(side[:, P * c:P * c + P], u_sb[:, c, P * t:P * t + P], ident[:])
        ins.then_inc(ut_ready, 1)
        side_last[0] = (ut_used, TT * b + t + 1)

    def pe_yt(pe, b):
        side_take(pe)
        for t in range(TT):
            ins = pe.transpose(side[:, P * t:P * t + P], y[:, t, :], ident[:])
        ins.then_inc(yt_ready, 1)
        side_last[0] = (yt_used, b + 1)

    def pe_proj(pe, b):
        side_take(pe)
        wait(pe, yt_used, b + 1)
        wait(pe, bcg_ready, b + 1)
        for t in range(TT):
            s = slice(P * t, P * t + P)
            ins = pe.matmul(side[:, s], y_t[:, s], wc_g[:], start=True, stop=True)
        ins.then_inc(proj_ready, 1)
        side_last[0] = (x1_ready, b + 1)

    def pe_ht(pe, b):
        side_take(pe)
        wait(pe, h2_ready, b + 1)
        for t in range(TT):
            ins = pe.transpose(side[:, P * t:P * t + P], h2[:, t, :], ident[:])
        ins.then_inc(ht_ready, 1)
        side_last[0] = (ht_used, b + 1)

    def pe_lg(pe, b):
        side_take(pe)
        wait(pe, ht_used, b + 1)
        for t in range(TT):
            ins = pe.matmul(side[:, E * t:E * t + E], h2_t[:, P * t:P * t + P], v["wr"][:], start=True, stop=True)
        ins.then_inc(lg_ready, 1)
        side_last[0] = (lg_used, b + 1)

    def pe_rank(pe, b):
        side_take(pe)
        wait(pe, both_ready, b + 1)
        pe.matmul(side[:, 0:TT * E], v["before"][:], both[:].rearrange("p t e -> p (t e)"),
                  start=True, stop=False, skip_group_check=True)
        for t in range(TT):
            later = TT - t
            ins = pe.matmul(side[:, E * (t + 1):E * (TT + 1)].rearrange("p (a e) -> p a e", e=E), v["ones_bf"][:],
                            both[:, t:t + 1, :].broadcast_to((P, later, E)), start=False, stop=(later == 1),
                            skip_group_check=True)
        ins.then_inc(rank_ready, 1)
        side_last[0] = (rank_used, b + 1)

    def pe_slot(pe, b, c, odd, first, last):
        for p in range(PIECES):
            if exists(c, 2, last) and AT["s_first"][p]:
                pe_s(pe, *at(b, c, 2), p)
            pe_st(pe, b, c, p)
            if exists(c, 2, last) and not AT["s_first"][p]:
                pe_s(pe, *at(b, c, 2), p)
            if p in AT["av"] and not (first and c == 0):
                pe_av(pe, *at(b, c, -1), odd if c else 1 - odd, AT["av"].index(p))
            if exists(c, 3, last) and p in AT["f"]:
                pe_f(pe, *at(b, c, 3), AT["f"].index(p))
            if c == 2 and p == AT["yt"] and not first:
                pe_yt(pe, b - 1)
            if c == 3 and p == AT["ht"] and not first:
                pe_ht(pe, b - 1)
            if p == AT["mt"][c] and exists(c, 1, last):
                pe_mt(pe, *at(b, c, 1))
            if c == 0 and not last:
                if p == AT["xt"]:
                    pe_xt(pe, b + 1)
                if p == AT["v"]:
                    pe_v(pe, b + 1)
            if c == 1 and p in AT["ut"] and not first:
                pe_ut(pe, b - 1, AT["ut"].index(p))
            if c == 2 and p == AT["proj"] and not first:
                pe_proj(pe, b - 1)
            if c == 3 and not first:
                if p == AT["lg"]:
                    pe_lg(pe, b - 1)
                if p == AT["rank"]:
                    pe_rank(pe, b - 1)

    def pe_open(pe):
        pe_xt(pe, 0)
        for c in range(3):
            for part in range(4):
                pe_f(pe, 0, c, part)
            if c == 0:
                pe_v(pe, 0)
            if c >= 1:
                for p in range(PIECES):
                    pe_s(pe, 0, c - 1, p)
            if c == 1:
                pe_mt(pe, 0, 0)

    def pe_close(pe, b):
        for j in range(TT):
            pe_av(pe, b, NCH - 1, b % 2, j)
        for t in range(TT):
            pe_ut(pe, b, t)
        pe_yt(pe, b)
        pe_proj(pe, b)
        pe_ht(pe, b)
        pe_lg(pe, b)
        pe_rank(pe, b)

    def act_exp(act, b, c, p):
        n = NCH * b + c
        if p == 0:
            wait(act, av_ready, n - 1)
        wait(act, st_ready, PIECES * n + p + 1)
        kind, heads = piece(p)
        src, h = st_bank[ST_BANK[p]], heads[0]
        pb = prob[c % 2]
        if kind == 2:
            dst = pb[:, P_COLS * h:P_COLS * (h + 2)].rearrange("p (a n) -> p a n", a=2)[:, :, P_OFF[2]:P_OFF[2] + 2 * P]
            act.activation(dst, src[:].rearrange("p (a n) -> p a n", a=2), ACT.Exp, scale=SCALE).then_inc(st_used, 1)
        else:
            o = P_COLS * h + (P_OFF[0] if kind == 0 else P_OFF[1])
            act.activation(pb[:, o:o + T], src[:], ACT.Exp, scale=SCALE).then_inc(st_used, 1)

    def act_u(act, b, c, ut_done):
        n = NCH * b + c
        wait(act, av_ready, n + 1)
        wait(act, ut_ready, ut_done)
        act.activation(u_sb[:, c, :], u_bank[:], ACT.Copy).then_inc(u_copied, 1)

    def act_k(act, b, c, part):
        n = NCH * b + c
        wait(act, f_ready, 4 * n + part + 1)
        wait(act, ksum_ready, n)
        dst, bias = ((k_cos, "bias_k"), (k_sin, "bias_kr"))[part]
        act.activation(dst[:], f_bank[:], ACT.Identity, bias=v[bias][:, c:c + 1]).then_inc(f_used, 1)

    def act_qh(act, b, c):
        n = NCH * b + c
        wait(act, f_ready, 4 * n + 4)
        wait(act, ql_ready, n)
        act.activation(qf[:], f_bank[:], ACT.Identity, bias=v["param"]("wqk_b"))
        pb, pc = at(b, c, -2)
        wait(act, stack_ready[pc], 112 * (pb + 1))
        act.activation(qh[c % 2][:], f_bank[:], ACT.Identity, bias=v["param"]("wqk_b")).then_inc(f_used, 1)

    def act_kh(act, b, c):
        n = NCH * b + c
        wait(act, ksum_ready, n + 1)
        pb, pc = at(b, c, -2)
        wait(act, stack_ready[pc], 112 * (pb + 1))
        act.activation(kh[c % 2][:], k_sum[:], ACT.Copy).then_inc(kh_ready, 1)

    def act_mh(act, b, c):
        n = NCH * b + c
        wait(act, mt_ready, n + 1)
        pb, pc = at(b, c, -1)
        wait(act, rows_ready[pc], 32 * (pb + 1))
        act.activation(mh[:], side[0:HG * TT, 0:P], ACT.Copy).then_inc(mh_ready, 1)

    def act_hf(act, b):
        wait(act, xt_ready, b + 1)
        wait(act, h_ready, b)
        wait(act, f_ready, 16 * b)
        wait(act, v_used, b)
        act.activation(hf[:], side[:], ACT.Identity, bias=col(v["mod_s"], b), scale=col(v["mod_c"], b))
        act.activation(hh[:], side[:], ACT.Identity, bias=col(v["mod_s"], b), scale=col(v["mod_c"], b))\
           .then_inc(hf_ready, 1)

    def col(t, b):
        return t[:, b:b + 1] if isinstance(b, int) else t[:, bass.ds(b, 1)]

    def act_yt(act, b):
        wait(act, yt_ready, b + 1)
        wait(act, proj_ready, b)
        act.activation(y_t[:], side[:], ACT.Copy).then_inc(yt_used, 1)

    def act_ht(act, b):
        wait(act, ht_ready, b + 1)
        wait(act, lg_ready, b)
        act.activation(h2_t[:], side[:], ACT.Copy).then_inc(ht_used, 1)

    def act_gexp(act, b):
        wait(act, gdiff_ready, b + 1)
        wait(act, gsum_ready, b)
        act.activation(gexp[:], gdiff[:], ACT.Exp).then_inc(gexp_ready, 1)

    def act_slot(act, b, c, odd, first, last):
        for p in range(PIECES):
            act_exp(act, b, c, p)
            if c == 2 and p == AT["yt_copy"] and not first:
                act_yt(act, b - 1)
            if c == 3 and p == AT["ht_copy"] and not first:
                act_ht(act, b - 1)
            if p == AT["mh"][c] and exists(c, 1, last):
                act_mh(act, *at(b, c, 1))
            if exists(c, 3, last):
                if p in AT["k_copy"]:
                    act_k(act, *at(b, c, 3), AT["k_copy"].index(p))
                if p == AT["qh"]:
                    act_qh(act, *at(b, c, 3))
                if p == AT["kh"]:
                    act_kh(act, *at(b, c, 3))
            if c == 0 and not last and p == AT["hf"]:
                act_hf(act, b + 1)
            if p == AT["u"] and not (first and c == 0):
                pb, pc = at(b, c, -1)
                act_u(act, pb, pc, TT * pb)
            if c == 3 and p == AT["gexp"] and not first:
                act_gexp(act, b - 1)

    def act_open(act):
        act_hf(act, 0)
        for c in range(3):
            act_k(act, 0, c, 0)
            act_k(act, 0, c, 1)
            act_kh(act, 0, c)
            act_qh(act, 0, c)
            if c == 1:
                act_mh(act, 0, 0)

    def act_close(act, b):
        act_u(act, b, NCH - 1, TT * b)
        act_yt(act, b)
        act_ht(act, b)
        act_gexp(act, b)

    def dve_max(dve, b, c, p):
        n = NCH * b + c
        if p == 0:
            wait(dve, mt_ready, n - 1)
        wait(dve, s_ready, PIECES * n + p + 1)
        kind, heads = piece(p)
        src, h, m = s_bank[p % 2], heads[0], mx[c % 2]
        if kind == 0:
            ins = dve.tensor_reduce(m[:, TT * h + 3:TT * h + 4], src[:], AX.X, ALU.max, negate=True)
        elif kind == 1:
            dve.tensor_reduce(m[:, TT * h + 2:TT * h + 3], src[:, 0:3 * P], AX.X, ALU.max, negate=True)
            ins = dve.tensor_reduce(m[:, TT * h:TT * h + 1], src[:, 3 * P:4 * P], AX.X, ALU.max, negate=True)
        else:
            ins = dve.tensor_reduce(m[:, TT * h + 1:TT * h + 2 + TT:TT], src[:].rearrange("p (a n) -> p a n", a=2),
                                    AX.X, ALU.max, negate=True)
        ins.then_inc(s_used, 1)

    def dve_ml(dve, b, c):
        n = NCH * b + c
        wait(dve, mh_ready, n + 1)
        dve.tensor_tensor(ml[:], side[0:HG * TT, 0:P], mh[:].bitcast(F32), ALU.subtract).then_inc(mt_used, 1)

    def dve_q(dve, b, c):
        n = NCH * b + c
        wait(dve, f_ready, 4 * n + 3)
        dve.scalar_tensor_tensor(q_cos[:], f_bank[:], v["bias_q"][:, c:c + 1], v["cos_t"][:], ALU.add, ALU.mult)
        dve.scalar_tensor_tensor(q_sin[:], f_bank[:], v["bias_q"][:, c:c + 1], v["sin_t"][:], ALU.add, ALU.mult)\
           .then_inc(f_used, 1)

    def dve_ksum(dve, b, c):
        n = NCH * b + c
        wait(dve, krope_ready, n + 1)
        wait(dve, kl_ready, n)
        dve.tensor_tensor(k_sum[:], k_cos[:], k_sin[:], ALU.add).then_inc(ksum_ready, 1)

    def dve_kl(dve, b, c):
        n = NCH * b + c
        wait(dve, kh_ready, n + 1)
        dve.tensor_tensor(kl[c % 2][:], k_sum[:], kh[c % 2][:].bitcast(F32), ALU.subtract).then_inc(kl_ready, 1)

    def dve_norm(dve, b, i, part, src, dst, done):
        w = ln[i]
        if part == 0:
            for t in range(TT):
                ins = dve.bn_stats(w["st"][:, t, :], src[:, t, :])
            ins.then_inc(st_step[i], 1)
            wait(dve, st_step[i], b + 1)
            dve.sem_inc(held, 1)
            for t in range(TT):
                ins = dve.bn_aggr(w["mv"][:, t, :], w["st"][:, t, :])
            ins.then_inc(mv_ready[i], 1)
            return
        if part == 1:
            wait(dve, rs_ready[i], b + 1)
        for t in {1: (0, 1), 2: (2, 3)}[part]:
            ins = dve.tensor_scalar(dst[:, t, :], src[:, t, :], w["mv"][:, t, 0:1], w["y"][:, t:t + 1],
                                    ALU.subtract, ALU.mult)
        if part == 2:
            ins.then_inc(done, 1)

    def dve_l(dve, b, part):
        if part == 0:
            wait(dve, x_loaded, 16 * (b + 1))
            wait(dve, xt_ready, b)
        dve_norm(dve, b, 0, part, x_in, xn, xn_ready)

    def dve_v(dve, b, odd):
        wait(dve, v_used, b + 1)
        wait(dve, av_ready, NCH * (b - 1))
        dve.tensor_tensor(vx[odd][:, :, :, 0:HD], side[:].rearrange("p (t h d) -> p t h d", t=TT, d=HD),
                          v["bias_v"][:].rearrange("p (h d) -> p h d", d=HD).unsqueeze(1).broadcast_to((P, TT, H, HD)),
                          ALU.add).then_inc(v_ready, 1)

    def dve_ut(dve, b, t):
        wait(dve, ut_ready, TT * b + t + 1)
        if t == 0:
            wait(dve, yt_ready, b)
        heads = side[:].rearrange("p (h l) -> p h l", l=L)
        dve.reciprocal(rden[:, t, :], heads[:, :, HD]).then_inc(rden_ready, 1)
        wait(dve, rden_ready, TT * b + t + 1)
        dve.tensor_tensor(y[:, t, :].rearrange("p (h d) -> p h d", d=HD), heads[:, :, 0:HD],
                          rden[:, t, :].unsqueeze(2).broadcast_to((P, H, HD)), ALU.mult).then_inc(ut_used, 1)

    def dve_x1(dve, b):
        wait(dve, proj_ready, b + 1)
        wait(dve, xb_ready, b + 1)
        dve.tensor_tensor(x1[:].rearrange("p t c -> p (t c)"), side[:], xb[:].rearrange("p t c -> p (t c)"), ALU.add)\
           .then_inc(x1_ready, 1)

    def dve_xn2(dve, b, part):
        if part == 0:
            wait(dve, x1_ready, b + 1)
        dve_norm(dve, b, 1, part, x1, xn2, xn2_ready)

    def dve_xh(dve, b, part):
        if part == 0:
            wait(dve, h2_ready, b + 1)
            wait(dve, scattered, SCATTERED * b)
        dve_norm(dve, b, 2, part, h2, queued[:, 0, :, 0:C], xh_ready)

    def dve_lg(dve, b):
        wait(dve, lg_ready, b + 1)
        dve.tensor_tensor(lg[:], side[:, 0:TT * E].rearrange("p (t e) -> p t e", e=E),
                          v["bias_r"][:].unsqueeze(1).broadcast_to((P, TT, E)), ALU.add).then_inc(lg_used, 1)

    def dve_router(dve, b, part):
        at_step = [(0, 3, 4, 8, 13)[part]]

        def link(ins):
            at_step[0] += 1
            ins.then_inc(rt_step, 1)
            wait(dve, rt_step, RT_STEPS * b + at_step[0])

        if part == 0:
            wait(dve, lg_used, b + 1)
            dve.sem_inc(held, 1)
            for t in range(TT):
                ins = dve.max(top8[:, t, :], lg[:, t, :])
            link(ins)
            dve.tensor_tensor(gdiff[:], top8[:, :, 1], top8[:, :, 0], ALU.subtract).then_inc(gdiff_ready, 1)
            for t in range(TT):
                ins = dve.max_index(idx8[:, t, :], top8[:, t, :], lg[:, t, :])
            link(ins)
            link(dve.tensor_copy(idxf[:], idx8[:, :, 0:TOP]))
        elif part == 1:
            for k in range(TOP):
                ins = dve.tensor_tensor(hot[:, k], v["iota_e"][:].unsqueeze(1).broadcast_to((P, TT, E)),
                                        idxf[:, :, k:k + 1].broadcast_to((P, TT, E)), ALU.is_equal)
            link(ins)
            wait(dve, rank_used, b)
            dve.tensor_tensor(both[:], hot[:, 0], hot[:, 1], ALU.add).then_inc(both_ready, 1)
        elif part == 2:
            wait(dve, gexp_ready, b + 1)
            link(dve.tensor_scalar(gden[:], gexp[:], 1.0, None, ALU.add))
            link(dve.reciprocal(gw[:, 0], gden[:]))
            link(dve.tensor_tensor(gw[:, 1], gw[:, 0], gexp[:], ALU.mult))
            wait(dve, scattered, SCATTERED * b)
            dve.tensor_scalar(queued[:, :, :, C], gw[:], 1.0, None, ALU.mult)
            link(dve.tensor_tensor(gsum[:], gw[:, 0], gw[:, 1], ALU.add))
            dve.sem_inc(gsum_ready, 1)
        elif part == 3:
            wait(dve, rank_ready, b + 1)
            link(dve.tensor_tensor(rank[:], side[:, 0:TT * E].rearrange("p (t e) -> p t e", e=E),
                                   v["end_row"][:].unsqueeze(1).broadcast_to((P, TT, E)), ALU.add))
            dve.tensor_tensor(v["end_row"][:], v["end_row"][:], side[:, TT * E:(TT + 1) * E], ALU.add)\
               .then_inc(rank_used, 1)
            for k in range(TOP):
                ins = dve.tensor_tensor(rank_k[:, k], rank[:], hot[:, k], ALU.mult)
            link(ins)
            link(dve.tensor_reduce(pos_f[:], rank_k[:], AX.X, ALU.add))
            link(dve.tensor_scalar(queued[:, :, :, C + 1].bitcast(U32), v["token"][:], 1.0, None, ALU.mult))
            link(dve.tensor_scalar(v["token"][:], v["token"][:], float(T), None, ALU.add))
            dve.tensor_scalar(pos[:], pos_f[:], 1.0, None, ALU.mult).then_inc(pos_ready, 1)
        else:
            wait(dve, gh_ready, b + 1)
            wait(dve, outs_stored, 16 * b)
            for t in range(TT):
                ins = dve.scalar_tensor_tensor(base[:, t, :], xn2[:, t, :], gsum[:, t:t + 1], x1[:, t, :], ALU.mult, ALU.add)
            ins.then_inc(base_ready, 1)

    def dve_slot(dve, b, c, odd, first, last):
        for p in range(PIECES):
            if exists(c, 2, last) and not AT["max_last"][p]:
                dve_max(dve, *at(b, c, 2), p)
            if exists(c, 3, last):
                if p == AT["q"]:
                    dve_q(dve, *at(b, c, 3))
                if p == AT["ksum"]:
                    dve_ksum(dve, *at(b, c, 3))
                if p == AT["kl"]:
                    dve_kl(dve, *at(b, c, 3))
            if p == AT["ml"][c] and exists(c, 1, last):
                dve_ml(dve, *at(b, c, 1))
            if c == 0 and not last:
                if p in AT["l"]:
                    dve_l(dve, b + 1, AT["l"].index(p))
                if p == AT["v_add"]:
                    dve_v(dve, b + 1, 1 - odd)
            if c == 1 and not first and p in AT["ut_div"]:
                dve_ut(dve, b - 1, AT["ut_div"].index(p))
            if c == 2 and not first:
                if p == AT["x1"]:
                    dve_x1(dve, b - 1)
                if p in AT["xn2"]:
                    dve_xn2(dve, b - 1, AT["xn2"].index(p))
            if c == 3 and not first:
                if p in AT["xh"]:
                    dve_xh(dve, b - 1, AT["xh"].index(p))
                if p == AT["lg_add"]:
                    dve_lg(dve, b - 1)
                if p in AT["router"]:
                    dve_router(dve, b - 1, AT["router"].index(p))
            if exists(c, 2, last) and AT["max_last"][p]:
                dve_max(dve, *at(b, c, 2), p)

    def dve_open(dve):
        for i in range(2):
            dve.memset(vx[i][:], 1.0)
        dve.memset(u_bank[:], 0.0)
        dve.memset(ml[:].bitcast(F32), 0.0)
        for part in range(3):
            dve_l(dve, 0, part)
        for c in range(3):
            dve_q(dve, 0, c)
            dve_ksum(dve, 0, c)
            dve_kl(dve, 0, c)
            if c == 0:
                dve_v(dve, 0, 0)
            if c >= 1:
                for p in range(PIECES):
                    dve_max(dve, 0, c - 1, p)
            if c == 1:
                dve_ml(dve, 0, 0)

    def dve_close(dve, b):
        for t in range(TT):
            dve_ut(dve, b, t)
        dve_x1(dve, b)
        for part in range(3):
            dve_xn2(dve, b, part)
        dve_xh(dve, b, 0)
        dve_lg(dve, b)
        dve_router(dve, b, 0)
        dve_router(dve, b, 1)
        for part in (1, 2):
            dve_xh(dve, b, part)
        for part in (2, 3, 4):
            dve_router(dve, b, part)

    def pool_rsqrt(pool, b, i, used):
        w, steps = ln[i], 0

        def link(ins):
            nonlocal steps
            steps += 1
            ins.then_inc(ln_step[i], 1)
            wait(pool, ln_step[i], LN_STEPS * b + steps)

        wait(pool, mv_ready[i], b + 1)
        wait(pool, used, b)
        link(pool.tensor_tensor(w["va"][:], w["mv"][:, :, 1], consts[:, 0], ALU.add))
        pool.sem_inc(held, 1)
        pool.tensor_scalar(w["y"][:].bitcast(I32), w["va"][:].bitcast(I32), -0.5, float(RSQRT_MAGIC), ALU.mult, ALU.add)
        link(pool.tensor_tensor(w["va"][:], w["va"][:], consts[:, 1], ALU.mult))
        for n in range(3):
            link(pool.tensor_tensor(w["t"][:], w["y"][:], w["y"][:], ALU.mult))
            link(pool.tensor_tensor(w["t"][:], w["t"][:], w["va"][:], ALU.mult))
            link(pool.tensor_tensor(w["t"][:], w["t"][:], consts[:, 2], ALU.add))
            link(pool.tensor_tensor(w["y"][:], w["y"][:], w["t"][:], ALU.mult))
        pool.sem_inc(rs_ready[i], 1)

    def pool_k(pool, b, c):
        n = NCH * b + c
        wait(pool, f_used, 4 * n + 1)
        pool.tensor_tensor(k_cos[:], k_cos[:], v["cos_t"][:], ALU.mult)
        wait(pool, f_used, 4 * n + 2)
        pool.tensor_tensor(k_sin[:], k_sin[:], v["sin_t"][:], ALU.mult).then_inc(krope_ready, 1)

    def pool_ql(pool, b, c):
        n = NCH * b + c
        wait(pool, f_used, 4 * n + 4)
        pool.tensor_tensor(ql[c % 2][:], qf[:], qh[c % 2][:].bitcast(F32), ALU.subtract).then_inc(ql_ready, 1)

    def pool_h(pool, b):
        wait(pool, hf_ready, b + 1)
        pool.tensor_tensor(hl[:], hf[:], hh[:].bitcast(F32), ALU.subtract).then_inc(h_ready, 1)

    def pool_xb(pool, b):
        wait(pool, t_loaded, 32 * (b + 1))
        wait(pool, proj_ready, b)
        wait(pool, x1_ready, b)
        pool.tensor_tensor(wc_g[:], v["param"]("cproj_t"), mod_b[:, 0, :], ALU.mult)
        pool.tensor_tensor(bias_cg[:], v["bias_c"][:], mod_b[:, 0, :], ALU.mult).then_inc(bcg_ready, 1)
        wait(pool, bcg_ready, b + 1)
        pool.tensor_tensor(xb[:], x_res[:], bias_cg[:].unsqueeze(1).broadcast_to((P, TT, C)), ALU.add).then_inc(xb_ready, 1)

    def pool_h2(pool, b):
        wait(pool, xn2_ready, b + 1)
        wait(pool, ht_ready, b)
        wait(pool, xh_ready, b)
        pool.tensor_tensor(h2[:], xn2[:], mod_b[:, 2, :].unsqueeze(1).broadcast_to((P, TT, C)), ALU.mult).then_inc(h2m_ready, 1)
        wait(pool, h2m_ready, b + 1)
        pool.tensor_tensor(h2[:], h2[:], mod_b[:, 1, :].unsqueeze(1).broadcast_to((P, TT, C)), ALU.add).then_inc(h2_ready, 1)
        wait(pool, h2_ready, b + 1)
        pool.tensor_tensor(xn2[:], h2[:], mod_b[:, 3, :].unsqueeze(1).broadcast_to((P, TT, C)), ALU.mult).then_inc(gh_ready, 1)

    def pool_scatter(pool, b, k):
        if k == 0:
            wait(pool, xh_ready, b + 1)
            wait(pool, pos_ready, b + 1)
        else:
            pool.tensor_copy(queued[:, 1, :, 0:C], queued[:, 0, :, 0:C]).then_inc(copy_ready, 1)
            wait(pool, copy_ready, b + 1)
        pool.sem_inc(held, 1)
        for t in range(TT):
            pool.indirect_dma_start(v["d_queue"], bass.IndirectOffsetOnAxis(pos[:, k, t:t + 1], 0),
                                    queued[:, k, t, :], None).then_inc(scattered, 16)

    def pool_slot(pool, b, c, odd, first, last):
        for stage in range(3):
            if stage == 1 and exists(c, 3, last):
                pool_k(pool, *at(b, c, 3))
            if stage == 2 and exists(c, 3, last):
                pool_ql(pool, *at(b, c, 3))
            if c == 0 and not last:
                if stage == AT["rsqrt"][0]:
                    pool_rsqrt(pool, b + 1, 0, xn_ready)
                if stage == 2:
                    pool_h(pool, b + 1)
            if c == 1 and stage == AT["xb"] and not first:
                pool_xb(pool, b - 1)
            if c == 2 and not first:
                if stage == AT["rsqrt"][1]:
                    pool_rsqrt(pool, b - 1, 1, xn2_ready)
                if stage == 2:
                    pool_h2(pool, b - 1)
            if c == 3 and stage == AT["rsqrt"][2] and not first:
                pool_rsqrt(pool, b - 1, 2, xh_ready)
            if c in (0, 1) and stage == AT["scatter"][c] and not first and not (isinstance(b, int) and b == 1):
                pool_scatter(pool, b - 2, c)

    def pool_open(pool):
        for k, value in enumerate((LN_EPS, -0.5, 1.5)):
            pool.memset(consts[:, k], value).then_inc(consts_ready, 1)
        pool.wait_ge(consts_ready, 3)
        pool_rsqrt(pool, 0, 0, xn_ready)
        pool_h(pool, 0)
        for c in range(3):
            pool_k(pool, 0, c)
            pool_ql(pool, 0, c)

    def pool_close(pool, b):
        pool_xb(pool, b)
        for k in range(TOP):
            pool_scatter(pool, b - 1, k)
        pool_rsqrt(pool, b, 1, xn2_ready)
        pool_h2(pool, b)
        pool_rsqrt(pool, b, 2, xh_ready)
        for k in range(TOP):
            pool_scatter(pool, b, k)

    def sp_wait(sp, semaphore, n):
        if isinstance(n, int) and n <= 0:
            return
        sp.wait_ge(semaphore, n)
        sp.sem_inc(held, 1)

    def tokens(ap, b, width):
        t = ap.rearrange("(b t p) c -> b p t c", p=P, t=TT)
        return t[b] if isinstance(b, int) else t[bass.ds(b, 1)].rearrange("a p t c -> (a p) t c")

    x_rows = v["x"].rearrange("b t c -> (b t) c")

    def sp_x(sp, b):
        sp_wait(sp, xn_ready, b)
        sp.dma_start(x_in[:], tokens(x_rows, b, C)).then_inc(x_loaded, 16)

    def sp_t(sp, b):
        sp_wait(sp, xb_ready, b)
        sp_wait(sp, gh_ready, b)
        sp.dma_start(x_res[:], tokens(x_rows, b, C)).then_inc(t_loaded, 16)
        m = v["d_mod"]
        row = m[b:b + 1, :] if isinstance(b, int) else m[bass.ds(b, 1), :]
        sp.dma_start(mod_b[:].rearrange("p m c -> p (m c)"), row.broadcast_to((P, 4 * C))).then_inc(t_loaded, 16)

    def sp_stack(sp, b, c):
        n = NCH * b + c
        sp_wait(sp, st_ready, PIECES * (n - NCH + 1))
        sp.dma_start(qs[c][ROW_MAX:ROW_MAX + 2, :].bitcast(F32), qs[c][ROW_MAX + 2:ROW_MAX + 4, :].bitcast(F32))\
          .then_inc(stack_ready[c], 16)
        sp_wait(sp, kh_ready, n + 1)
        for r, src in ((0, kh[c % 2]), (L, kh[c % 2])):
            sp.dma_start(ks[c][r:r + L, :].bitcast(F32), src[:].bitcast(F32)).then_inc(stack_ready[c], 16)
        sp_wait(sp, kl_ready, n + 1)
        sp.dma_start(ks[c][2 * L:3 * L, :].bitcast(F32), kl[c % 2][:].bitcast(F32)).then_inc(stack_ready[c], 16)
        sp_wait(sp, ql_ready, n + 1)
        for r, src in ((0, qh[c % 2]), (2 * L, qh[c % 2]), (L, ql[c % 2])):
            sp.dma_start(qs[c][r:r + L, :].bitcast(F32), src[:].bitcast(F32)).then_inc(stack_ready[c], 16)

    def sp_rows(sp, b, c):
        n = NCH * b + c
        sp_wait(sp, mt_used, n + 1)
        sp_wait(sp, mh_ready, n + 1)
        for r, src in ((ROW_MAX, mh), (ROW_MAX + 1, ml)):
            sp.dma_start(qs[c][r:r + 1, :].bitcast(F32), src[:].bitcast(F32)).then_inc(rows_ready[c], 16)

    def sp_out(sp, b):
        sp_wait(sp, base_ready, b + 1)
        sp.dma_start(tokens(v["d_base"], b, C), base[:]).then_inc(outs_stored, 16)

    def sp_slot(sp, b, c, odd, first, last):
        if c == 1 and not (isinstance(b, int) and b + 2 >= B):
            sp_x(sp, b + 2)
        if exists(c, 1, last):
            sp_rows(sp, *at(b, c, 1))
        if exists(c, 3, last):
            sp_stack(sp, *at(b, c, 3))
        if c == 0 and not first:
            sp_t(sp, b - 1)
        if c == 3 and not first:
            sp_out(sp, b - 1)

    def sp_open(sp):
        sp_x(sp, 0)
        sp_stack(sp, 0, 0)
        sp_stack(sp, 0, 1)
        sp_rows(sp, 0, 0)
        sp_x(sp, 1)
        sp_stack(sp, 0, 2)

    def sp_close(sp, b):
        sp_t(sp, b)
        sp_out(sp, b)
        sp.wait_ge(outs_stored, 16 * B)
        sp.wait_ge(scattered, SCATTERED * B)

    def run(eng, opening, slot, closing):
        side_last[0] = None
        opening(eng)
        for b in (0, 1):
            for c in range(NCH):
                slot(eng, b, c, b, b == 0, False)
        with eng.Fori(2, B - 3, 2) as i:
            for odd in (0, 1):
                for c in range(NCH):
                    slot(eng, i + 1 if odd else i, c, odd, False, False)
        for b in (B - 2, B - 1):
            for c in range(NCH):
                slot(eng, b, c, b % 2, False, b == B - 1)
        closing(eng, B - 1)

    with nc.Block() as block:
        @block.sync
        def _(sp):
            run(sp, sp_open, sp_slot, sp_close)

        @block.gpsimd
        def _(pool):
            run(pool, pool_open, pool_slot, pool_close)

        @block.scalar
        def _(act):
            run(act, act_open, act_slot, act_close)

        @block.vector
        def _(dve):
            run(dve, dve_open, dve_slot, dve_close)

        @block.tensor
        def _(pe):
            run(pe, pe_open, pe_slot, pe_close)


def feed_forward(nc, ctx, sb, sem, bank, v):
    NF = FF // P
    LAST = TILES - 1
    ROUND = RING * 3
    assert (TILES - 2 * RING) % ROUND == 0
    ident = v["ident"]
    g, b1t, base_all, gb_all = v["param"]("ln_g_t"), v["b1t"], v["base_all"], v["gb_all"]
    w1h, w1l = sb(ctx, "w1h", [P, E * FF], F32R), sb(ctx, "w1l", [P, E * FF], F32R)
    w2s = sb(ctx, "w2s", [P, E * NF, 2, C], F32R)
    w2f = w2s[:].rearrange("p b k c -> p (b k c)")
    b1_rows = sb(ctx, "b1_rows", [P, E * FF], F32R)
    b2_rows = sb(ctx, "b2_rows", [P, E * C], F32R)
    ones = sb(ctx, "ones", [P, P], F32R)
    w1 = sb(ctx, "w1", [P, E * FF])
    w2 = sb(ctx, "w2", [P, E * FF])
    b2f, b2h, b2l = sb(ctx, "b2f", [E, C]), sb(ctx, "b2h", [E, C], F32R), sb(ctx, "b2l", [E, C], F32R)
    fill = sb(ctx, "fill", [P, 2 * E, ROW])
    count, count_i, tiles_e = sb(ctx, "count", [1, E]), sb(ctx, "count_i", [1, E], I32), sb(ctx, "tiles_e", [1, E])
    ends, skip = sb(ctx, "ends", [1, E]), sb(ctx, "skip", [1, E])
    past, past_skip = sb(ctx, "past", [1, TILES, E]), sb(ctx, "past_skip", [1, TILES, E])
    sum_past, sum_skip, row_f = sb(ctx, "sum_past", [1, TILES]), sb(ctx, "sum_skip", [1, TILES]), sb(ctx, "row_f", [1, TILES])
    expert_of, row_of = sb(ctx, "expert_of", [1, TILES + ROUND], U32), sb(ctx, "row_of", [1, TILES + ROUND], U32)
    fill_at = sb(ctx, "fill_at", [1, E], U32)
    table_call = sb(ctx, "table_call", [P, 1])
    xq = [sb(ctx, f"xq{r}", [P, ROW]) for r in range(RING)]
    y_lo = sb(ctx, "y_lo", [P, C])
    z = [sb(ctx, f"z{r}", [P, C]) for r in range(RING)]
    xth = [sb(ctx, f"xth{i}", [P, P], F32R) for i in range(2)]
    xtl = [sb(ctx, f"xtl{i}", [P, P], F32R) for i in range(2)]
    a = [sb(ctx, f"a{i}", [P, FF]) for i in range(2)]
    ah = [sb(ctx, f"ah{i}", [P, FF], F32R) for i in range(2)]
    al = [sb(ctx, f"al{i}", [P, FF], F32R) for i in range(2)]

    w_loaded = [sem(f"w_loaded{e}") for e in range(0, E, 2)]
    w2l_ready = sem("w2l_ready")
    b_loaded, fill_stored, b_stored = sem("b_loaded"), sem("fill_stored"), sem("b_rows_stored")
    tab_step, tables_ready, fill_ready = sem("tab_step"), sem("tables_ready"), sem("fill_ready")
    bias_out, zeroed = sem("bias_out"), sem("rows_zeroed")
    wh_ready, wl_ready = sem("wh_ready"), sem("wl_ready")
    x_loaded = [sem(f"xq_loaded{r}") for r in range(RING)]
    z_stored = [sem(f"z_stored{r}") for r in range(RING)]
    xt_ready, xh_ready, xl_ready = sem("q_xt_ready"), sem("q_xh_ready"), sem("q_xl_ready")
    hid_ready, a_ready, at_ready = sem("hid_ready"), sem("a_ready"), sem("at_ready")
    ah_ready, al_ready, y_ready, z_ready = sem("ah_ready"), sem("al_ready"), sem("y_ready"), sem("z_ready")
    fill_at_ready, fill_zeroed = sem("fill_at_ready"), sem("fill_zeroed")
    y_lo_ready, sums_loaded = sem("y_lo_ready"), sem("sums_loaded")
    held = sem("f_held")
    h_bank, at_bank, x_bank, y_bank = bank[0:2], bank[2:4], bank[4:6], bank[6:8]

    def stored_by(base, r):
        return base * (16 // RING) + 16 * (r // RING + 1)

    def hold(eng, semaphore, n):
        if isinstance(n, int) and n <= 0:
            return
        eng.wait_ge(semaphore, n)
        eng.sem_inc(held, 1)

    def entry(table, at):
        return table[0:1, at:at + 1] if isinstance(at, int) else table[0:1, bass.ds(at, 1)]

    def tiles(step, eng, read=None):
        def one_round(base, steps):
            regs = (read(base),) if read else ()
            for r in range(steps):
                step(base, r, *regs)

        one_round(0, RING)
        with eng.Fori(RING, TILES - RING, ROUND) as i:
            one_round(i, ROUND)
        one_round(TILES - RING, RING)

    def early(base, r, n):
        return isinstance(base, int) and base + r < n

    def final(base, r):
        return isinstance(base, int) and base + r == LAST

    with nc.Block() as block:
        @block.sync
        def _(sp):
            sp.dma_start(b2f[:], v["b2"]).then_inc(b_loaded, 16)
            for e in range(0, E, 2):
                s = slice(FF * e, FF * (e + 2))
                sp.dma_start(w1[:, s].rearrange("p (e f) -> p e f", f=FF), v["w1"][e:e + 2].rearrange("e p f -> p e f"))\
                  .then_inc(w_loaded[e // 2], 16)
                sp.dma_start(w2[:, s].rearrange("p (n c) -> p n c", c=C),
                             v["w2"][e:e + 2].rearrange("e (f p) c -> p (e f) c", p=P)).then_inc(w_loaded[e // 2], 16)
            sp.wait_ge(fill_ready, 1)
            sp.dma_start(v["d_queue"][E * REGION:, :].rearrange("(g p) c -> p g c", p=P), fill[:, E:, :])\
              .then_inc(fill_stored, 16)
            sp.wait_ge(fill_at_ready, 1)
            for e in range(E):
                row = sp.value_load(fill_at[0:1, e:e + 1], min_val=e * REGION, max_val=e * REGION + N_TOK)
                sp.dma_start(v["d_queue"][bass.ds(row, P), :], fill[:, e, :]).then_inc(fill_stored, 16)
            sp.wait_ge(zeroed, 1)
            sp.wait_ge(bias_out, 1)
            for k, part in ((0, b2h), (1, b2l)):
                sp.dma_start(b1_rows[k:k + 1, :].bitcast(F32), b1t[:, k, :]).then_inc(b_stored, 16)
                sp.dma_start(b2_rows[k:k + 1, :].bitcast(F32), part[:].bitcast(F32)).then_inc(b_stored, 16)
            sp.wait_ge(fill_stored, 16 * (E + 1))
            sp.wait_ge(tables_ready, 1)

            def step(base, r):
                row = sp.value_load(entry(row_of, base + r), min_val=0, max_val=E * REGION + (E - 1) * P)
                hold(sp, z_stored[r % RING], stored_by(base, r) - 16)
                sp.dma_start(xq[r % RING][:], v["d_queue"][bass.ds(row, P), :]).then_inc(x_loaded[r % RING], 16)

            tiles(step, sp)
            sp.dma_start(gb_all[:], v["d_mod"][:, 3 * C:4 * C].rearrange("(a b) c -> a b c", a=1).broadcast_to((P, B, C)))\
              .then_inc(sums_loaded, 16)
            for q in range(B // TT):
                sp.dma_start(base_all[:, TT * TT * q:TT * TT * (q + 1), :],
                             v["d_base"][TT * T * q:TT * T * (q + 1), :].rearrange("(n p) c -> p n c", p=P))\
                  .then_inc(sums_loaded, 16)
            sp.wait_ge(sums_loaded, 16 * (B // TT + 1))
            for r in range(RING):
                sp.wait_ge(z_stored[r], 16 * (TILES // RING))

        @block.gpsimd
        def _(pool):
            pool.memset(fill[:], 0.0).then_inc(fill_zeroed, 1)
            pool.memset(b1_rows[:].bitcast(F32), 0.0)
            pool.memset(b2_rows[:].bitcast(F32), 0.0)
            pool.memset(ones[:].bitcast(F32), 1.0).then_inc(zeroed, 1)
            for e in range(E):
                s = slice(FF * e, FF * e + FF)
                hi, lo = w2s[:, NF * e:NF * e + NF, 0], w2s[:, NF * e:NF * e + NF, 1]
                pool.wait_ge(wh_ready, 2 * e + 2)
                ins = pool.tensor_tensor(lo, w2[:, s].rearrange("p (f c) -> p f c", c=C), hi.bitcast(F32), ALU.subtract)
            ins.then_inc(w2l_ready, 1)

            def step(base, r):
                hold(pool, z_ready, base + (r + 1))
                target = xq[r % RING][:, C + 1:C + 2].bitcast(U32)
                pool.indirect_dma_start(v["d_y"], bass.IndirectOffsetOnAxis(target, 0),
                                        z[r % RING][:], None).then_inc(z_stored[r % RING], 16)

            tiles(step, pool)

        @block.scalar
        def _(act):
            act.activation(table_call[:], ident[:, 0:1], ACT.Gelu)
            for e in range(E):
                s = slice(FF * e, FF * e + FF)
                act.wait_ge(w_loaded[e // 2], 32)
                act.activation(w1h[:, s], w1[:, s], ACT.Copy, scale=g[:, e:e + 1]).then_inc(wh_ready, 1)
                act.activation(w2s[:, NF * e:NF * e + NF, 0], w2[:, s].rearrange("p (f c) -> p f c", c=C), ACT.Copy).then_inc(wh_ready, 1)

            def x_hi(base, r):
                act.wait_ge(xt_ready, base + (r + 1))
                act.activation(xth[r % 2][:], x_bank[r % 2][:, 0:P], ACT.Copy).then_inc(xh_ready, 1)

            def a_hi(base, r):
                act.wait_ge(at_ready, base + (r + 1))
                if not early(base, r, 2):
                    act.wait_ge(y_ready, base + (r - 1))
                act.activation(ah[r % 2][:], at_bank[r % 2][:], ACT.Copy).then_inc(ah_ready, 1)

            x_hi(0, 0)

            def step(base, r):
                act.wait_ge(hid_ready, base + (r + 1))
                if not early(base, r, 2):
                    act.wait_ge(at_ready, base + (r - 1))
                act.activation(a[r % 2][:], h_bank[r % 2][:], ACT.Gelu).then_inc(a_ready, 1)
                if not final(base, r):
                    x_hi(base, r + 1)
                if not early(base, r, 1):
                    a_hi(base, r - 1)

            tiles(step, act)
            a_hi(TILES, -1)

        @block.vector
        def _(dve):
            steps = 0

            def link(ins):
                nonlocal steps
                steps += 1
                ins.then_inc(tab_step, 1)
                dve.wait_ge(tab_step, steps)

            dve.tensor_copy(fill_at[:], v["end_row"][0:1, :]).then_inc(fill_at_ready, 1)
            link(dve.scalar_tensor_tensor(count[:], v["iota_e"][0:1, :], -float(REGION), v["end_row"][0:1, :],
                                          ALU.mult, ALU.add))
            link(dve.tensor_scalar(count_i[:], count[:], float(P - 1), None, ALU.add))
            link(dve.tensor_scalar(count_i[:], count_i[:], P.bit_length() - 1, None, ALU.logical_shift_right))
            link(dve.tensor_copy(tiles_e[:], count_i[:]))
            link(dve.tensor_copy(ends[:], tiles_e[:]))
            for e in range(1, E):
                link(dve.tensor_tensor(ends[:, e:e + 1], ends[:, e - 1:e], tiles_e[:, e:e + 1], ALU.add))
            dve.wait_ge(fill_zeroed, 1)
            dve.tensor_copy(fill[:, :, C + 1].bitcast(U32), v["fill_target"]).then_inc(fill_ready, 1)
            link(dve.tensor_scalar(skip[:], tiles_e[:], -float(P), float(REGION), ALU.mult, ALU.add))
            number = v["tile_no"][0:1, :]
            link(dve.tensor_tensor(past[:], number.unsqueeze(2).broadcast_to((1, TILES, E)),
                                   ends[:].unsqueeze(1).broadcast_to((1, TILES, E)), ALU.is_ge))
            dve.tensor_reduce(sum_past[:], past[:], AX.X, ALU.add)
            link(dve.tensor_tensor(past_skip[:], past[:], skip[:].unsqueeze(1).broadcast_to((1, TILES, E)), ALU.mult))
            link(dve.tensor_reduce(sum_skip[:], past_skip[:], AX.X, ALU.add))
            dve.tensor_scalar(expert_of[:, 0:TILES], sum_past[:], float(E - 1), None, ALU.min)
            link(dve.scalar_tensor_tensor(row_f[:], number, float(P), sum_skip[:], ALU.mult, ALU.add))
            dve.tensor_copy(row_of[:, 0:TILES], row_f[:]).then_inc(tables_ready, 1)
            dve.wait_ge(b_loaded, 16)
            link(dve.tensor_copy(b2h[:], b2f[:]))
            dve.tensor_tensor(b2l[:], b2f[:], b2h[:].bitcast(F32), ALU.subtract).then_inc(bias_out, 1)
            for e in range(E):
                s = slice(FF * e, FF * e + FF)
                dve.wait_ge(wh_ready, 2 * e + 1)
                ins = dve.scalar_tensor_tensor(w1l[:, s], w1[:, s], g[:, e:e + 1], w1h[:, s].bitcast(F32), ALU.mult, ALU.subtract)
            ins.then_inc(wl_ready, 1)

            def x_lo(base, r):
                dve.wait_ge(xh_ready, base + (r + 1))
                dve.tensor_tensor(xtl[r % 2][:], x_bank[r % 2][:, 0:P], xth[r % 2][:].bitcast(F32), ALU.subtract)\
                   .then_inc(xl_ready, 1)

            def a_lo(base, r):
                dve.wait_ge(ah_ready, base + (r + 1))
                dve.tensor_tensor(al[r % 2][:], at_bank[r % 2][:], ah[r % 2][:].bitcast(F32), ALU.subtract)\
                   .then_inc(al_ready, 1)

            def out(base, r, place):
                y, w = y_bank[place % 2], xq[place][:, C:C + 1]
                dve.wait_ge(y_ready, base + (r + 1))
                if not early(base, r, 1):
                    dve.wait_ge(z_ready, base + r)
                dve.tensor_scalar(y_lo[:], y[:, C:2 * C], w, None, ALU.mult).then_inc(y_lo_ready, 1)
                dve.wait_ge(y_lo_ready, base + (r + 1))
                dve.scalar_tensor_tensor(z[place][:], y[:, 0:C], w, y_lo[:], ALU.mult, ALU.add).then_inc(z_ready, 1)

            x_lo(0, 0)

            def step(base, r):
                if not final(base, r):
                    x_lo(base, r + 1)
                if not early(base, r, 1):
                    a_lo(base, r - 1)
                if not early(base, r, 2):
                    out(base, r - 2, (r - 2) % RING)

            tiles(step, dve)
            a_lo(TILES, -1)
            out(TILES, -2, RING - 2)
            out(TILES, -1, RING - 1)

        @block.tensor
        def _(pe):
            def turn_x(base, r):
                pe.wait_ge(x_loaded[r % RING], stored_by(base, r))
                pe.transpose(x_bank[r % 2][:, 0:P], xq[r % RING][:, 0:C], ident[:]).then_inc(xt_ready, 1)

            def expert(base, r):
                return pe.value_load(entry(expert_of, base + r), min_val=0, max_val=E - 1)

            def hidden(base, r, n):
                pe.wait_ge(xl_ready, base + (r + 1))
                if not early(base, r, 2):
                    pe.wait_ge(a_ready, base + (r - 1))
                h = h_bank[r % 2][:]
                s = bass.ds(n * FF, FF)
                pe.matmul(h, xth[r % 2][:], w1h[:, s], start=True, stop=False)
                pe.matmul(h, xth[r % 2][:], w1l[:, s], start=False, stop=False)
                pe.matmul(h, xtl[r % 2][:], w1h[:, s], start=False, stop=False)
                pe.matmul(h, ones[:], b1_rows[:, s], start=False, stop=True).then_inc(hid_ready, 1)

            def turn_a(base, r):
                pe.wait_ge(a_ready, base + (r + 1))
                if not early(base, r, 2):
                    pe.wait_ge(al_ready, base + (r - 1))
                for f in range(NF):
                    ins = pe.transpose(at_bank[r % 2][:, P * f:P * f + P], a[r % 2][:, P * f:P * f + P], ident[:])
                ins.then_inc(at_ready, 1)

            def output(base, r, n):
                pe.wait_ge(al_ready, base + (r + 1))
                if not early(base, r, 2):
                    pe.wait_ge(z_ready, base + (r - 1))
                y = y_bank[r % 2]
                for f in range(NF):
                    pe.matmul(y[:, 0:2 * C], ah[r % 2][:, P * f:P * f + P], w2f[:, bass.ds(n * 2 * FF + 2 * C * f, 2 * C)],
                              start=(f == 0), stop=False, skip_group_check=True)
                for f in range(NF):
                    pe.matmul(y[:, 0:C], al[r % 2][:, P * f:P * f + P], w2f[:, bass.ds(n * 2 * FF + 2 * C * f, C)],
                              start=False, stop=False, skip_group_check=True)
                pe.matmul(y[:, 0:C], ones[:], b2_rows[:, bass.ds(n * C, C)],
                          start=False, stop=True, skip_group_check=True).then_inc(y_ready, 1)

            pe.wait_ge(wl_ready, 1)
            pe.wait_ge(w2l_ready, 1)
            pe.wait_ge(zeroed, 1)
            pe.wait_ge(b_stored, 64)
            pe.wait_ge(tables_ready, 1)
            turn_x(0, 0)

            def step(base, r, experts):
                hidden(base, r, experts[r])
                if not final(base, r):
                    turn_x(base, r + 1)
                if not early(base, r, 1):
                    turn_a(base, r - 1)
                if r < 2 and not early(base, r, 2):
                    experts[r - 2] = expert(base, r - 2)
                if r + 1 < (RING if isinstance(base, int) else ROUND):
                    experts[r + 1] = expert(base, r + 1)
                if not early(base, r, 2):
                    output(base, r - 2, experts[r - 2])

            tiles(step, pe, lambda base: {0: expert(base, 0)})
            turn_a(TILES, -1)
            output(TILES, -2, expert(TILES, -2))
            output(TILES, -1, expert(TILES, -1))


def combine(nc, ctx, sb, sem, v):
    PLACES = 4
    base, gb = v["base_all"], v["gb_all"]
    y = [[sb(ctx, f"c_y{k}_{r}", [P, TT, C]) for r in range(PLACES)] for k in range(TOP)]
    s = [sb(ctx, f"c_sum{r}", [P, TT, C]) for r in range(PLACES)]
    o = [sb(ctx, f"c_out{r}", [P, TT, C]) for r in range(PLACES)]
    loaded = [sem(f"c_loaded{r}") for r in range(PLACES)]
    stored = [sem(f"c_stored{r}") for r in range(PLACES)]
    added, scaled, out_ready, held = sem("c_added"), sem("c_scaled"), sem("c_out_ready"), sem("c_held")

    def tokens(ap, b):
        t = ap.rearrange("(b t p) c -> b p t c", p=P, t=TT)
        return t[b] if isinstance(b, int) else t[bass.ds(b, 1)].rearrange("a p t c -> (a p) t c")

    def batches(eng, step):
        for r in range(PLACES):
            step(r, r, 0)
        with eng.Fori(PLACES, B - PLACES + 1, PLACES) as i:
            for r in range(PLACES):
                step(i + r, r, i * (16 // PLACES))

    with nc.Block() as block:
        @block.sync
        def _(sp):
            def step(b, r, before):
                if not isinstance(before, int):
                    sp.wait_ge(added, b - (PLACES - 1))
                    sp.sem_inc(held, 1)
                sp.dma_start(y[0][r][:], tokens(v["d_y"][0:N_TOK, :], b)).then_inc(loaded[r], 16)
                sp.dma_start(y[1][r][:], tokens(v["d_y"][N_TOK:TOP * N_TOK, :], b)).then_inc(loaded[r], 16)

            batches(sp, step)
            for r in range(PLACES):
                sp.wait_ge(stored[r], 16 * (B // PLACES))

        @block.scalar
        def _(act):
            def step(b, r, before):
                act.wait_ge(out_ready, b + 1)
                act.sem_inc(held, 1)
                act.dma_start(tokens(v["out"].rearrange("b t c -> (b t) c"), b), o[r][:]).then_inc(stored[r], 16)

            batches(act, step)

        @block.gpsimd
        def _(pool):
            def step(b, r, before):
                row = gb[:, b:b + 1, :] if isinstance(b, int) else gb[:, bass.ds(b, 1), :]
                pool.wait_ge(added, b + 1)
                pool.tensor_tensor(s[r][:], s[r][:], row.broadcast_to((P, TT, C)), ALU.mult).then_inc(scaled, 1)

            batches(pool, step)

        @block.vector
        def _(dve):
            def add(b, r, before):
                dve.wait_ge(loaded[r], before * 2 + 32)
                if not isinstance(before, int):
                    dve.wait_ge(out_ready, b - (PLACES - 1))
                dve.tensor_tensor(s[r][:], y[0][r][:], y[1][r][:], ALU.add).then_inc(added, 1)

            def total(b, r, before):
                rows = base[:, TT * b:TT * b + TT, :] if isinstance(b, int) else base[:, bass.ds(b * TT, TT), :]
                dve.wait_ge(scaled, b + 1)
                if not isinstance(before, int):
                    dve.wait_ge(stored[r], before)
                dve.tensor_tensor(o[r][:], s[r][:], rows, ALU.add).then_inc(out_ready, 1)

            def one_round(first, before):
                for r in range(PLACES):
                    add(first + r, r, before)
                    if r:
                        total(first + r - 1, r - 1, before)
                total(first + PLACES - 1, PLACES - 1, before)

            one_round(0, 0)
            with dve.Fori(PLACES, B - PLACES + 1, PLACES) as i:
                one_round(i, i * (16 // PLACES))


_INS = ['attn_x', 'attn_c_attn_w', 'attn_c_attn_b', 'attn_q2l_w', 'attn_q2l_b', 'attn_kv2l_w', 'attn_kv2l_b',
        'attn_l2o_w', 'attn_l2o_b', 'attn_wqk_w', 'attn_wqk_b', 'attn_cproj_w', 'attn_cproj_b',
        'ffn_router_W', 'ffn_router_b', 'ffn_ln_g', 'ffn_ln_b', 'ffn_W1', 'ffn_b1', 'ffn_W2', 'ffn_b2', 'c', 'wmod']
_OUTS = [((16, 512, 128), 'float32')]


def _constants():
    import numpy as np
    latent, heads = np.arange(P) // HG, np.arange(P) % HG
    inv = (np.float32(1.0) / np.float32(10000.0) ** (np.arange(0, L, 2, dtype=np.float32) / np.float32(L))).astype(np.float32)
    angle = np.outer(np.arange(T, dtype=np.float32), inv).astype(np.float32)
    cos = np.cos(angle).astype(np.float32).T[latent // 2]
    sin = np.sin(angle).astype(np.float32).T[latent // 2]
    rot = np.zeros((P, P), np.float32)
    for r in range(P):
        other = r + HG if latent[r] % 2 == 0 else r - HG
        rot[r, other] = -1.0 if latent[r] % 2 == 0 else 1.0
    mats = np.concatenate([np.eye(P, dtype=np.float32), rot], 1)
    q, k = np.meshgrid(np.arange(P), np.arange(P), indexing="ij")
    hide = np.where(k > q, np.float32(-1e30), np.float32(0))
    sel = np.concatenate([(np.arange(P)[:, None] // HD == np.arange(H)), (heads[:, None] == np.arange(HG)),
                          np.broadcast_to(np.arange(E), (P, E))], 1)
    masks = np.concatenate([hide, hide.T, sel], 1).astype(np.float32)
    p = np.arange(P)[:, None]
    route = np.concatenate([k > q, (np.arange(TOP)[:, None] * N_TOK + np.arange(TT) * P).reshape(1, -1) + p,
                            TOP * N_TOK + np.arange(2 * E) * P + p,
                            np.broadcast_to(np.arange(TILES), (P, TILES))], 1).astype(np.float32)
    return {"c_cos": np.ascontiguousarray(cos), "c_sin": np.ascontiguousarray(sin), "c_mats": mats, "c_masks": masks,
            "c_route": route}


def _small(w):
    import numpy as np
    latent_col = lambda b: np.repeat(b, HG)[:, None]
    parts = {"b_attn": w["attn_c_attn_b"].reshape(3, C).T, "q2l_b": latent_col(w["attn_q2l_b"]),
             "kv2l_b": latent_col(w["attn_kv2l_b"]), "wqk_b": latent_col(w["attn_wqk_b"]),
             "q2l_t": np.tile(w["attn_q2l_w"].T, (H, 1)), "kv2l_t": np.tile(w["attn_kv2l_w"].T, (H, 1)),
             "wqk_t": np.repeat(w["attn_wqk_w"].T, HG, axis=0), "cproj_t": w["attn_cproj_w"].T,
             "ln_g_t": w["ffn_ln_g"].T, "ln_b_t": w["ffn_ln_b"].T,
             "b1_t": w["ffn_b1"].reshape(E * FF // P, P).T, "cond_t": w["c"].T}
    return np.ascontiguousarray(np.concatenate([parts[name] for name, _ in SMALL], 1))


def kernel(**inputs):
    import numpy as _np
    import concourse.bacc as _bacc
    from concourse import mybir as _mybir
    from concourse.bass_utils import run_bass_kernel_spmd as _run

    nc = _bacc.Bacc("TRN2", target_bir_lowering=False, num_devices=1)
    w = {name: _np.ascontiguousarray(inputs["L0_" + name]) for name in _INS}
    arrays = {"x": w["attn_x"], "w_attn": w["attn_c_attn_w"], "kv2l_h": _np.tile(w["attn_kv2l_w"], (1, H)),
              "kvb_col": w["attn_kv2l_b"][:, None], "l2o_t": _np.ascontiguousarray(w["attn_l2o_w"].T),
              "l2o_b": w["attn_l2o_b"][None], "cproj_b": w["attn_cproj_b"][None], "router_w": w["ffn_router_W"],
              "router_b": w["ffn_router_b"][None], "w1": w["ffn_W1"], "w2": w["ffn_W2"], "b2": w["ffn_b2"],
              "wmod": w["wmod"], "small": _small(w), **_constants()}
    arrays = {"in_" + name: _np.ascontiguousarray(a) for name, a in arrays.items()}
    args = [nc.dram_tensor(name, a.shape, _mybir.dt.from_np(a.dtype), kind="ExternalInput").ap()
            for name, a in arrays.items()]
    for i, (shape, dtype) in enumerate(_OUTS):
        dt = _mybir.dt.from_np(_np.dtype(dtype))
        args.append(nc.dram_tensor(f"out_{i}", shape, dt, kind="ExternalOutput").ap())
    adaln_block(nc, *args)
    r = _run(nc, [arrays], core_ids=[0])
    return r.results[0]["out_0"]
```
